# Optimizing a Trainium2 kernel written in Bass

```python
import numpy as np
import jax
import jax.numpy as jnp

def _softmax(x, axis=-1):
    return jax.nn.softmax(x, axis=axis)

def _gelu(x):
    return jax.nn.gelu(x, approximate=True)

def _silu(x):
    return jax.nn.silu(x)

def _sigmoid(x):
    return jax.nn.sigmoid(x)

def _layernorm(x, axis=-1, eps=1e-05):
    m = jnp.mean(x, axis=axis, keepdims=True)
    v = jnp.var(x, axis=axis, keepdims=True)
    return (x - m) / jnp.sqrt(v + eps)

def _scatter_add(tgt, idx, src, axis=0):
    return tgt.at[idx].add(src)

def _segment_sum(src, seg, n):
    return jax.ops.segment_sum(src, seg, n)
kernel_name = 'mk_decoder_preln_d2_seqx_r8_149c9f'

def setup_inputs(seed: int=0):
    np.random.seed(seed)
    _w = jnp.asarray

    def _rec_inputs():
        import jax
        import jax.numpy as jnp
        _rk = jax.random.key(seed)
        x = 7.22e-05 + 1 * jax.random.normal(jax.random.fold_in(_rk, 1), (32, 128, 128), jnp.float32)
        _lenS = 128 - jax.random.randint(jax.random.fold_in(_rk, 7), (32,), 0, max(1, 128 // 4) + 1, jnp.int32)
        _lenS2 = 128 - jax.random.randint(jax.random.fold_in(_rk, 8), (32,), 0, max(1, 128 // 4) + 1, jnp.int32)
        _ctx_1024P = jax.random.normal(jax.random.fold_in(_rk, 11), (32, 16, 128), jnp.float32)
        _ctx_1024c = jax.random.dirichlet(jax.random.fold_in(_rk, 511), 0.3 * jnp.ones((16,), jnp.float32), (32, 128))
        _ctx_1024t = jnp.einsum('bsk,bkd->bsd', _ctx_1024c, _ctx_1024P)
        _ctx_1024t = _ctx_1024t * jax.lax.rsqrt(jnp.mean(jnp.square(_ctx_1024t)) + 1e-12) * 0.953939
        ctx_1024 = 4.13588e-05 + 0.999923 * (_ctx_1024t + 0.3 * jax.random.normal(jax.random.fold_in(_rk, 611), (32, 128, 128), jnp.float32))
        _validS = jnp.arange(128)[None, :] < _lenS[:, None]
        _validS2 = jnp.arange(128)[None, :] < _lenS2[:, None]
        _causal = jnp.tril(jnp.ones((128, 128), dtype=bool))
        mask_BxS2_ff1 = jnp.where(jnp.ones((32, 128), dtype=bool), 1.0, 0.0).astype(jnp.float32)
        return (x, ctx_1024, mask_BxS2_ff1)
    x, ctx_1024, mask_BxS2_ff1 = _rec_inputs()

    def _L0_attn_setup():
        import jax, jax.numpy as jnp
        import numpy as np
        B, S, D_IN = (2, 256, 128)
        D_OUT, H, WINDOW = (128, 16, 64)
        HD = D_OUT // H
        key = jax.random.key(seed)
        k1, k2, k3, k4 = jax.random.split(key, 4)
        scale_in = 1.0 / np.sqrt(D_IN)
        scale_out = 1.0 / np.sqrt(D_OUT)
        return {'x': jax.random.normal(k1, (B, S, D_IN), dtype=jnp.float32), 'w_qkv': jax.random.normal(k2, (3 * D_OUT, D_IN), dtype=jnp.float32) * scale_in, 'w_out': jax.random.normal(k3, (D_OUT, D_OUT), dtype=jnp.float32) * scale_out, 'b_out': jax.random.normal(k4, (D_OUT,), dtype=jnp.float32) * scale_out}
    _L0_attn_all = _L0_attn_setup()
    _L0_attn_in = {k: v for k, v in _L0_attn_all.items() if k in ('w_qkv', 'w_out', 'b_out')}
    del _L0_attn_all

    def _L0_xattn_setup():
        import jax, jax.numpy as jnp
        import numpy as np
        EMB = 128
        HEADS = 16
        HEAD_DIM = EMB // HEADS
        key = jax.random.key(seed)
        ks = jax.random.split(key, 11)
        B, S = (4, 256)
        scale = 1.0 / np.sqrt(EMB)
        inp = {'query': jax.random.normal(ks[0], (B, S, EMB), jnp.float32), 'key': jax.random.normal(ks[1], (B, S, EMB), jnp.float32), 'value': jax.random.normal(ks[2], (B, S, EMB), jnp.float32), 'Wq': jax.random.normal(ks[3], (EMB, EMB), jnp.float32) * scale, 'bq': jnp.zeros((EMB,), jnp.float32), 'Wk': jax.random.normal(ks[4], (EMB, EMB), jnp.float32) * scale, 'bk': jnp.zeros((EMB,), jnp.float32), 'Wv': jax.random.normal(ks[5], (EMB, EMB), jnp.float32) * scale, 'bv': jnp.zeros((EMB,), jnp.float32), 'Wo': jax.random.normal(ks[6], (EMB, EMB), jnp.float32) * scale, 'bo': jnp.zeros((EMB,), jnp.float32)}
        return inp
    _L0_xattn_all = _L0_xattn_setup()
    _L0_xattn_in = {k: v for k, v in _L0_xattn_all.items() if k in ('Wq', 'bq', 'Wk', 'bk', 'Wv', 'bv', 'Wo', 'bo')}
    del _L0_xattn_all

    def _L0_ffn_setup():
        import math
        import jax, jax.numpy as jnp
        import numpy as np
        B, S, D, H, E, F = (2, 128, 128, 16, 16, 512)
        HEAD = D // H
        MOE_TOKEN_DROPOUT = 0.2
        EPS = 1e-05

        def layer_norm(x, w, b):
            mu = x.mean(-1, keepdims=True)
            var = ((x - mu) ** 2).mean(-1, keepdims=True)
            return (x - mu) * jax.lax.rsqrt(var + EPS) * w + b
        key = jax.random.key(seed)
        ks = jax.random.split(key, 16)
        w = lambda k, shape: jax.random.normal(k, shape, jnp.float32) * 0.02
        return {'hidden_states': jax.random.normal(ks[0], (B, S, D), jnp.float32), 'ln1_w': jnp.ones((D,), jnp.float32), 'ln1_b': jnp.zeros((D,), jnp.float32), 'q_w': w(ks[1], (D, D)), 'q_b': jnp.zeros((D,), jnp.float32), 'k_w': w(ks[2], (D, D)), 'k_b': jnp.zeros((D,), jnp.float32), 'v_w': w(ks[3], (D, D)), 'v_b': jnp.zeros((D,), jnp.float32), 'o_w': w(ks[4], (D, D)), 'o_b': jnp.zeros((D,), jnp.float32), 'ln2_w': jnp.ones((D,), jnp.float32), 'ln2_b': jnp.zeros((D,), jnp.float32), 'router_w': w(ks[5], (D, E)), 'fc1_w': w(ks[6], (E, D, F)), 'fc1_b': jnp.zeros((E, F), jnp.float32), 'fc2_w': w(ks[7], (E, F, D)), 'fc2_b': jnp.zeros((E, D), jnp.float32)}
    _L0_ffn_all = _L0_ffn_setup()
    _L0_ffn_in = {k: v for k, v in _L0_ffn_all.items() if k in ('ln1_w', 'ln1_b', 'q_w', 'q_b', 'k_w', 'k_b', 'v_w', 'v_b', 'o_w', 'o_b', 'ln2_w', 'ln2_b', 'router_w', 'fc1_w', 'fc1_b', 'fc2_w', 'fc2_b')}
    del _L0_ffn_all

    def _L1_attn_setup():
        import jax, jax.numpy as jnp
        import numpy as np
        NUM_HEADS = 16
        THETA = 10000.0

        def _rotate_half(x):
            x = x.reshape(x.shape[:-1] + (-1, 2))
            x1, x2 = (x[..., 0], x[..., 1])
            return jnp.stack((-x2, x1), axis=-1).reshape(x.shape[:-2] + (-1,))

        def _rope(x):
            d_k = x.shape[-1]
            seq_len = x.shape[-2]
            inv_freq = 1.0 / THETA ** (jnp.arange(0, d_k, 2, dtype=jnp.float32) / d_k)
            pos = jnp.arange(seq_len, dtype=jnp.float32)
            theta = pos[:, None] * inv_freq[None, :]
            cos = jnp.repeat(jnp.cos(theta), 2, axis=-1)
            sin = jnp.repeat(jnp.sin(theta), 2, axis=-1)
            return x * cos + _rotate_half(x) * sin
        key = jax.random.key(seed)
        kx, kq, kk, kv, ko = jax.random.split(key, 5)
        B, S, D = (2, 256, 128)
        std = 1.0 / (2.0 * (2 * D) ** 0.5)
        return {'x': jax.random.normal(kx, (B, S, D), dtype=jnp.float32), 'Wq': jax.random.normal(kq, (D, D), dtype=jnp.float32) * std, 'Wk': jax.random.normal(kk, (D, D), dtype=jnp.float32) * std, 'Wv': jax.random.normal(kv, (D, D), dtype=jnp.float32) * std, 'Wo': jax.random.normal(ko, (D, D), dtype=jnp.float32) * std}
    _L1_attn_all = _L1_attn_setup()
    _L1_attn_in = {k: v for k, v in _L1_attn_all.items() if k in ('Wq', 'Wk', 'Wv', 'Wo')}
    del _L1_attn_all

    def _L1_xattn_setup():
        import jax, jax.numpy as jnp
        import numpy as np
        NUM_HEADS = 16
        key = jax.random.key(seed)
        ks = jax.random.split(key, 8)
        B, S, D = (4, 256, 128)
        scale = 1.0 / np.sqrt(D)
        return {'query': jax.random.normal(ks[0], (B, S, D), dtype=jnp.float32), 'key': jax.random.normal(ks[1], (B, S, D), dtype=jnp.float32), 'value': jax.random.normal(ks[2], (B, S, D), dtype=jnp.float32), 'mask': jnp.ones((B, S), dtype=jnp.float32), 'Wq': jax.random.normal(ks[3], (D, D), dtype=jnp.float32) * scale, 'bq': jnp.zeros((D,), dtype=jnp.float32), 'Wk': jax.random.normal(ks[4], (D, D), dtype=jnp.float32) * scale, 'bk': jnp.zeros((D,), dtype=jnp.float32), 'Wv': jax.random.normal(ks[5], (D, D), dtype=jnp.float32) * scale, 'bv': jnp.zeros((D,), dtype=jnp.float32), 'Wo': jax.random.normal(ks[6], (D, D), dtype=jnp.float32) * scale, 'bo': jnp.zeros((D,), dtype=jnp.float32)}
    _L1_xattn_all = _L1_xattn_setup()
    _L1_xattn_in = {k: v for k, v in _L1_xattn_all.items() if k in ('Wq', 'bq', 'Wk', 'bk', 'Wv', 'bv', 'Wo', 'bo')}
    del _L1_xattn_all

    def _L1_ffn_setup():
        import jax, jax.numpy as jnp
        import numpy as np
        TOP_K = 2
        key = jax.random.key(seed)
        ks = jax.random.split(key, 6)
        B, T, D, H, E = (4, 256, 128, 512, 8)
        s = 0.02
        return {'x': jax.random.normal(ks[0], (B, T, D), dtype=jnp.float32), 'Wg': jax.random.normal(ks[1], (E, D), dtype=jnp.float32) * s, 'W1': jax.random.normal(ks[2], (E, H, D), dtype=jnp.float32) * s, 'b1': jax.random.normal(ks[3], (E, H), dtype=jnp.float32) * s, 'W2': jax.random.normal(ks[4], (E, D, H), dtype=jnp.float32) * s, 'b2': jax.random.normal(ks[5], (E, D), dtype=jnp.float32) * s}
    _L1_ffn_all = _L1_ffn_setup()
    _L1_ffn_in = {k: v for k, v in _L1_ffn_all.items() if k in ('Wg', 'W1', 'b1', 'W2', 'b2')}
    del _L1_ffn_all
    return {'x': x, 'ctx_1024': ctx_1024, 'mask_BxS2_ff1': mask_BxS2_ff1, 'L0_attn_w_qkv': _L0_attn_in['w_qkv'], 'L0_attn_w_out': _L0_attn_in['w_out'], 'L0_attn_b_out': _L0_attn_in['b_out'], 'L0_xattn_Wq': _L0_xattn_in['Wq'], 'L0_xattn_bq': _L0_xattn_in['bq'], 'L0_xattn_Wk': _L0_xattn_in['Wk'], 'L0_xattn_bk': _L0_xattn_in['bk'], 'L0_xattn_Wv': _L0_xattn_in['Wv'], 'L0_xattn_bv': _L0_xattn_in['bv'], 'L0_xattn_Wo': _L0_xattn_in['Wo'], 'L0_xattn_bo': _L0_xattn_in['bo'], 'L0_ffn_ln1_w': _L0_ffn_in['ln1_w'], 'L0_ffn_ln1_b': _L0_ffn_in['ln1_b'], 'L0_ffn_q_w': _L0_ffn_in['q_w'], 'L0_ffn_q_b': _L0_ffn_in['q_b'], 'L0_ffn_k_w': _L0_ffn_in['k_w'], 'L0_ffn_k_b': _L0_ffn_in['k_b'], 'L0_ffn_v_w': _L0_ffn_in['v_w'], 'L0_ffn_v_b': _L0_ffn_in['v_b'], 'L0_ffn_o_w': _L0_ffn_in['o_w'], 'L0_ffn_o_b': _L0_ffn_in['o_b'], 'L0_ffn_ln2_w': _L0_ffn_in['ln2_w'], 'L0_ffn_ln2_b': _L0_ffn_in['ln2_b'], 'L0_ffn_router_w': _L0_ffn_in['router_w'], 'L0_ffn_fc1_w': _L0_ffn_in['fc1_w'], 'L0_ffn_fc1_b': _L0_ffn_in['fc1_b'], 'L0_ffn_fc2_w': _L0_ffn_in['fc2_w'], 'L0_ffn_fc2_b': _L0_ffn_in['fc2_b'], 'L1_attn_Wq': _L1_attn_in['Wq'], 'L1_attn_Wk': _L1_attn_in['Wk'], 'L1_attn_Wv': _L1_attn_in['Wv'], 'L1_attn_Wo': _L1_attn_in['Wo'], 'L1_xattn_Wq': _L1_xattn_in['Wq'], 'L1_xattn_bq': _L1_xattn_in['bq'], 'L1_xattn_Wk': _L1_xattn_in['Wk'], 'L1_xattn_bk': _L1_xattn_in['bk'], 'L1_xattn_Wv': _L1_xattn_in['Wv'], 'L1_xattn_bv': _L1_xattn_in['bv'], 'L1_xattn_Wo': _L1_xattn_in['Wo'], 'L1_xattn_bo': _L1_xattn_in['bo'], 'L1_ffn_Wg': _L1_ffn_in['Wg'], 'L1_ffn_W1': _L1_ffn_in['W1'], 'L1_ffn_b1': _L1_ffn_in['b1'], 'L1_ffn_W2': _L1_ffn_in['W2'], 'L1_ffn_b2': _L1_ffn_in['b2']}

def reference(x, ctx_1024, mask_BxS2_ff1, L0_attn_w_qkv, L0_attn_w_out, L0_attn_b_out, L0_xattn_Wq, L0_xattn_bq, L0_xattn_Wk, L0_xattn_bk, L0_xattn_Wv, L0_xattn_bv, L0_xattn_Wo, L0_xattn_bo, L0_ffn_ln1_w, L0_ffn_ln1_b, L0_ffn_q_w, L0_ffn_q_b, L0_ffn_k_w, L0_ffn_k_b, L0_ffn_v_w, L0_ffn_v_b, L0_ffn_o_w, L0_ffn_o_b, L0_ffn_ln2_w, L0_ffn_ln2_b, L0_ffn_router_w, L0_ffn_fc1_w, L0_ffn_fc1_b, L0_ffn_fc2_w, L0_ffn_fc2_b, L1_attn_Wq, L1_attn_Wk, L1_attn_Wv, L1_attn_Wo, L1_xattn_Wq, L1_xattn_bq, L1_xattn_Wk, L1_xattn_bk, L1_xattn_Wv, L1_xattn_bv, L1_xattn_Wo, L1_xattn_bo, L1_ffn_Wg, L1_ffn_W1, L1_ffn_b1, L1_ffn_W2, L1_ffn_b2):
    import jax
    import jax.numpy as jnp

    def _L0_attn_ref(x, w_qkv, w_out, b_out):
        import jax, jax.numpy as jnp
        import numpy as np
        B, S, D_IN = (2, 256, 128)
        D_OUT, H, WINDOW = (128, 16, 64)
        HD = D_OUT // H
        b, s, _ = x.shape
        qkv = jnp.einsum('bsi,oi->bso', x, w_qkv)
        q, k, v = jnp.split(qkv, 3, axis=-1)

        def heads(t):
            return t.reshape(b, s, H, HD).transpose(0, 2, 1, 3)
        q, k, v = (heads(q), heads(k), heads(v))
        scores = jnp.einsum('bhqd,bhkd->bhqk', q, k) / jnp.sqrt(jnp.asarray(HD, x.dtype))
        i = jnp.arange(s)[:, None]
        j = jnp.arange(s)[None, :]
        allowed = (j <= i) & (i - j < WINDOW)
        scores = jnp.where(allowed[None, None], scores, jnp.asarray(-jnp.inf, x.dtype))
        attn = jax.nn.softmax(scores, axis=-1)
        ctx = jnp.einsum('bhqk,bhkd->bhqd', attn, v)
        ctx = ctx.transpose(0, 2, 1, 3).reshape(b, s, D_OUT)
        return jnp.einsum('bso,po->bsp', ctx, w_out) + b_out

    def _L0_xattn_ref(query, key, value, Wq, bq, Wk, bk, Wv, bv, Wo, bo):
        import jax, jax.numpy as jnp
        import numpy as np
        EMB = 128
        HEADS = 16
        HEAD_DIM = EMB // HEADS
        B, S, E = query.shape
        H, D = (HEADS, HEAD_DIM)

        def split_heads(x):
            return x.reshape(B, -1, H, D).transpose(0, 2, 1, 3)
        Q = split_heads(query @ Wq + bq)
        K = split_heads(key @ Wk + bk)
        V = split_heads(value @ Wv + bv)
        scores = jnp.einsum('bhqd,bhkd->bhqk', Q, K) / jnp.sqrt(jnp.float32(D))
        attn = jax.nn.softmax(scores, axis=-1)
        out = jnp.einsum('bhqk,bhkd->bhqd', attn, V)
        out = out.transpose(0, 2, 1, 3).reshape(B, S, E)
        return out @ Wo + bo

    def _L0_ffn_ref(hidden_states, ln1_w, ln1_b, q_w, q_b, k_w, k_b, v_w, v_b, o_w, o_b, ln2_w, ln2_b, router_w, fc1_w, fc1_b, fc2_w, fc2_b):
        import math
        import jax, jax.numpy as jnp
        import numpy as np
        B, S, D, H, E, F = (2, 128, 128, 16, 16, 512)
        HEAD = D // H
        MOE_TOKEN_DROPOUT = 0.2
        EPS = 1e-05

        def layer_norm(x, w, b):
            mu = x.mean(-1, keepdims=True)
            var = ((x - mu) ** 2).mean(-1, keepdims=True)
            return (x - mu) * jax.lax.rsqrt(var + EPS) * w + b
        b, s, _ = hidden_states.shape
        T = b * s
        neg = jnp.finfo(jnp.float32).min
        resid = hidden_states
        x = layer_norm(hidden_states, ln1_w, ln1_b)
        q = (x @ q_w + q_b) / math.sqrt(HEAD)
        k = x @ k_w + k_b
        v = x @ v_w + v_b
        split = lambda t: t.reshape(b, s, H, HEAD).transpose(0, 2, 1, 3)
        q, k, v = (split(q), split(k), split(v))
        scores = jnp.einsum('bhqd,bhkd->bhqk', q, k)
        causal = jnp.tril(jnp.ones((s, s), bool))
        scores = jnp.where(causal, scores, neg)
        attn = jax.nn.softmax(scores, axis=-1)
        ctx = jnp.einsum('bhqk,bhkd->bhqd', attn, v)
        ctx = ctx.transpose(0, 2, 1, 3).reshape(b, s, D)
        hidden = resid + (ctx @ o_w + o_b)
        resid = hidden
        xt = layer_norm(hidden, ln2_w, ln2_b).reshape(T, D)
        logits = xt @ router_w
        probs = jax.nn.softmax(logits, axis=-1)
        top1 = jnp.argmax(probs, axis=-1)
        m1 = jax.nn.one_hot(top1, E, dtype=jnp.float32)
        logits_no1 = jnp.where(m1 > 0, -jnp.inf, logits)
        top2 = jnp.argmax(logits_no1, axis=-1)
        m2 = jax.nn.one_hot(top2, E, dtype=jnp.float32)
        loc1 = jnp.cumsum(m1, axis=0) - 1.0
        loc2 = jnp.cumsum(m2, axis=0) - 1.0 + m1.sum(axis=0, keepdims=True)
        C = 2 * math.ceil(T / E)
        m1 = m1 * (loc1 < C)
        m2 = m2 * (loc2 < C)
        g1 = (probs * m1).sum(-1)
        g2 = (probs * m2).sum(-1)
        denom = jnp.maximum(g1 + g2, jnp.finfo(jnp.float32).eps)
        g1, g2 = (g1 / denom, g2 / denom)
        slot1 = (loc1 * m1).sum(-1).astype(jnp.int32)
        slot2 = (loc2 * m2).sum(-1).astype(jnp.int32)
        d1 = m1[:, :, None] * jax.nn.one_hot(slot1, C, dtype=jnp.float32)[:, None, :]
        d2 = m2[:, :, None] * jax.nn.one_hot(slot2, C, dtype=jnp.float32)[:, None, :]
        dispatch = d1 + d2
        combine = g1[:, None, None] * d1 + g2[:, None, None] * d2
        xin = jnp.einsum('tec,td->ecd', dispatch, xt)
        h = jnp.einsum('ecd,edf->ecf', xin, fc1_w) + fc1_b[:, None, :]
        h = jax.nn.gelu(h, approximate=False)
        eout = jnp.einsum('ecf,efd->ecd', h, fc2_w) + fc2_b[:, None, :]
        eout = eout * (1.0 - MOE_TOKEN_DROPOUT)
        moe_out = jnp.einsum('tec,ecd->td', combine, eout).reshape(b, s, D)
        return resid + moe_out

    def _L1_attn_ref(x, Wq, Wk, Wv, Wo):
        import jax, jax.numpy as jnp
        import numpy as np
        NUM_HEADS = 16
        THETA = 10000.0

        def _rotate_half(x):
            x = x.reshape(x.shape[:-1] + (-1, 2))
            x1, x2 = (x[..., 0], x[..., 1])
            return jnp.stack((-x2, x1), axis=-1).reshape(x.shape[:-2] + (-1,))

        def _rope(x):
            d_k = x.shape[-1]
            seq_len = x.shape[-2]
            inv_freq = 1.0 / THETA ** (jnp.arange(0, d_k, 2, dtype=jnp.float32) / d_k)
            pos = jnp.arange(seq_len, dtype=jnp.float32)
            theta = pos[:, None] * inv_freq[None, :]
            cos = jnp.repeat(jnp.cos(theta), 2, axis=-1)
            sin = jnp.repeat(jnp.sin(theta), 2, axis=-1)
            return x * cos + _rotate_half(x) * sin
        B, S, D = x.shape
        H = NUM_HEADS
        d_k = D // H

        def split_heads(t):
            return t.reshape(B, S, H, d_k).transpose(0, 2, 1, 3)
        Q = split_heads(x @ Wq)
        K = split_heads(x @ Wk)
        V = split_heads(x @ Wv)
        Q = _rope(Q)
        K = _rope(K)
        scores = jnp.einsum('bhqd,bhkd->bhqk', Q, K) / jnp.sqrt(jnp.float32(d_k))
        causal = jnp.tril(jnp.ones((S, S), dtype=bool))
        scores = jnp.where(causal[None, None], scores, -jnp.inf)
        attn = jax.nn.softmax(scores, axis=-1)
        out = jnp.einsum('bhqk,bhkd->bhqd', attn, V)
        out = out.transpose(0, 2, 1, 3).reshape(B, S, D)
        return out @ Wo

    def _L1_xattn_ref(query, key, value, mask, Wq, bq, Wk, bk, Wv, bv, Wo, bo):
        import jax, jax.numpy as jnp
        import numpy as np
        NUM_HEADS = 16
        B, S, D = query.shape
        H = NUM_HEADS
        dh = D // H

        def split_heads(x):
            return x.reshape(B, S, H, dh).transpose(0, 2, 1, 3)
        q = split_heads(query @ Wq + bq) * (1.0 / jnp.sqrt(jnp.float32(dh)))
        k = split_heads(key @ Wk + bk)
        v = split_heads(value @ Wv + bv)
        scores = jnp.einsum('bhqd,bhkd->bhqk', q, k)
        m = mask.reshape(B, 1, 1, S).astype(scores.dtype)
        scores = scores - 1e+30 * (1.0 - m)
        weights = jax.nn.softmax(scores, axis=-1)
        context = jnp.einsum('bhqk,bhkd->bhqd', weights, v)
        context = context.transpose(0, 2, 1, 3).reshape(B, S, D)
        return context @ Wo + bo

    def _L1_ffn_ref(x, Wg, W1, b1, W2, b2):
        import jax, jax.numpy as jnp
        import numpy as np
        TOP_K = 2
        B, T, D = x.shape
        N = B * T
        xf = x.reshape(N, D)
        logits = jnp.einsum('nd,ed->ne', xf, Wg)
        top_logits, top_idx = jax.lax.top_k(logits, TOP_K)
        top_w = jax.nn.softmax(top_logits, axis=-1)
        h = jax.nn.gelu(jnp.einsum('nd,ehd->neh', xf, W1) + b1[None], approximate=False)
        all_out = jnp.einsum('neh,edh->ned', h, W2) + b2[None]
        selected = jnp.take_along_axis(all_out, top_idx[:, :, None], axis=1)
        out = jnp.sum(selected * top_w[:, :, None], axis=1)
        return out.reshape(B, T, D)
    x = x + _L0_attn_ref(_layernorm(x, axis=-1), L0_attn_w_qkv, L0_attn_w_out, L0_attn_b_out)
    x = x + _L0_xattn_ref(_layernorm(x, axis=-1), ctx_1024, ctx_1024, L0_xattn_Wq, L0_xattn_bq, L0_xattn_Wk, L0_xattn_bk, L0_xattn_Wv, L0_xattn_bv, L0_xattn_Wo, L0_xattn_bo)
    x = x + _L0_ffn_ref(_layernorm(x, axis=-1), L0_ffn_ln1_w, L0_ffn_ln1_b, L0_ffn_q_w, L0_ffn_q_b, L0_ffn_k_w, L0_ffn_k_b, L0_ffn_v_w, L0_ffn_v_b, L0_ffn_o_w, L0_ffn_o_b, L0_ffn_ln2_w, L0_ffn_ln2_b, L0_ffn_router_w, L0_ffn_fc1_w, L0_ffn_fc1_b, L0_ffn_fc2_w, L0_ffn_fc2_b)
    x = x + _L1_attn_ref(_layernorm(x, axis=-1), L1_attn_Wq, L1_attn_Wk, L1_attn_Wv, L1_attn_Wo)
    x = x + _L1_xattn_ref(_layernorm(x, axis=-1), ctx_1024, ctx_1024, mask_BxS2_ff1, L1_xattn_Wq, L1_xattn_bq, L1_xattn_Wk, L1_xattn_bk, L1_xattn_Wv, L1_xattn_bv, L1_xattn_Wo, L1_xattn_bo)
    x = x + _L1_ffn_ref(_layernorm(x, axis=-1), L1_ffn_Wg, L1_ffn_W1, L1_ffn_b1, L1_ffn_W2, L1_ffn_b2)
    return x

_drawn_inputs = setup_inputs


def setup_inputs(seed=0):
    import zlib

    import numpy as np

    out = dict(_drawn_inputs(seed))
    spreads = {'L0_xattn_bq': (0.0, 0.388),
     'L0_xattn_bk': (0.0, 0.8),
     'L0_xattn_bv': (0.0, 0.1),
     'L0_xattn_bo': (0.0, 0.1),
     'L0_ffn_ln1_w': (1.0, 0.6),
     'L0_ffn_ln1_b': (0.0, 0.8),
     'L0_ffn_q_b': (0.0, 0.8),
     'L0_ffn_k_b': (0.0, 0.8),
     'L0_ffn_v_b': (0.0, 0.767),
     'L0_ffn_o_b': (0.0, 0.1),
     'L0_ffn_ln2_w': (1.0, 0.6),
     'L0_ffn_ln2_b': (0.0, 0.607),
     'L0_ffn_fc1_b': (0.0, 0.8),
     'L0_ffn_fc2_b': (0.0, 0.313),
     'L1_xattn_bq': (0.0, 0.8),
     'L1_xattn_bk': (0.0, 0.8),
     'L1_xattn_bv': (0.0, 0.1),
     'L1_xattn_bo': (0.0, 0.1)}
    factors = {'L0_ffn_q_w': 8.0,
     'L0_ffn_k_w': 8.0,
     'L0_ffn_v_w': 4.237,
     'L0_ffn_o_w': 3.759,
     'L0_ffn_fc1_w': 3.906,
     'L0_ffn_fc2_w': 3.565,
     'L1_attn_Wq': 8.0,
     'L1_attn_Wk': 8.0,
     'L1_ffn_Wg': 3.964,
     'L1_ffn_W1': 3.747,
     'L1_ffn_b1': 8.0,
     'L1_ffn_W2': 3.689,
     'L1_ffn_b2': 8.0}
    for name, (base, spread) in spreads.items():
        noise = np.random.default_rng([zlib.crc32(name.encode()), seed]).standard_normal(out[name].shape)
        drawn = base * np.exp(spread * noise) if base else spread * noise
        out[name] = jnp.asarray(drawn.astype(out[name].dtype))
    for name, factor in factors.items():
        out[name] = (out[name] * factor).astype(out[name].dtype)
    return out
```

```python
from contextlib import ExitStack

import numpy as np

import concourse.bass as bass
from concourse import mybir

F32 = mybir.dt.float32
BF16 = mybir.dt.bfloat16
I32 = mybir.dt.int32
U32 = mybir.dt.uint32
ALU = mybir.AluOpType
ACT = mybir.ActivationFunctionType
X_AXIS = mybir.AxisListType.X

B, S, D, H, HD = 32, 128, 128, 16, 8
T = B * S
GROUPS, PER = 4, 4
HALF = 8
SCALE = HD ** -0.5
EPS = 1e-5
BIG = 1e30
WINDOW = 64
F = 512
FCH = F // 128

STAGES = [
    dict(name="L0_attn", cross=False, mask="window", rope=False, bo=True, inner=False),
    dict(name="L0_xattn", cross=True, mask=None, rope=False, bo=True, inner=False),
    dict(name="L0_ffn", cross=False, mask="causal", rope=False, bo=True, inner=True),
    dict(name="L1_attn", cross=False, mask="causal", rope=True, bo=False, inner=False),
    dict(name="L1_xattn", cross=True, mask="keys", rope=False, bo=True, inner=False),
]
COL_BQ, COL_BK, COL_BV = 0, 5, 10
COL_LN1W, COL_LN1B, COL_LN2W, COL_LN2B, COL_ONE, COL_ZERO = 15, 16, 17, 18, 19, 20
NCOL = 21
W_SWQ, W_SWK, NW = 20, 21, 22

MOE = [dict(E=16, R=512, tiles=16, cap=2 * T // 16, factor=0.8),
       dict(E=8, R=256, tiles=(2 * T + 8 * 255) // 256, cap=None, factor=1.0)]
ROWS = [MOE[0]["E"] * MOE[0]["cap"], MOE[1]["R"] * MOE[1]["tiles"]]
ONEHOT, DIFFS, ROUTED = (2, 50), (4, 51), (48, 85)
N_ZERO = 2 * 1 + 2 * 2
PACK = F + F + FCH + 128


def build(nc, x_in, ctx_in, keymask_in, weights_in, cols_in, rows_in, router_in, pack0_in, pack1_in,
          ident_in, masks_in, row_head_in, max_head_in, rope_in, iotas_in, restart_in, lower_in, out, stop=99):
    xin = [nc.dram_tensor(f"expert_in{l}", (ROWS[l] + 2 * T, D), F32).ap() for l in range(2)]
    eout = [nc.dram_tensor(f"expert_out{l}", (ROWS[l], D), F32).ap() for l in range(2)]
    packs = [pack0_in, pack1_in]

    with ExitStack() as ctx:
        def sb(name, shape, dt=F32):
            return ctx.enter_context(nc.sbuf_tensor(name, shape, dt))

        def sem(name):
            return ctx.enter_context(nc.semaphore(name))

        x_all = sb("x_all", [128, B, D])
        h_all = sb("h_all", [128, B, D])
        weights = sb("weights", [128, NW, 128])
        cols = sb("cols", [128, NCOL])
        rows = sb("rows", [1, 5, 128])
        router = sb("router", [128, 2, 16])
        ident = sb("ident", [128, 128])
        ident_bf = sb("ident_bf", [128, 128], BF16)
        masks = sb("masks", [128, 4, 512], BF16)
        ones_bf = sb("ones_bf", [128, 512], BF16)
        ones_row = sb("ones_row", [1, 128])
        row_head = sb("row_head", [128, HALF])
        max_head = sb("max_head", [128, PER])
        rope = sb("rope", [128, 2, 128])
        iotas = sb("iotas", [128, 96])
        restart = sb("restart", [128, 512])
        lower = sb("lower", [128, 128])
        lower_bf = sb("lower_bf", [128, 128], BF16)
        stats = sb("stats", [128, 2, 6])
        meanvar = sb("meanvar", [128, 2, 2])
        vareps = sb("vareps", [128, 2])
        rstd = sb("rstd", [128, 2])
        neghalf = sb("neghalf", [128, 1])
        ones_e = sb("ones_e", [128, 16])
        xn = sb("xn", [128, 2, D])
        xT = sb("xT", [128, 2, S])
        ctxT = sb("ctxT", [128, 2, S])
        raw = sb("raw", [128, 2, 4, S])
        prod = sb("prod", [128, 2, 4, S])
        qT = sb("qT", [128, 2, S])
        q_bf = sb("q_bf", [128, 2, S], BF16)
        kT = sb("kT", [128, 2, S])
        v_aug = sb("v_aug", [128, 2, H, HD + 1])
        q_masked = sb("q_masked", [128, 2, HALF, S])
        k_masked = sb("k_masked", [128, 2, HALF, S], BF16)
        keyrow = sb("keyrow", [1, 2, S])
        keyrow_bf = sb("keyrow_bf", [128, 2, S], BF16)
        negmax = sb("negmax", [128, 2, GROUPS, 32])
        shift = sb("shift", [128, 2, PER, S], BF16)
        probs = sb("probs", [128, 2, H, S])
        masks_f32 = probs[:, 0].rearrange("p h s -> p (h s)")
        o_sb = sb("o_sb", [128, 2, 4, S])
        rden = sb("rden", [128, 2, H])
        att = sb("att", [128, 2, D])
        attT = sb("attT", [128, 2, S])
        bank = [ctx.enter_context(nc.psum_tensor(f"bank{i}", [128, 512], F32)) for i in range(8)]
        rowmax_bank, score_bank, o_bank, ot_bank, kv_bank, misc_bank = (
            bank[0:2], bank[2:4], bank[4], bank[5], bank[6], bank[7])
        XT_COLS, Q_COLS, QSW_COLS, NEGMAX_COLS = (slice(128 * i, 128 * i + 128) for i in range(4))
        K_COLS, V_COLS, KSW_COLS = (slice(128 * i, 128 * i + 128) for i in range(3))
        lg = sb("lg", [128, 2, 16])
        top = sb("top", [128, 2, 8])
        topi = sb("topi", [128, 2, 8], U32)
        logits = sb("logits", [128, B, 16])
        top_all = sb("top_all", [128, B, 2])
        choice = sb("choice", [128, B, 2])
        onehot = sb("onehot", [128, 2, B, 16], BF16)
        total = sb("total", [128, 2, 16, B])
        upto = sb("upto", [128, 2, 16, B])
        place = sb("place", [128, 2, B, 16])
        zexp = sb("zexp", [128, B, 16])
        small = sb("small", [128, 16, B])
        per_e = sb("per_e", [128, 8, 16])
        per_ei = sb("per_ei", [128, 2, 16], I32)
        tile_cmp = sb("tile_cmp", [128, 48, 16])
        tile_f = sb("tile_f", [128, 48])
        tile_expert = sb("tile_expert", [128, 48], I32)
        dest = sb("dest", [128, 2, B], I32)
        source = sb("source", [128, 2, B], I32)
        weight = sb("weight", [128, 2, B])
        index = sb("index", [128, 2, 2], I32)
        moved = sb("moved", [128, 2, 2, D])
        pack = sb("pack", [128, 2, PACK])
        tile_rows = sb("tile_rows", [128, 2, 4, D])
        rowsT = sb("rowsT", [128, 2, 512])
        hidden = sb("hidden", [128, 2, FCH, 512])
        rows_out = sb("rows_out", [128, 2, 4, D])

        const_in, setup_done, zero_in = sem("const_in"), sem("setup_done"), sem("zero_in")
        x_in_sem = [sem(f"x_in{c}") for c in range(4)]
        ctx_in_sem = [sem(f"ctx_in{p}") for p in range(2)]
        key_in_sem = [sem(f"key_in{p}") for p in range(2)]
        pack_in_sem = [sem(f"pack_in{p}") for p in range(2)]
        tile_in_sem = [sem(f"tile_in{p}") for p in range(2)]
        stored = [sem(f"stored{p}") for p in range(2)]
        scattered = [sem(f"scattered{p}") for p in range(2)]
        gathered = [sem(f"gathered{p}") for p in range(2)]
        (stats_done, aggr_done, vareps_done, rstd_done, xn_done, xT_ps, xT_done, q_ps, kv_ps, q_bf_done,
         q_masked_done, k_done, v_done, k_masked_done, rowmax_ps, max_done, negmaxT_ps, shift_done,
         score_ps, exp_done, pv_ps, o_done, oT_ps, rden_done, att_done, attT_ps, attT_done, y_ps,
         hidden_kept, h2_done, resid_done, keyrow_done, rawk_done, rawq_done, qprod_done, qT_done,
         kprod_done, r_stats_done, r_aggr_done, r_vareps_done, r_rstd_done, r_xs_done, r_xT_ps,
         r_xT_done, r_logit_ps, r_logit_done, r_top_done, r_topi_done, r_kept, r_copied, routed_dve,
         routed_pe, routed_act, index_done, moved_done, mix_half, mix_done, rowsT_ps, rowsT_done,
         fc1_ps, gelu_done, fc2_ps, rows_out_done, written) = (sem(n) for n in (
            "stats_done aggr_done vareps_done rstd_done xn_done xT_ps xT_done q_ps kv_ps q_bf_done "
            "q_masked_done k_done v_done k_masked_done rowmax_ps max_done negmaxT_ps shift_done "
            "score_ps exp_done pv_ps o_done oT_ps rden_done att_done attT_ps attT_done y_ps "
            "hidden_kept h2_done resid_done keyrow_done rawk_done rawq_done qprod_done qT_done "
            "kprod_done r_stats_done r_aggr_done r_vareps_done r_rstd_done r_xs_done r_xT_ps "
            "r_xT_done r_logit_ps r_logit_done r_top_done r_topi_done r_kept r_copied routed_dve "
            "routed_pe routed_act index_done moved_done mix_half mix_done rowsT_ps rowsT_done "
            "fc1_ps gelu_done fc2_ps rows_out_done written").split())

        carried = {e: sem(f"carried_{n}") for e, n in ((nc.tensor.engine, "pe"), (nc.vector.engine, "dve"),
                                                     (nc.gpsimd.engine, "pool"))}

        def steps(eng, lag, body, total=B, first=2):
            lead = max(first, lag + lag % 2)
            turns = (total - lead) // 2
            for t in range(lead):
                body(t, t % 2)
            with eng.Fori(0, turns) as i:
                for u in range(2):
                    body(i * 2 + (lead + u), u)
            for t in range(lead + 2 * turns, total + lag):
                body(t, t % 2)

        def item(t, par, lag, total=B):
            b = t - lag
            if isinstance(b, int) and not 0 <= b < total:
                return None, None
            return b, (par + lag) % 2

        def after(eng, semaphore, count):
            if not (isinstance(count, int) and count <= 0):
                eng.wait_ge(semaphore, count)

        def apart(eng, *waits):
            for semaphore, count in waits:
                after(eng, semaphore, count)
            eng.sem_inc(carried[eng.engine])

        def start(eng):
            eng.wait_ge(const_in, 16 * N_CONST)
            eng.wait_ge(setup_done, SETUP)

        N_CONST, SETUP = 12, 12
        block = ctx.enter_context(nc.Block())

        @block.sync
        def _(sp):
            def load_x(c):
                sp.dma_start(x_all[:, 8 * c:8 * c + 8, :],
                             x_in[8 * c:8 * c + 8].rearrange("b t d -> t b d")).then_inc(x_in_sem[c], 16)

            load_x(0)
            for dst, src in ((ident, ident_in), (weights, weights_in), (cols, cols_in), (rows, rows_in),
                             (row_head, row_head_in), (max_head, max_head_in), (rope, rope_in),
                             (router, router_in), (iotas, iotas_in), (restart, restart_in),
                             (lower, lower_in)):
                sp.dma_start(dst[:], src).then_inc(const_in, 16)
            sp.dma_start(masks_f32, masks_in.rearrange("p m c -> p (m c)")).then_inc(const_in, 16)
            for c in range(1, 4):
                load_x(c)
            sp.wait_ge(setup_done, SETUP)
            zeros = hidden[:].rearrange("p a b c -> p (a b c)")
            for l in range(2):
                tiles = xin[l][0:ROWS[l], :].rearrange("(a p r) d -> a p (r d)", p=128, r=ROWS[l] // 256)
                for a in range(2):
                    for lo in range(0, tiles.shape[2], 4096):
                        w = min(4096, tiles.shape[2] - lo)
                        sp.dma_start(tiles[a, :, lo:lo + w], zeros[:, 0:w]).then_inc(zero_in, 16)

            def attention(n, st):
                cross = sum(x["cross"] for x in STAGES[:n])

                def body(t, par):
                    b, p = item(t, par, 0)
                    after(sp, kv_ps, B * n + b - 1)
                    sp.dma_start(ctxT[:, p, :], ctx_in[:, bass.ts(b, S)]).then_inc(ctx_in_sem[p], 16)
                    if st["mask"] == "keys":
                        after(sp, keyrow_done, b - 1)
                        sp.dma_start(keyrow[:, p, :], keymask_in[:, bass.ts(b, S)]).then_inc(key_in_sem[p], 16)
                if st["cross"]:
                    steps(sp, 0, body)

            def experts(l):
                m = MOE[l]
                R, blocks, base = m["R"], m["R"] // 128, sum(x["tiles"] for x in MOE[:l])
                for p in range(2):
                    sp.wait_ge(scattered[p], 16 * 2 * 16 * (l + 1))
                sp.wait_ge(zero_in, 16 * N_ZERO)
                if l == 1:
                    sp.wait_ge(routed_dve, ROUTED[1])

                def body(t, par):
                    a, p = item(t, par, 0, m["tiles"])
                    if a is not None:
                        g = base + a
                        expert = a if l == 0 else sp.value_load(tile_expert[0:1, bass.ds(a, 1)], min_val=0,
                                                               max_val=m["E"] - 1)
                        after(sp, fc2_ps, g - 1)
                        after(sp, rows_out_done, g - 1)
                        sp.dma_start(pack[:, p, :], packs[l][bass.ds(expert, 1)].rearrange("e p c -> (e p) c")) \
                            .then_inc(pack_in_sem[p], 16)
                        after(sp, rowsT_ps, g - 1)
                        sp.dma_start(tile_rows[:, p, 0:blocks, :],
                                     xin[l][bass.ts(a, R), :].rearrange("(r p) d -> p r d", p=128)) \
                            .then_inc(tile_in_sem[p], 16)
                    a, p = item(t, par, 2, m["tiles"])
                    if a is not None:
                        after(sp, rows_out_done, base + a + 1)
                        sp.dma_start(eout[l][bass.ts(a, R), :].rearrange("(r p) d -> p r d", p=128),
                                     rows_out[:, p, 0:blocks, :]).then_inc(stored[p], 16)
                steps(sp, 2, body, m["tiles"], 4)

            for n, st in enumerate(STAGES[:stop]):
                attention(n, st)
                if n == 2 and stop > 2:
                    experts(0)
            if stop > 5:
                experts(1)

                def body(t, par):
                    sp.wait_ge(mix_done, B + t + 1)
                    sp.dma_start(out[bass.ds(t, 1)].rearrange("b t d -> t (b d)"), x_all[:, t, :]) \
                        .then_inc(written, 16)
                steps(sp, 0, body)
                sp.wait_ge(written, 16 * B)
            else:
                sp.wait_ge(resid_done, B * min(stop, 5))
                if stop > 2:
                    sp.wait_ge(mix_done, B)
                sp.dma_start(out.rearrange("b t d -> t b d"), x_all[:]).then_inc(written, 16)
                sp.wait_ge(written, 16)

        @block.tensor
        def _(pe):
            def mm(dst, lhsT, rhs, first=True, last=True):
                return pe.matmul(dst, lhsT, rhs, start=first, stop=last)

            def attention(n, st):
                w = lambda k: weights[:, 4 * n + k, :]
                cross = sum(x["cross"] for x in STAGES[:n])
                mask_qk, mask_kq = {"window": (0, 1), "causal": (2, 3)}.get(st["mask"], (None, None))

                half = lambda gr: slice(64 * (gr // 2), 64 * (gr // 2) + 64)
                heads_of = lambda gr: slice(PER * (gr % 2), PER * (gr % 2) + PER)

                def row_scores(b, p, gr):
                    g, dst, part, heads = B * n + b, rowmax_bank[gr % 2], half(gr), heads_of(gr)
                    apart(pe, *([(k_masked_done, g + 1), (q_bf_done, g + 1)] if gr == 0 else []),
                          *([(keyrow_done, b + 1)] if gr == 0 and st["mask"] == "keys" else []),
                          (max_done, 4 * g + gr - 1))
                    ins = mm(dst[:], q_bf[part, p, :], k_masked[part, p, heads, :], last=st["mask"] is None)
                    if st["mask"] in ("window", "causal"):
                        ins = mm(dst[:], ident_bf[:], masks[:, mask_qk, :], first=False)
                    elif st["mask"] == "keys":
                        ins = mm(dst[:], ones_bf[:, 0:128],
                                 keyrow_bf[:, p, :].unsqueeze(1).to_broadcast([128, PER, S]), first=False)
                    ins.then_inc(rowmax_ps, 1)

                def key_scores(b, p, gr):
                    g, dst, rows_ = B * n + b, score_bank[gr % 2], slice(32 * gr, 32 * gr + 32)
                    if gr == 0:
                        after(pe, k_done, g + 1)
                        after(pe, q_masked_done, g + 1)
                        after(pe, shift_done, g + 1)
                    after(pe, exp_done, 4 * g + gr - 1)
                    mm(dst[:], kT[half(gr), p, :], q_masked[half(gr), p, heads_of(gr), :], last=False)
                    if st["mask"] in ("window", "causal"):
                        mm(dst[:], ident_bf[:], masks[:, mask_kq, :], first=False, last=False)
                    elif st["mask"] == "keys":
                        mm(dst[:], keyrow_bf[:, p, :], ones_bf[:], first=False, last=False)
                    mm(dst[:], ones_bf[rows_, 0:128], shift[rows_, p], first=False).then_inc(score_ps, 1)

                def body(t, par):
                    a, pa = item(t, par, 1)
                    c, pc = item(t, par, 2)
                    f, pf = item(t, par, 3)
                    if c is not None:
                        row_scores(c, pc, 0)
                        row_scores(c, pc, 1)
                    if f is not None:
                        g = B * n + f
                        after(pe, exp_done, 4 * g + 4)
                        after(pe, v_done, g + 1)
                        after(pe, resid_done, g)
                        for h in range(H):
                            ins = mm(o_bank[32 * (h % 4):32 * (h % 4) + HD + 1, 128 * (h // 4):128 * (h // 4) + 128],
                                     v_aug[:, pf, h, :], probs[:, pf, h, :])
                        ins.then_inc(pv_ps, 1)
                    if c is not None:
                        row_scores(c, pc, 2)
                        row_scores(c, pc, 3)
                    if a is not None:
                        g = B * n + a
                        after(pe, xn_done, g + 1)
                        after(pe, q_bf_done, g)
                        after(pe, q_masked_done, g)
                        after(pe, shift_done, g - 1)
                        pe.transpose(misc_bank[:, XT_COLS], xn[:, pa, :], ident[:]).then_inc(xT_ps, 1)
                    if f is not None:
                        g = B * n + f
                        after(pe, o_done, g + 1)
                        after(pe, attT_done, g)
                        for j in range(4):
                            ins = pe.transpose(ot_bank[:, 128 * j:128 * j + 128], o_sb[:, pf, j, :], ident[:])
                        ins.then_inc(oT_ps, 1)
                    if c is not None:
                        g = B * n + c
                        after(pe, max_done, 4 * g + 4)
                        if a is not None:
                            after(pe, xT_done, g + 2)
                        else:
                            after(pe, q_masked_done, g + 1)
                        pe.transpose(misc_bank[:, NEGMAX_COLS], negmax[:, pc].rearrange("p g j -> p (g j)"),
                                     ident[:]).then_inc(negmaxT_ps, 1)
                    if a is not None:
                        g = B * n + a
                        src = ctxT if st["cross"] else xT
                        after(pe, xT_done, g + 1)
                        after(pe, shift_done, g)
                        ins = mm(misc_bank[:, Q_COLS], w(0), xT[:, pa, :])
                        if st["rope"]:
                            ins = mm(misc_bank[:, QSW_COLS], weights[:, W_SWQ, :], xT[:, pa, :])
                        ins.then_inc(q_ps, 1)
                        if st["cross"]:
                            pe.wait_ge(ctx_in_sem[pa], (a // 2 + (16 * cross + 1)) * 16)
                        after(pe, k_done, g)
                        after(pe, v_done, g)
                        mm(kv_bank[:, K_COLS], w(1), src[:, pa, :])
                        if st["rope"]:
                            mm(kv_bank[:, KSW_COLS], weights[:, W_SWK, :], src[:, pa, :])
                        mm(kv_bank[:, V_COLS], src[:, pa, :], w(2)).then_inc(kv_ps, 1)
                    if f is not None:
                        after(pe, att_done, B * n + f + 1)
                        pe.transpose(ot_bank[:, 0:128], att[:, pf, :], ident[:]).then_inc(attT_ps, 1)
                    if c is not None:
                        key_scores(c, pc, 0)
                    if f is not None:
                        after(pe, attT_done, B * n + f + 1)
                        ins = mm(o_bank[:, 0:D], attT[:, pf, :], w(3), last=not st["bo"])
                        if st["bo"]:
                            ins = mm(o_bank[:, 0:D], ones_row[:], rows[:, n, :], first=False)
                        ins.then_inc(y_ps, 1)
                    if c is not None:
                        for gr in range(1, 4):
                            key_scores(c, pc, gr)
                steps(pe, 3, body)

            def route(l):
                def body(t, par):
                    b, p = item(t, par, 1)
                    if b is None:
                        return
                    g = B * l + b
                    after(pe, r_xs_done, g + 1)
                    after(pe, r_xT_done, g)
                    pe.transpose(misc_bank[:, XT_COLS], xn[:, p, :], ident[:]).then_inc(r_xT_ps, 1)
                    after(pe, r_xT_done, g + 1)
                    after(pe, r_logit_done, g)
                    mm(ot_bank[:, 0:16], xT[:, p, :], router[:, l, :]).then_inc(r_logit_ps, 1)
                steps(pe, 2, body, first=4)
                pe.wait_ge(routed_dve, ONEHOT[l])
                for k in range(2):
                    rhs = onehot[:, k].rearrange("p b e -> p (b e)")
                    mm(bank[2 * k][:], lower_bf[:], rhs)
                    ins = mm(bank[2 * k + 1][:], ones_bf[:, 0:128], rhs)
                ins.then_inc(routed_pe, 1)

            def experts(l):
                m = MOE[l]
                R, blocks, base = m["R"], m["R"] // 128, sum(x["tiles"] for x in MOE[:l])
                pe.wait_ge(routed_dve, ROUTED[l])

                def body(t, par):
                    a, p = item(t, par, 1, m["tiles"])
                    if a is not None:
                        g = base + a
                        pe.wait_ge(pack_in_sem[p], (a // 2 + (base // 2 + 1)) * 16)
                        after(pe, rowsT_done, g + 1)
                        for f in range(FCH):
                            after(pe, gelu_done, 4 * g + (f - 3))
                            mm(bank[f][:, 0:R], pack[:, p, 128 * f:128 * f + 128], rowsT[:, p, 0:R]) \
                                .then_inc(fc1_ps, 1)
                    d, q = item(t, par, 0, m["tiles"])
                    if d is not None:
                        g = base + d
                        pe.wait_ge(tile_in_sem[q], (d // 2 + (base // 2 + 1)) * 16)
                        after(pe, rowsT_done, g)
                        for r in range(blocks):
                            ins = pe.transpose(ot_bank[:, 128 * r:128 * r + 128], tile_rows[:, q, r, :], ident[:])
                        ins.then_inc(rowsT_ps, 1)
                    if a is not None:
                        g = base + a
                        after(pe, gelu_done, 4 * g + 4)
                        after(pe, rows_out_done, g - 1)
                        for r in range(blocks):
                            for f in range(FCH):
                                ins = mm((o_bank, kv_bank)[p][:, 128 * r:128 * r + 128],
                                         hidden[:, p, f, 128 * r:128 * r + 128],
                                         pack[:, p, F + 128 * f:F + 128 * f + 128], f == 0, f == FCH - 1)
                        ins.then_inc(fc2_ps, 1)
                steps(pe, 2, body, m["tiles"], 4)

            start(pe)
            for n, st in enumerate(STAGES[:stop]):
                attention(n, st)
                if n == 2 and stop > 2:
                    route(0)
                    experts(0)
            if stop > 5:
                route(1)
                experts(1)

        @block.scalar
        def _(act):
            col = lambda i: cols[:, i:i + 1]

            def attention(n, st):
                def body(t, par):
                    a, pa = item(t, par, 1)
                    c, pc = item(t, par, 2)
                    f, pf = item(t, par, 3)
                    if f is not None:
                        g = B * n + f
                        after(act, pv_ps, g + 1)
                        after(act, oT_ps, g - 1)
                        act.activation(o_sb[:, pf].rearrange("p j q -> p (j q)"), o_bank[:], ACT.Copy) \
                            .then_inc(o_done, 1)
                    if a is not None:
                        g = B * n + a
                        after(act, xT_ps, g + 1)
                        after(act, kv_ps, g - 1)
                        if st["inner"]:
                            ins = act.activation(xT[:, pa, :], misc_bank[:, XT_COLS], ACT.Identity,
                                                 bias=col(COL_LN1B), scale=col(COL_LN1W))
                        else:
                            ins = act.activation(xT[:, pa, :], misc_bank[:, XT_COLS], ACT.Copy)
                        ins.then_inc(xT_done, 1)
                        after(act, kv_ps, g + 1)
                        if st["rope"]:
                            after(act, k_done, g - 1)
                            act.activation(raw[:, pa, 2:4, :],
                                           kv_bank[:].rearrange("p (j s) -> p j s", s=S)[:, 0:3:2, :],
                                           ACT.Copy).then_inc(rawk_done, 1)
                        else:
                            after(act, k_masked_done, g - 1)
                            after(act, score_ps, 4 * g - 4)
                            act.activation(kT[:, pa, :], kv_bank[:, K_COLS], ACT.Identity,
                                           bias=col(COL_BK + n)).then_inc(k_done, 1)
                        after(act, pv_ps, g - 1)
                        act.activation(v_aug[:, pa, :, 0:HD],
                                       kv_bank[:, V_COLS].rearrange("p (h d) -> p h d", d=HD), ACT.Copy) \
                            .then_inc(v_done, 1)
                    if f is not None:
                        g = B * n + f
                        after(act, attT_ps, g + 1)
                        after(act, y_ps, g - 1)
                        act.activation(attT[:, pf, :], ot_bank[:, 0:128], ACT.Identity,
                                       bias=col(COL_BV + n)).then_inc(attT_done, 1)
                    if a is not None:
                        g = B * n + a
                        after(act, q_ps, g + 1)
                        if st["rope"]:
                            after(act, q_masked_done, g - 1)
                            act.activation(raw[:, pa, 0:2, :],
                                           misc_bank[:].rearrange("p (j s) -> p j s", s=S)[:, 1:3, :],
                                           ACT.Copy).then_inc(rawq_done, 1)
                            after(act, qT_done, a + 1)
                            after(act, rowmax_ps, 4 * g - 4)
                            act.activation(q_bf[:, pa, :], qT[:, pa, :], ACT.Copy).then_inc(q_bf_done, 1)
                        else:
                            after(act, rowmax_ps, 4 * g - 4)
                            act.activation(q_bf[:, pa, :], misc_bank[:, Q_COLS], ACT.Identity,
                                           bias=col(COL_BQ + n)).then_inc(q_bf_done, 1)
                    if c is not None:
                        g = B * n + c
                        after(act, pv_ps, g - 1)
                        for gr in range(GROUPS):
                            after(act, score_ps, 4 * g + gr + 1)
                            act.activation(probs[:, pc, PER * gr:PER * gr + PER, :], score_bank[gr % 2][:],
                                           ACT.Exp, scale=SCALE).then_inc(exp_done, 1)
                steps(act, 3, body)

            def route(l):
                def body(t, par):
                    b, p = item(t, par, 1)
                    if b is None:
                        return
                    g = B * l + b
                    after(act, r_xT_ps, g + 1)
                    after(act, r_logit_ps, g - 1)
                    if l == 0:
                        ins = act.activation(xT[:, p, :], misc_bank[:, XT_COLS], ACT.Identity,
                                             bias=col(COL_LN2B), scale=col(COL_LN2W))
                    else:
                        ins = act.activation(xT[:, p, :], misc_bank[:, XT_COLS], ACT.Copy)
                    ins.then_inc(r_xT_done, 1)
                steps(act, 2, body, first=4)
                act.wait_ge(routed_dve, DIFFS[l])
                act.activation(small[:, 2, :], small[:, 1, :], ACT.Exp).then_inc(routed_act, 1)
                if l == 0:
                    act.activation(zexp[:], logits[:], ACT.Exp).then_inc(routed_act, 1)

            def experts(l):
                m = MOE[l]
                R, base = m["R"], sum(x["tiles"] for x in MOE[:l])

                def body(t, par):
                    a, p = item(t, par, 1, m["tiles"])
                    if a is not None:
                        g = base + a
                        after(act, fc2_ps, g - 1)
                        for f in range(FCH):
                            after(act, fc1_ps, 4 * g + f + 1)
                            act.activation(hidden[:, p, f, 0:R], bank[f][:, 0:R], ACT.Gelu,
                                           bias=pack[:, p, 2 * F + f:2 * F + f + 1]).then_inc(gelu_done, 1)
                    d, q = item(t, par, 0, m["tiles"])
                    if d is not None:
                        g = base + d
                        after(act, rowsT_ps, g + 1)
                        after(act, fc1_ps, 4 * g - 4)
                        if l == 0:
                            ins = act.activation(rowsT[:, q, 0:R], ot_bank[:, 0:R], ACT.Identity,
                                                 bias=col(COL_LN2B), scale=col(COL_LN2W))
                        else:
                            ins = act.activation(rowsT[:, q, 0:R], ot_bank[:, 0:R], ACT.Copy)
                        ins.then_inc(rowsT_done, 1)
                steps(act, 2, body, m["tiles"], 4)

            start(act)
            for n, st in enumerate(STAGES[:stop]):
                attention(n, st)
                if n == 2 and stop > 2:
                    route(0)
                    experts(0)
            if stop > 5:
                route(1)
                experts(1)

        @block.vector
        def _(dve):
            seqs, seqs8 = [128, PER, S], [128, HALF, S]
            head_of_row = row_head[:].unsqueeze(2).to_broadcast(seqs8)
            head_of_max = max_head[:].unsqueeze(2).to_broadcast(seqs)
            routed = [0]

            def link(ins):
                routed[0] += 1
                ins.then_inc(routed_dve, 1)
                dve.wait_ge(routed_dve, routed[0])

            def attention(n, st):
                def norm_source(b):
                    if n == 0:
                        return
                    if n == 3:
                        dve.wait_ge(mix_done, b + 1)
                    else:
                        dve.wait_ge(resid_done, B * (n - 1) + b + 1)

                def body(t, par):
                    e, pe_ = item(t, par, 0)
                    a, pa = item(t, par, 1)
                    c, pc = item(t, par, 2)
                    f, pf = item(t, par, 3)

                    def maximum(gr):
                        g = B * n + c
                        after(dve, rowmax_ps, 4 * g + gr + 1)
                        if gr == 0:
                            after(dve, negmaxT_ps, g - 1)
                        dve.tensor_reduce(negmax[:, pc, gr, 0:PER],
                                          rowmax_bank[gr % 2][:].rearrange("p (h k) -> p h k", k=S),
                                          X_AXIS, ALU.max, negate=True).then_inc(max_done, 1)
                    if c is not None:
                        maximum(0)
                        maximum(1)
                    if e is not None:
                        g = B * n + e
                        if n == 0 and isinstance(e, int) and e in (0, 3):
                            for q in range(4) if e else range(1):
                                dve.wait_ge(x_in_sem[q], 16)
                        norm_source(e)
                        after(dve, aggr_done, g - 1)
                        dve.bn_stats(stats[:, pe_, :], x_all[:, e, :]).then_inc(stats_done, 1)
                    if c is not None:
                        maximum(2)
                    if e is not None:
                        g = B * n + e
                        apart(dve, (stats_done, g + 1),
                              (vareps_done, g - 1),
                              (xn_done, g - 1))
                        dve.bn_aggr(meanvar[:, pe_, :], stats[:, pe_, :]).then_inc(aggr_done, 1)
                    if c is not None:
                        maximum(3)
                    if f is not None:
                        g = B * n + f
                        per_head = ot_bank[:].rearrange("p (h c) -> p h c", c=32)
                        after(dve, oT_ps, g + 1)
                        after(dve, att_done, g - 1)
                        dve.reciprocal(rden[:, pf, :].unsqueeze(2), per_head[:, :, HD:HD + 1]).then_inc(rden_done, 1)
                        after(dve, rden_done, g + 1)
                        after(dve, attT_ps, g - 1)
                        dve.tensor_tensor(att[:, pf, :].rearrange("p (h d) -> p h d", d=HD),
                                          per_head[:, :, 0:HD],
                                          rden[:, pf, :].unsqueeze(2).to_broadcast([128, H, HD]),
                                          ALU.mult).then_inc(att_done, 1)
                    if c is not None:
                        g = B * n + c
                        after(dve, negmaxT_ps, g + 1)
                        after(dve, score_ps, 4 * g - 4)
                        dve.tensor_tensor(shift[:, pc], misc_bank[:, NEGMAX_COLS].unsqueeze(1).to_broadcast(seqs),
                                          head_of_max, ALU.mult).then_inc(shift_done, 1)
                    if e is not None:
                        g = B * n + e
                        after(dve, rstd_done, g + 1)
                        after(dve, xT_ps, g - 1)
                        if st["inner"]:
                            after(dve, hidden_kept, e - 1)
                        dve.tensor_scalar(xn[:, pe_, :], x_all[:, e, :], meanvar[:, pe_, 0:1], rstd[:, pe_:pe_ + 1],
                                          ALU.subtract, ALU.mult).then_inc(xn_done, 1)
                    if a is not None:
                        g = B * n + a
                        if st["mask"] == "keys":
                            dve.wait_ge(key_in_sem[pa], (a // 2 + 1) * 16)
                            after(dve, score_ps, 4 * g - 4)
                            dve.tensor_scalar(keyrow_bf[0:1, pa, :], keyrow[:, pa, :], BIG / SCALE, -BIG / SCALE,
                                              ALU.mult, ALU.add).then_inc(keyrow_done, 1)
                        if st["rope"]:
                            after(dve, rawq_done, a + 1)
                            after(dve, qT_done, a - 1)
                            dve.tensor_tensor(prod[:, pa, 0:2, :], raw[:, pa, 0:2, :], rope[:], ALU.mult) \
                                .then_inc(qprod_done, 1)
                            after(dve, qprod_done, a + 1)
                            after(dve, q_bf_done, g - 1)
                            dve.tensor_tensor(qT[:, pa, :], prod[:, pa, 0, :], prod[:, pa, 1, :], ALU.add) \
                                .then_inc(qT_done, 1)
                            after(dve, qT_done, a + 1)
                            after(dve, score_ps, 4 * g - 4)
                            dve.tensor_tensor(q_masked[:, pa], qT[:, pa, :].unsqueeze(1).to_broadcast(seqs8),
                                              head_of_row, ALU.mult).then_inc(q_masked_done, 1)
                        else:
                            after(dve, q_bf_done, g + 1)
                            after(dve, score_ps, 4 * g - 4)
                            dve.scalar_tensor_tensor(out=q_masked[:, pa],
                                                     in0=misc_bank[:, Q_COLS].unsqueeze(1).to_broadcast(seqs8),
                                                     scalar=cols[:, COL_BQ + n:COL_BQ + n + 1], in1=head_of_row,
                                                     op0=ALU.add, op1=ALU.mult).then_inc(q_masked_done, 1)
                    if f is not None:
                        g = B * n + f
                        after(dve, y_ps, g + 1)
                        if st["inner"]:
                            after(dve, hidden_kept, f + 1)
                            dve.tensor_tensor(h_all[:, f, :], h_all[:, f, :], o_bank[:, 0:D], ALU.add) \
                                .then_inc(h2_done, 1)
                            after(dve, h2_done, f + 1)
                            ins = dve.tensor_tensor(x_all[:, f, :], x_all[:, f, :], h_all[:, f, :], ALU.add)
                        else:
                            ins = dve.tensor_tensor(x_all[:, f, :], x_all[:, f, :], o_bank[:, 0:D], ALU.add)
                        ins.then_inc(resid_done, 1)
                steps(dve, 3, body)

            def route(l):
                m = MOE[l]
                E = m["E"]
                last = 3 if l == 0 else 5
                rows_of = h_all if l == 0 else x_all

                def body(t, par):
                    e, p = item(t, par, 0)
                    if e is not None:
                        g = B * l + e
                        dve.wait_ge(resid_done, B * (last - 1) + e + 1)
                        after(dve, r_aggr_done, g - 1)
                        dve.bn_stats(stats[:, p, :], rows_of[:, e, :]).then_inc(r_stats_done, 1)
                        apart(dve, (r_stats_done, g + 1),
                              (r_vareps_done, g - 1),
                              (r_xs_done, g - 1))
                        dve.bn_aggr(meanvar[:, p, :], stats[:, p, :]).then_inc(r_aggr_done, 1)
                    b, q = item(t, par, 2)
                    if b is not None:
                        g = B * l + b
                        after(dve, r_logit_ps, g + 1)
                        after(dve, r_copied, 3 * (g - 1))
                        dve.tensor_copy(lg[:, q, :], ot_bank[:, 0:16]).then_inc(r_logit_done, 1)
                        apart(dve, (r_logit_done, g + 1))
                        dve.max(top[:, q, :], lg[:, q, 0:E]).then_inc(r_top_done, 1)
                        apart(dve, (r_top_done, g + 1))
                        dve.max_index(topi[:, q, :], top[:, q, :], lg[:, q, 0:E]).then_inc(r_topi_done, 1)
                    if e is not None:
                        g = B * l + e
                        after(dve, r_rstd_done, g + 1)
                        after(dve, r_xT_ps, g - 1)
                        after(dve, r_kept, g - 1)
                        dve.tensor_scalar(xn[:, p, :], rows_of[:, e, :], meanvar[:, p, 0:1], rstd[:, p:p + 1],
                                          ALU.subtract, ALU.mult).then_inc(r_xs_done, 1)
                steps(dve, 2, body, first=4)
                dve.wait_ge(r_copied, 3 * B * (l + 1))
                for k in range(2):
                    link(dve.tensor_tensor(onehot[:, k], iotas[:, 0:16].unsqueeze(1).to_broadcast([128, B, 16]),
                                           choice[:, :, k:k + 1].to_broadcast([128, B, 16]), ALU.is_equal))
                assert routed[0] == ONEHOT[l]
                link(dve.tensor_tensor(small[:, 1, :], top_all[:, :, 1], top_all[:, :, 0], ALU.subtract))
                if l == 0:
                    link(dve.tensor_tensor(logits[:], logits[:], top_all[:, :, 0:1].to_broadcast([128, B, 16]),
                                           ALU.subtract))
                assert routed[0] == DIFFS[l]
                dve.wait_ge(routed_pe, l + 1)
                by_expert = lambda ap: ap.rearrange("p (b e) -> p e b", e=16)
                flat = lambda ap: ap.rearrange("p a b -> p (a b)")
                for k in range(2):
                    link(dve.tensor_copy(total[:, k], by_expert(bank[2 * k + 1][:])))
                    link(dve.tensor_tensor_scan(flat(upto[:, k]), restart[:], flat(total[:, k]), 0.0,
                                                ALU.mult, ALU.add))
                    link(dve.tensor_tensor(total[:, k], upto[:, k], total[:, k], ALU.subtract))
                    link(dve.tensor_tensor(place[:, k], bank[2 * k][:].rearrange("p (b e) -> p b e", e=16),
                                           total[:, k].rearrange("p e b -> p b e"), ALU.add))
                first, second = upto[:, 0, :, B - 1], upto[:, 1, :, B - 1]
                if l == 0:
                    link(dve.memset(per_e[:, 0, :], -1.0))
                else:
                    link(dve.tensor_tensor(per_e[:, 1, :], first, second, ALU.add))
                    link(dve.tensor_scalar(per_e[:, 1, :], per_e[:, 1, :], float(m["R"] - 1), None, ALU.add))
                    link(dve.tensor_copy(per_ei[:, 0, :], per_e[:, 1, :]))
                    link(dve.tensor_scalar(per_ei[:, 1, :], per_ei[:, 0, :], m["R"].bit_length() - 1, None,
                                           ALU.arith_shift_right))
                    link(dve.tensor_copy(per_e[:, 2, :], per_ei[:, 1, :]))
                    link(dve.tensor_tensor_scan(per_e[:, 3, :], ones_e[:], per_e[:, 2, :], 0.0, ALU.mult, ALU.add))
                    link(dve.tensor_tensor(per_e[:, 4, :], per_e[:, 3, :], per_e[:, 2, :], ALU.subtract))
                    link(dve.tensor_scalar(per_e[:, 0, :], per_e[:, 4, :], float(m["R"]), -1.0, ALU.mult, ALU.add))
                    link(dve.tensor_tensor(tile_cmp[:], per_e[:, 3, :].unsqueeze(1).to_broadcast([128, 48, 16]),
                                           iotas[:, 16:64].unsqueeze(2).to_broadcast([128, 48, 16]), ALU.is_le))
                    link(dve.tensor_reduce(tile_f[:], tile_cmp[:], X_AXIS, ALU.add))
                    link(dve.tensor_scalar(tile_f[:], tile_f[:], float(E - 1), None, ALU.min))
                    link(dve.tensor_copy(tile_expert[:], tile_f[:]))
                link(dve.tensor_tensor(per_e[:, 5, :], per_e[:, 0, :], first, ALU.add))
                for k, base in ((0, 0), (1, 5)):
                    link(dve.tensor_tensor(place[:, k], place[:, k],
                                           per_e[:, base, :].unsqueeze(1).to_broadcast([128, B, 16]), ALU.add))
                    link(dve.tensor_tensor(place[:, k], place[:, k], onehot[:, k], ALU.mult))
                    link(dve.tensor_reduce(small[:, 3 + k, :], place[:, k], X_AXIS, ALU.add))
                if l == 0:
                    tokens = iotas[:, 64:96]
                    for k in range(2):
                        slot, kept, row, spare = small[:, 3 + k, :], small[:, 5 + k, :], small[:, 7, :], small[:, 8, :]
                        link(dve.tensor_scalar(kept, slot, float(m["cap"]), None, ALU.is_lt))
                        link(dve.scalar_tensor_tensor(out=row, in0=choice[:, :, k], scalar=float(m["cap"]),
                                                      in1=slot, op0=ALU.mult, op1=ALU.add))
                        link(dve.tensor_scalar(spare, tokens, float(ROWS[0] + k * T), None, ALU.add))
                        link(dve.tensor_tensor(row, row, spare, ALU.subtract))
                        link(dve.tensor_tensor(row, row, kept, ALU.mult))
                        link(dve.tensor_tensor(row, row, spare, ALU.add))
                        link(dve.tensor_copy(dest[:, k, :], row))
                        link(dve.tensor_scalar(row, row, float(ROWS[0] - 1), None, ALU.min))
                        link(dve.tensor_copy(source[:, k, :], row))
                    dve.wait_ge(routed_act, 2)
                    z, g1, g2, den = (small[:, i, :] for i in (9, 10, 11, 12))
                    link(dve.tensor_reduce(z, zexp[:], X_AXIS, ALU.add))
                    link(dve.reciprocal(z, z))
                    link(dve.tensor_tensor(g1, small[:, 5, :], z, ALU.mult))
                    link(dve.tensor_tensor(g2, small[:, 6, :], z, ALU.mult))
                    link(dve.tensor_tensor(g2, g2, small[:, 2, :], ALU.mult))
                    link(dve.tensor_tensor(den, g1, g2, ALU.add))
                    link(dve.tensor_scalar(den, den, float(np.finfo(np.float32).eps), None, ALU.max))
                    link(dve.reciprocal(den, den))
                    for k, gk in enumerate((g1, g2)):
                        link(dve.scalar_tensor_tensor(out=weight[:, k, :], in0=gk, scalar=m["factor"], in1=den,
                                                      op0=ALU.mult, op1=ALU.mult))
                else:
                    for k in range(2):
                        link(dve.tensor_copy(dest[:, k, :], small[:, 3 + k, :]))
                        link(dve.tensor_copy(source[:, k, :], small[:, 3 + k, :]))
                    dve.wait_ge(routed_act, 3)
                    link(dve.tensor_scalar(small[:, 9, :], small[:, 2, :], 1.0, None, ALU.add))
                    link(dve.reciprocal(weight[:, 0, :], small[:, 9, :]))
                    link(dve.tensor_tensor(weight[:, 1, :], weight[:, 0, :], small[:, 2, :], ALU.mult))
                assert routed[0] == ROUTED[l], routed

                def send(t, par):
                    g = B * 2 * l + t
                    if isinstance(t, int) and t < 2:
                        for q in range(2):
                            after(dve, scattered[q], 16 * 32 * l)
                            after(dve, gathered[q], 16 * 32 * l)
                    else:
                        dve.wait_ge(scattered[par], (t // 2 + 16 * l) * 32)
                    dve.tensor_copy(index[:, par, :], dest[:, :, t]).then_inc(index_done, 1)
                    dve.wait_ge(r_kept, B * l + t + 1)
                    dve.tensor_copy(moved[:, par, 0, :], h_all[:, t, :]).then_inc(moved_done, 1)
                for t in range(2):
                    send(t, t)
                with dve.Fori(1, B // 2) as i:
                    for u in range(2):
                        send(i * 2 + u, u)

            def experts(l):
                m = MOE[l]
                blocks, base = m["R"] // 128, sum(x["tiles"] for x in MOE[:l])

                def body(t, par):
                    a, p = item(t, par, 1, m["tiles"])
                    if a is None:
                        return
                    g = base + a
                    after(dve, fc2_ps, g + 1)
                    if not (isinstance(a, int) and g < 2):
                        dve.wait_ge(stored[p], (a // 2 + base // 2) * 16)
                    dve.tensor_tensor(rows_out[:, p, 0:blocks, :],
                                      (o_bank, kv_bank)[p][:, 0:128 * blocks].rearrange("p (r d) -> p r d", d=D),
                                      pack[:, p, 2 * F + FCH:].unsqueeze(1).to_broadcast([128, blocks, D]),
                                      ALU.add).then_inc(rows_out_done, 1)
                steps(dve, 2, body, m["tiles"], 4)

            def mix(l):
                def fetch(t, par):
                    if isinstance(t, int) and t < 2:
                        dve.wait_ge(scattered[par], 16 * 32 * (l + 1))
                    else:
                        dve.wait_ge(gathered[par], (t // 2 + 16 * l) * 32)
                    dve.tensor_copy(index[:, par, :], source[:, :, t]).then_inc(index_done, 1)

                def add(t, par):
                    dve.wait_ge(gathered[par], (t // 2 + 16 * l + 1) * 32)
                    dve.scalar_tensor_tensor(out=x_all[:, t, :], in0=moved[:, par, 0, :], scalar=weight[:, 0, bass.ds(t, 1)],
                                             in1=x_all[:, t, :], op0=ALU.mult, op1=ALU.add).then_inc(mix_half, 1)
                    dve.wait_ge(mix_half, B * l + t + 1)
                    dve.scalar_tensor_tensor(out=x_all[:, t, :], in0=moved[:, par, 1, :], scalar=weight[:, 1, bass.ds(t, 1)],
                                             in1=x_all[:, t, :], op0=ALU.mult, op1=ALU.add).then_inc(mix_done, 1)

                def body(t, par):
                    f, pf = item(t, par, 0)
                    if f is not None:
                        fetch(f, pf)
                    a, pa = item(t, par, 1)
                    if a is not None:
                        add(a, pa)
                steps(dve, 1, body)

            for ap, v in ((ones_bf[:], 1.0), (ones_row[:], 1.0), (v_aug[:], 1.0), (negmax[:], 0.0),
                          (keyrow_bf[:], 0.0)):
                dve.memset(ap, v).then_inc(setup_done, 1)
            dve.memset(o_bank[:], 0.0).then_inc(setup_done, 1)
            dve.memset(ones_e[:], 1.0).then_inc(setup_done, 1)
            dve.wait_ge(const_in, 16 * N_CONST)
            dve.tensor_copy(masks[:].rearrange("p m c -> p (m c)"), masks_f32).then_inc(setup_done, 1)
            dve.tensor_copy(ident_bf[:], ident[:]).then_inc(setup_done, 1)
            dve.tensor_copy(lower_bf[:], lower[:]).then_inc(setup_done, 1)
            start(dve)
            for n, st in enumerate(STAGES[:stop]):
                attention(n, st)
                if n == 2 and stop > 2:
                    route(0)
                    experts(0)
                    mix(0)
            if stop > 5:
                route(1)
                experts(1)
                mix(1)

        @block.gpsimd
        def _(pool):
            head_of_row = row_head[:].unsqueeze(2).to_broadcast([128, HALF, S])

            def rsqrt(g, p, ready, first_done, done, used):
                apart(pool, (ready, g + 1),
                      (done, g - 1))
                pool.tensor_scalar(vareps[:, p:p + 1], meanvar[:, p, 1:2], EPS, None, ALU.add) \
                    .then_inc(first_done, 1)
                apart(pool, (first_done, g + 1),
                      (used, g - 1))
                pool.tensor_tensor(rstd[:, p:p + 1], vareps[:, p:p + 1], neghalf[:], ALU.pow) \
                    .then_inc(done, 1)

            def attention(n, st):
                def body(t, par):
                    e, pe_ = item(t, par, 0)
                    a, pa = item(t, par, 1)
                    if e is not None:
                        rsqrt(B * n + e, pe_, aggr_done, vareps_done, rstd_done, xn_done)
                    if a is not None:
                        g = B * n + a
                        if st["rope"]:
                            pool.wait_ge(rawk_done, a + 1)
                            after(pool, k_done, g - 1)
                            pool.tensor_tensor(prod[:, pa, 2:4, :], raw[:, pa, 2:4, :], rope[:], ALU.mult) \
                                .then_inc(kprod_done, 1)
                            pool.wait_ge(kprod_done, a + 1)
                            after(pool, score_ps, 4 * g - 4)
                            after(pool, k_masked_done, g - 1)
                            pool.tensor_tensor(kT[:, pa, :], prod[:, pa, 2, :], prod[:, pa, 3, :], ALU.add) \
                                .then_inc(k_done, 1)
                        after(pool, k_done, g + 1)
                        after(pool, rowmax_ps, 4 * g - 4)
                        pool.tensor_tensor(k_masked[:, pa], kT[:, pa, :].unsqueeze(1).to_broadcast([128, HALF, S]),
                                           head_of_row, ALU.mult).then_inc(k_masked_done, 1)
                    if e is not None and st["inner"]:
                        apart(pool, (xn_done, B * n + e + 1))
                        pool.tensor_copy(h_all[:, e, :], xn[:, pe_, :]).then_inc(hidden_kept, 1)
                steps(pool, 3, body)

            def route(l):
                def body(t, par):
                    e, p = item(t, par, 0)
                    if e is not None:
                        rsqrt(B * l + e, p, r_aggr_done, r_vareps_done, r_rstd_done, r_xs_done)
                        apart(pool, (r_xs_done, B * l + e + 1))
                        pool.tensor_copy(h_all[:, e, :], xn[:, p, :]).then_inc(r_kept, 1)
                    b, q = item(t, par, 2)
                    if b is not None:
                        apart(pool, (r_topi_done, B * l + b + 1))
                        pool.tensor_copy(logits[:, b, :], lg[:, q, :]).then_inc(r_copied, 1)
                        pool.tensor_copy(top_all[:, b, :], top[:, q, 0:2]).then_inc(r_copied, 1)
                        pool.tensor_copy(choice[:, b, :], topi[:, q, 0:2]).then_inc(r_copied, 1)
                steps(pool, 2, body, first=4)

                def scatter(t, par):
                    apart(pool, (index_done, 2 * B * l + t + 1),
                          (moved_done, B * l + t + 1))
                    for k in range(2):
                        pool.indirect_dma_start(
                            out=xin[l], out_offset=bass.IndirectOffsetOnAxis(ap=index[:, par, k:k + 1].bitcast(U32), axis=0),
                            in_=moved[:, par, 0, :], in_offset=None).then_inc(scattered[par], 16)
                pool.wait_ge(zero_in, 16 * N_ZERO)
                steps(pool, 0, scatter)

            def gather(l):
                def body(t, par):
                    apart(pool, (index_done, 2 * B * l + B + t + 1),
                          (mix_done, B * l if isinstance(t, int) and t < 2 else B * l + t - 1))
                    for k in range(2):
                        pool.indirect_dma_start(
                            out=moved[:, par, k, :], out_offset=None, in_=eout[l],
                            in_offset=bass.IndirectOffsetOnAxis(ap=index[:, par, k:k + 1].bitcast(U32), axis=0)) \
                            .then_inc(gathered[par], 16)
                tiles = sum(m["tiles"] for m in MOE[:l + 1])
                pool.wait_ge(stored[0], 16 * ((tiles + 1) // 2))
                pool.wait_ge(stored[1], 16 * (tiles // 2))
                for t in range(2):
                    body(t, t)
                with pool.Fori(1, B // 2) as i:
                    for u in range(2):
                        body(i * 2 + u, u)

            pool.memset(neghalf[:], -0.5).then_inc(setup_done, 1)
            pool.memset(hidden[:], 0.0).then_inc(setup_done, 1)
            start(pool)
            for n, st in enumerate(STAGES[:stop]):
                attention(n, st)
                if n == 2 and stop > 2:
                    route(0)
                    gather(0)
            if stop > 5:
                route(1)
                gather(1)


def constants():
    q, k = np.arange(S)[:, None], np.arange(S)[None, :]
    window = np.where((k <= q) & (q - k < WINDOW), 0.0, -BIG)
    causal = np.where(k <= q, 0.0, -BIG)
    masks = np.stack([np.tile(m, (1, PER)) for m in (window, window.T, causal, causal.T)], 1)
    p = np.arange(128)
    row_head = (p[:, None] % 64) // HD == np.arange(HALF)
    max_head = p[:, None] % 32 == np.arange(PER)
    inv_freq = 1.0 / np.float32(10000.0) ** (np.arange(0, HD, 2, dtype=np.float32) / np.float32(HD))
    theta = np.arange(S, dtype=np.float32)[:, None] * inv_freq[None, :].astype(np.float32)
    cos, sin = (np.tile(np.repeat(f(theta), 2, axis=1), (1, H)).T for f in (np.cos, np.sin))
    sign = np.where(p % 2 == 0, -1.0, 1.0)[:, None]
    iotas = np.concatenate([np.tile(np.arange(16), (128, 1)), np.tile(np.arange(48), (128, 1)),
                            np.arange(B)[None, :] * S + p[:, None]], 1)
    restart = np.tile((np.arange(512) % B != 0), (128, 1))
    f32 = lambda a: np.ascontiguousarray(a, np.float32)
    return dict(ident=f32(np.eye(128)), masks=f32(masks),
                row_head=f32(row_head), max_head=f32(max_head), rope=f32(np.stack([cos, sin * sign], 1)), iotas=f32(iotas),
                restart=f32(restart), lower=f32(p[:, None] <= p[None, :]))


def layout(inputs):
    a = {k: np.asarray(v) for k, v in inputs.items()}
    qkv = a["L0_attn_w_qkv"]
    w = [qkv[0:128].T, qkv[128:256].T, qkv[256:384].T, a["L0_attn_w_out"].T]
    w += [a["L0_xattn_W" + k] for k in "qkvo"] + [a[f"L0_ffn_{k}_w"] for k in "qkvo"]
    w += [a["L1_attn_W" + k] for k in "qkvo"] + [a["L1_xattn_W" + k] for k in "qkvo"]
    swap = np.arange(128) ^ 1
    w += [a["L1_attn_Wq"][:, swap], a["L1_attn_Wk"][:, swap]]
    zero, one = np.zeros(128, np.float32), np.ones(128, np.float32)
    bias = lambda k: [zero, a["L0_xattn_b" + k], a[f"L0_ffn_{k}_b"], zero, a["L1_xattn_b" + k]]
    cols = bias("q") + bias("k") + bias("v") + [a["L0_ffn_ln1_w"], a["L0_ffn_ln1_b"], a["L0_ffn_ln2_w"],
                                                a["L0_ffn_ln2_b"], one, zero]
    rows = [a["L0_attn_b_out"], a["L0_xattn_bo"], a["L0_ffn_o_b"], zero, a["L1_xattn_bo"]]
    router = np.zeros((128, 2, 16), np.float32)
    router[:, 0, :] = a["L0_ffn_router_w"]
    router[:, 1, 0:8] = a["L1_ffn_Wg"].T

    def pack(w1, b1, w2, b2):
        E = w1.shape[0]
        return np.concatenate([
            w1, w2.reshape(E, FCH, 128, D).transpose(0, 2, 1, 3).reshape(E, 128, FCH * D),
            b1.reshape(E, FCH, 128).transpose(0, 2, 1), np.broadcast_to(b2[:, None, :], (E, 128, D))], axis=2)
    return dict(
        x=a["x"], ctx=a["ctx_1024"].reshape(T, D).T, keymask=a["mask_BxS2_ff1"].reshape(1, T),
        weights=np.stack(w, 1), cols=np.stack(cols, 1), rows=np.stack(rows)[None], router=router,
        pack0=pack(a["L0_ffn_fc1_w"], a["L0_ffn_fc1_b"], a["L0_ffn_fc2_w"], a["L0_ffn_fc2_b"]),
        pack1=pack(a["L1_ffn_W1"].transpose(0, 2, 1), a["L1_ffn_b1"], a["L1_ffn_W2"].transpose(0, 2, 1),
                   a["L1_ffn_b2"]))


def kernel(**inputs):
    import concourse.bacc as bacc
    from concourse.bass_utils import run_bass_kernel_spmd

    nc = bacc.Bacc("TRN2", target_bir_lowering=False, num_devices=1)
    arrays, args = {}, []
    for name, a in {**layout(inputs), **constants()}.items():
        a = np.ascontiguousarray(a)
        arrays[f"in_{name}"] = a
        args.append(nc.dram_tensor(f"in_{name}", a.shape, mybir.dt.from_np(a.dtype), kind="ExternalInput").ap())
    args.append(nc.dram_tensor("out_0", (B, S, D), F32, kind="ExternalOutput").ap())
    build(nc, *args)
    r = run_bass_kernel_spmd(nc, [arrays], core_ids=[0])
    return r.results[0]["out_0"]
```

```python
from contextlib import ExitStack

import numpy as np

import concourse.bass as bass
from concourse import mybir

F32 = mybir.dt.float32
BF16 = mybir.dt.bfloat16
I32 = mybir.dt.int32
U32 = mybir.dt.uint32
ALU = mybir.AluOpType
ACT = mybir.ActivationFunctionType
X_AXIS = mybir.AxisListType.X

B, S, D, H, HD = 32, 128, 128, 16, 8
T = B * S
GROUPS, PER = 4, 4
HALF = 8
SCALE = HD ** -0.5
EPS = 1e-5
BIG = 1e30
WINDOW = 64
F = 512
WARM_UP = 24
MIX, NORM, PROJECT, ROW_MAX, KEYS, FINISH, NORM2, ROUTER, PLACE = 0, 1, 2, 3, 4, 5, 6, 7, 8
HEAD = PLACE
LEAD = [8, 6, 10, 6, 8]
FCH = F // 128

STAGES = [
    dict(name="L0_attn", cross=False, mask="window", rope=False, bo=True, inner=False),
    dict(name="L0_xattn", cross=True, mask=None, rope=False, bo=True, inner=False),
    dict(name="L0_ffn", cross=False, mask="causal", rope=False, bo=True, inner=True),
    dict(name="L1_attn", cross=False, mask="causal", rope=True, bo=False, inner=False),
    dict(name="L1_xattn", cross=True, mask="keys", rope=False, bo=True, inner=False),
]
COL_BQ, COL_BK, COL_BV = 0, 5, 10
COL_LN1W, COL_LN1B, COL_LN2W, COL_LN2B, COL_ONE, COL_ZERO = 15, 16, 17, 18, 19, 20
NCOL = 21
W_SWQ, W_SWK, NW = 20, 21, 22

MOE = [dict(E=16, R=512, tiles=16, cap=2 * T // 16, factor=0.8),
       dict(E=8, R=256, tiles=(2 * T + 8 * 255) // 256, cap=None, factor=1.0)]
REGION = [T + MOE[0]["cap"], T]
ROWS_IN = [MOE[0]["E"] * REGION[0], MOE[1]["E"] * REGION[1] + MOE[1]["R"]]
ROWS_OUT = [MOE[0]["E"] * MOE[0]["cap"], MOE[1]["tiles"] * MOE[1]["R"]]
TILED, DIFFS, ROUTED = (2, 49), (4, 50), (29, 63)
N_ZERO = 2 * 2 + 9
N_KEPT = 28
LOGITS, TOP, CHOICE, PLACES = slice(0, 16), slice(16, 24), slice(24, 26), slice(26, 28)
PACK = F + F + FCH + 128


def build(nc, x_in, ctx_in, keymask_in, weights_in, cols_in, rows_in, router_in, pack0_in, pack1_in,
          ident_in, masks_in, row_head_in, max_head_in, rope_in, iotas_in, carry_in, lower_in, out, stop=99):
    xin = [nc.dram_tensor(f"expert_in{l}", (ROWS_IN[l], D), F32).ap() for l in range(2)]
    eout = [nc.dram_tensor(f"expert_out{l}", (ROWS_OUT[l], D), F32).ap() for l in range(2)]
    packs = [pack0_in, pack1_in]

    with ExitStack() as ctx:
        def sb(name, shape, dt=F32):
            return ctx.enter_context(nc.sbuf_tensor(name, shape, dt))

        def sem(name):
            return ctx.enter_context(nc.semaphore(name))

        x_all = sb("x_all", [128, B, D])
        h_all = sb("h_all", [128, B, D])
        weights = sb("weights", [128, NW, 128])
        cols = sb("cols", [128, NCOL])
        rows = sb("rows", [1, 5, 128])
        router = sb("router", [128, 2, 16])
        ident = sb("ident", [128, 128])
        ident_bf = sb("ident_bf", [128, 128], BF16)
        masks = sb("masks", [128, 4, 512], BF16)
        ones_bf = sb("ones_bf", [128, 512], BF16)
        ones_row = sb("ones_row", [1, 128])
        row_head = sb("row_head", [128, HALF])
        max_head = sb("max_head", [128, PER])
        rope = sb("rope", [128, 2, 128])
        iotas = sb("iotas", [128, 68])
        lower = sb("lower", [128, 128])
        lower_bf = sb("lower_bf", [128, 128], BF16)
        stats = sb("stats", [128, 2, 6])
        meanvar = sb("meanvar", [128, 2, 2])
        vareps = sb("vareps", [128, 2])
        rstd = sb("rstd", [128, 2])
        neghalf = sb("neghalf", [128, 1])
        ones_e = sb("ones_e", [128, 16])
        xn = sb("xn", [128, 2, D])
        xT = sb("xT", [128, 2, S])
        ctxT = sb("ctxT", [128, 2, S])
        raw = sb("raw", [128, 2, 4, S])
        prod = sb("prod", [128, 2, 4, S])
        qT = sb("qT", [128, 2, S])
        q_bf = sb("q_bf", [128, 2, S], BF16)
        kT = sb("kT", [128, 2, S])
        v_aug = sb("v_aug", [128, 2, H, HD + 1])
        q_masked = sb("q_masked", [128, 2, HALF, S])
        k_masked = sb("k_masked", [128, 2, HALF, S], BF16)
        keyrow = sb("keyrow", [1, 2, S])
        keyrow_bf = sb("keyrow_bf", [128, 2, S], BF16)
        negmax = sb("negmax", [128, 2, GROUPS, 32])
        shift = sb("shift", [128, 2, PER, S], BF16)
        probs = sb("probs", [128, 2, H, S])
        masks_f32 = probs[:, 0].rearrange("p h s -> p (h s)")
        o_sb = sb("o_sb", [128, 2, 4, S])
        rden = sb("rden", [128, 2, H])
        att = sb("att", [128, 2, D])
        attT = sb("attT", [128, 2, S])
        bank = [ctx.enter_context(nc.psum_tensor(f"bank{i}", [128, 512], F32)) for i in range(8)]
        rowmax_bank, score_bank, o_bank, ot_bank, kv_bank, misc_bank = (
            bank[0:2], bank[2:4], bank[4], bank[5], bank[6], bank[7])
        XT_COLS, Q_COLS, QSW_COLS = (slice(128 * i, 128 * i + 128) for i in range(3))
        K_COLS, V_COLS, KSW_COLS = (slice(128 * i, 128 * i + 128) for i in range(3))
        ATT_COLS, RX_COLS = slice(0, 128), slice(256, 384)
        NEGMAX_COLS, LOGIT_COLS, COUNT_COLS, TOTAL_COLS = (slice(128, 256), slice(384, 400), slice(400, 432),
                                                           slice(432, 464))
        r_stats = sb("r_stats", [128, 2, 6])
        r_meanvar = sb("r_meanvar", [128, 2, 2])
        r_vareps = sb("r_vareps", [128, 2])
        r_rstd = sb("r_rstd", [128, 2])
        r_x = sb("r_x", [128, 2, D])
        r_xT = sb("r_xT", [128, 2, S])
        r_row = sb("r_row", [128, 2, N_KEPT])
        topi = sb("topi", [128, 2, 8], U32)
        onehot = sb("onehot", [128, 2, 2, 16], BF16)
        carry = sb("carry", [128, 2, 2, 2, 16])
        place = sb("place", [128, 2, 2, 16])
        placed = sb("placed", [128, 2, 2, 16])
        dest = sb("dest", [128, 2, 2], I32)
        sent = sb("sent", [128, 2, D])
        kept = sb("kept", [128, B, N_KEPT])
        wide = sb("wide", [128, 2, B, 16])
        small = sb("small", [128, 16, B])
        per_e = sb("per_e", [128, 8, 16])
        per_ei = sb("per_ei", [128, 2, 16], I32)
        tile_cmp = sb("tile_cmp", [128, 2, 48, 16])
        tile_f = sb("tile_f", [128, 4, 48])
        tile_expert = sb("tile_expert", [128, 48], I32)
        tile_row = sb("tile_row", [128, 48], I32)
        second = sb("second", [128, 4, 16])
        source = sb("source", [128, 2, B], I32)
        weight = sb("weight", [128, 2, B])
        index = sb("index", [128, 2, 2], I32)
        moved = sb("moved", [128, 2, 2, D])
        pack = sb("pack", [128, 2, PACK])
        tile_rows = sb("tile_rows", [128, 2, 4, D])
        tile_rows2 = sb("tile_rows2", [128, 2, 4, D])
        rowsT = sb("rowsT", [128, 2, 512])
        hidden = sb("hidden", [128, 2, FCH, 512])
        rows_out = sb("rows_out", [128, 2, 4, D])

        const_in, setup_done, zero_in = sem("const_in"), sem("setup_done"), sem("zero_in")
        x_in_sem = [sem(f"x_in{c}") for c in range(4)]
        ctx_in_sem = [sem(f"ctx_in{p}") for p in range(2)]
        key_in_sem = [sem(f"key_in{p}") for p in range(2)]
        pack_in_sem = [sem(f"pack_in{p}") for p in range(2)]
        tile_in_sem = [sem(f"tile_in{p}") for p in range(2)]
        stored = [sem(f"stored{p}") for p in range(2)]
        scattered = [sem(f"scattered{p}") for p in range(2)]
        gathered = [sem(f"gathered{p}") for p in range(2)]
        (stats_done, aggr_done, vareps_done, rstd_done, xn_done, xT_ps, xT_done, q_ps, kv_ps, q_bf_done,
         q_masked_done, k_done, v_done, k_masked_done, rowmax_ps, max_done, negmaxT_ps, shift_done,
         score_ps, exp_done, pv_ps, o_done, oT_ps, rden_done, att_done, attT_ps, attT_done, y_ps,
         hidden_kept, h2_done, resid_done, keyrow_done, rawk_done, rawq_done, qprod_done, qT_done,
         kprod_done, r_stats_done, r_aggr_done, r_vareps_done, r_rstd_done, r_x_done, r_h_kept, r_xT_ps,
         r_xT_done, r_logit_ps, r_logit_done, r_top_done, r_topi_done, r_choice_done, r_onehot_done,
         r_count_ps, r_place_done, r_carry_done, r_placed_done, r_sum_done, r_dest_done, r_kept, sent_done,
         routed_dve, routed_act, index_done, mix_half, mix_done, tile_done, rowsT_ps, rowsT_done,
         fc1_ps, gelu_done, fc2_ps, rows_out_done, written) = (sem(n) for n in (
            "stats_done aggr_done vareps_done rstd_done xn_done xT_ps xT_done q_ps kv_ps q_bf_done "
            "q_masked_done k_done v_done k_masked_done rowmax_ps max_done negmaxT_ps shift_done "
            "score_ps exp_done pv_ps o_done oT_ps rden_done att_done attT_ps attT_done y_ps "
            "hidden_kept h2_done resid_done keyrow_done rawk_done rawq_done qprod_done qT_done "
            "kprod_done r_stats_done r_aggr_done r_vareps_done r_rstd_done r_x_done r_h_kept r_xT_ps "
            "r_xT_done r_logit_ps r_logit_done r_top_done r_topi_done r_choice_done r_onehot_done "
            "r_count_ps r_place_done r_carry_done r_placed_done r_sum_done r_dest_done r_kept sent_done "
            "routed_dve routed_act index_done mix_half mix_done tile_done rowsT_ps rowsT_done "
            "fc1_ps gelu_done fc2_ps rows_out_done written").split())

        carried = {e: sem(f"carried_{n}") for e, n in ((nc.tensor.engine, "pe"), (nc.vector.engine, "dve"),
                                                     (nc.gpsimd.engine, "pool"))}

        def steps(eng, lag, body, total=B, first=2):
            lead = max(first, lag + lag % 2)
            turns = (total - lead) // 2
            for t in range(lead):
                body(t, t % 2)
            with eng.Fori(0, turns) as i:
                for u in range(2):
                    body(i * 2 + (lead + u), u)
            for t in range(lead + 2 * turns, total + lag):
                body(t, t % 2)

        def item(t, par, lag, total=B):
            b = t - lag
            if isinstance(b, int) and not 0 <= b < total:
                return None, None
            return b, (par + lag) % 2

        def sequences(eng, segment, body):
            for n in segment:
                lead = LEAD[n]
                for t in range(lead):
                    body(n, t, t % 2)
                with eng.Fori(0, (B - lead) // 2) as i:
                    for u in range(2):
                        body(n, i * 2 + (lead + u), u)
            for t in range(B, B + HEAD):
                body(segment[-1], t, t % 2)

        def sequence(segment, n, t, par, lag):
            b = t - lag
            if isinstance(b, int) and b < 0:
                n, b = n - 1, b + B
            if isinstance(b, int) and (n not in segment or b >= B):
                return n, None, None, None
            return n, b, B * n + b, (par + lag) % 2

        def router_item(segment, n, t, par, lag):
            m, b, g, p = sequence(segment, n, t, par, lag)
            if b is None or m not in layer_of:
                return m, None, None, None
            return m, b, B * layer_of[m] + b, p

        def after(eng, semaphore, count):
            if not (isinstance(count, int) and count <= 0):
                eng.wait_ge(semaphore, count)

        def apart(eng, *waits):
            for semaphore, count in waits:
                after(eng, semaphore, count)
            eng.sem_inc(carried[eng.engine])

        def start(eng):
            eng.wait_ge(const_in, 16 * N_CONST)
            eng.wait_ge(setup_done, SETUP)

        N_CONST, SETUP = 12, 12
        layer_of = {2: 0, 4: 1}
        SEGMENTS = [x for x in ([n for n in seg if n < stop] for seg in ((0, 1, 2), (3, 4))) if x]
        block = ctx.enter_context(nc.Block())

        @block.sync
        def _(sp):
            def load_x(c):
                sp.dma_start(x_all[:, 8 * c:8 * c + 8, :],
                             x_in[8 * c:8 * c + 8].rearrange("b t d -> t b d")).then_inc(x_in_sem[c], 16)

            load_x(0)
            for dst, src in ((ident, ident_in), (weights, weights_in), (cols, cols_in), (rows, rows_in),
                             (row_head, row_head_in), (max_head, max_head_in), (rope, rope_in),
                             (router, router_in), (iotas, iotas_in),
                             (lower, lower_in)):
                sp.dma_start(dst[:], src).then_inc(const_in, 16)
            sp.dma_start(carry[:, :, 0], carry_in).then_inc(const_in, 16)
            sp.dma_start(masks_f32, masks_in.rearrange("p m c -> p (m c)")).then_inc(const_in, 16)
            for c in range(1, 4):
                load_x(c)
            sp.wait_ge(setup_done, SETUP)
            zeros = hidden[:].rearrange("p a b c -> p (a b c)")
            tiles = xin[0].rearrange("(e h p r) d -> h p e (r d)", h=REGION[0] // MOE[0]["cap"], p=128, r=4)
            for h in (0, REGION[0] // MOE[0]["cap"] - 1):
                for e in (0, 8):
                    sp.dma_start(tiles[h, :, e:e + 8], zeros.rearrange("p (e w) -> p e w", e=8)) \
                        .then_inc(zero_in, 16)
            tiles = xin[1].rearrange("(p r) d -> p (r d)", p=128)
            for lo in range(0, tiles.shape[1], 4096):
                w = min(4096, tiles.shape[1] - lo)
                sp.dma_start(tiles[:, lo:lo + w], zeros[:, 0:w]).then_inc(zero_in, 16)

            def attention(n, st):
                cross = sum(x["cross"] for x in STAGES[:n])

                def body(t, par):
                    b, p = item(t, par, 0)
                    after(sp, kv_ps, B * n + b - 1)
                    sp.dma_start(ctxT[:, p, :], ctx_in[:, bass.ts(b, S)]).then_inc(ctx_in_sem[p], 16)
                    if st["mask"] == "keys":
                        after(sp, keyrow_done, b - 1)
                        sp.dma_start(keyrow[:, p, :], keymask_in[:, bass.ts(b, S)]).then_inc(key_in_sem[p], 16)
                if st["cross"]:
                    steps(sp, 0, body)

            def experts(l):
                m = MOE[l]
                R, blocks, base = m["R"], m["R"] // 128, sum(x["tiles"] for x in MOE[:l])
                for p in range(2):
                    sp.wait_ge(scattered[p], 16 * 2 * 16 * (l + 1))
                sp.wait_ge(zero_in, 16 * N_ZERO)
                if l == 1:
                    sp.wait_ge(routed_dve, TILED[1])

                def rows_at(a, table, most):
                    return sp.value_load(table[0:1, bass.ds(a, 1)], min_val=0, max_val=most)

                def load(a, g, p):
                    if l == 0:
                        after(sp, rowsT_ps, g - 1)
                        after(sp, tile_done, g - 1)
                        regions = xin[0].rearrange("(e h r p) d -> e h p r d", h=REGION[0] // R, p=128, r=blocks)
                        for rows_, h in ((tile_rows, 0), (tile_rows2, REGION[0] // R - 1)):
                            sp.dma_start(rows_[:, p, 0:blocks, :],
                                         regions[bass.ds(a, 1), h].rearrange("e p r d -> (e p) r d")) \
                                .then_inc(tile_in_sem[p], 16)
                    else:
                        row = rows_at(a, tile_row, m["E"] * REGION[1])
                        after(sp, rowsT_ps, g - 1)
                        sp.dma_start(tile_rows[:, p, 0:blocks, :],
                                     xin[1][bass.ds(row, R), :].rearrange("(r p) d -> p r d", p=128)) \
                            .then_inc(tile_in_sem[p], 16)
                    expert = a if l == 0 else rows_at(a, tile_expert, m["E"] - 1)
                    after(sp, fc2_ps, g - 1)
                    after(sp, rows_out_done, g - 1)
                    sp.dma_start(pack[:, p, :], packs[l][bass.ds(expert, 1)].rearrange("e p c -> (e p) c")) \
                        .then_inc(pack_in_sem[p], 16)

                def body(t, par):
                    a, p = item(t, par, 0, m["tiles"])
                    if a is not None:
                        load(a, base + a, p)
                    a, p = item(t, par, 2, m["tiles"])
                    if a is not None:
                        after(sp, rows_out_done, base + a + 1)
                        sp.dma_start(eout[l][bass.ts(a, R), :].rearrange("(r p) d -> p r d", p=128),
                                     rows_out[:, p, 0:blocks, :]).then_inc(stored[p], 16)
                steps(sp, 2, body, m["tiles"], 4)

            for n, st in enumerate(STAGES[:stop]):
                attention(n, st)
                if n == 2 and stop > 2:
                    experts(0)
            if stop > 5:
                experts(1)

                def body(t, par):
                    sp.wait_ge(mix_done, B + t + 1)
                    sp.dma_start(out[bass.ds(t, 1)].rearrange("b t d -> t (b d)"), x_all[:, t, :]) \
                        .then_inc(written, 16)
                steps(sp, 0, body)
                sp.wait_ge(written, 16 * B)
            else:
                sp.wait_ge(resid_done, B * min(stop, 5))
                if stop > 2:
                    sp.wait_ge(mix_done, B)
                sp.dma_start(out.rearrange("b t d -> t b d"), x_all[:]).then_inc(written, 16)
                sp.wait_ge(written, 16)

        @block.tensor
        def _(pe):
            def mm(dst, lhsT, rhs, first=True, last=True):
                return pe.matmul(dst, lhsT, rhs, start=first, stop=last)

            def warm_up(n):
                if n:
                    pe.wait_ge(mix_done, 1)
                for _ in range(WARM_UP):
                    mm(kv_bank[:], ident_bf[:], ones_bf[:])

            half = lambda gr: slice(64 * (gr // 2), 64 * (gr // 2) + 64)
            heads_of = lambda gr: slice(PER * (gr % 2), PER * (gr % 2) + PER)
            mask_of = lambda st: {"window": (0, 1), "causal": (2, 3)}.get(st["mask"], (None, None))

            def row_scores(n, b, g, p, gr):
                st, dst, part, heads = STAGES[n], rowmax_bank[gr % 2], half(gr), heads_of(gr)
                apart(pe, *([(k_masked_done, g + 1), (q_bf_done, g + 1)] if gr == 0 else []),
                      *([(keyrow_done, b + 1)] if gr == 0 and st["mask"] == "keys" else []),
                      (max_done, 4 * g + gr - 1))
                ins = mm(dst[:], q_bf[part, p, :], k_masked[part, p, heads, :], last=st["mask"] is None)
                if st["mask"] in ("window", "causal"):
                    ins = mm(dst[:], ident_bf[:], masks[:, mask_of(st)[0], :], first=False)
                elif st["mask"] == "keys":
                    ins = mm(dst[:], ones_bf[:, 0:128],
                             keyrow_bf[:, p, :].unsqueeze(1).to_broadcast([128, PER, S]), first=False)
                ins.then_inc(rowmax_ps, 1)

            def key_scores(n, g, p, gr):
                st, dst, rows_ = STAGES[n], score_bank[gr % 2], slice(32 * gr, 32 * gr + 32)
                if gr == 0:
                    after(pe, k_done, g + 1)
                    after(pe, q_masked_done, g + 1)
                    after(pe, shift_done, g + 1)
                after(pe, exp_done, 4 * g + gr - 1)
                mm(dst[:], kT[half(gr), p, :], q_masked[half(gr), p, heads_of(gr), :], last=False)
                if st["mask"] in ("window", "causal"):
                    mm(dst[:], ident_bf[:], masks[:, mask_of(st)[1], :], first=False, last=False)
                elif st["mask"] == "keys":
                    mm(dst[:], keyrow_bf[:, p, :], ones_bf[:], first=False, last=False)
                mm(dst[:], ones_bf[rows_, 0:128], shift[rows_, p], first=False).then_inc(score_ps, 1)

            def attention(segment):
                def body(n_, t, par):
                    an, a, ag, ap = sequence(segment, n_, t, par, PROJECT)
                    cn, c, cg, cp = sequence(segment, n_, t, par, ROW_MAX)
                    kn, k, kg, kp = sequence(segment, n_, t, par, KEYS)
                    fn, f, fg, fp = sequence(segment, n_, t, par, FINISH)
                    un, u, ug, up = router_item(segment, n_, t, par, ROUTER)
                    wn, w, wg, wp = router_item(segment, n_, t, par, PLACE)
                    if k is not None:
                        key_scores(kn, kg, kp, 0)
                    if f is not None:
                        after(pe, o_done, fg + 1)
                        after(pe, attT_done, fg)
                        after(pe, shift_done, fg + 1 + (k is not None))
                        if w is not None:
                            after(pe, r_logit_done, wg + 1)
                            after(pe, r_carry_done, wg)
                        for j in range(4):
                            ins = pe.transpose(ot_bank[:, 128 * j:128 * j + 128], o_sb[:, fp, j, :], ident[:])
                        ins.then_inc(oT_ps, 1)
                    if c is not None:
                        row_scores(cn, c, cg, cp, 0)
                    if k is not None:
                        key_scores(kn, kg, kp, 1)
                    if c is not None:
                        row_scores(cn, c, cg, cp, 1)
                    if u is not None:
                        after(pe, r_x_done, ug + 1)
                        after(pe, att_done, fg + 1 if f is not None else B * (un + 1))
                        if w is not None:
                            after(pe, r_logit_done, wg + 1)
                            after(pe, r_carry_done, wg)
                        pe.transpose(ot_bank[:, RX_COLS], r_x[:, up, :], ident[:]).then_inc(r_xT_ps, 1)
                    if f is not None:
                        after(pe, att_done, fg + 1)
                        pe.transpose(ot_bank[:, ATT_COLS], att[:, fp, :], ident[:]).then_inc(attT_ps, 1)
                    if k is not None:
                        key_scores(kn, kg, kp, 2)
                    if a is not None:
                        after(pe, xn_done, ag + 1)
                        after(pe, q_bf_done, ag)
                        after(pe, q_masked_done, ag)
                        pe.transpose(misc_bank[:, XT_COLS], xn[:, ap, :], ident[:]).then_inc(xT_ps, 1)
                    if c is not None:
                        row_scores(cn, c, cg, cp, 2)
                        row_scores(cn, c, cg, cp, 3)
                    if f is not None:
                        bias = STAGES[fn]["bo"]
                        after(pe, attT_done, fg + 1)
                        ins = mm(o_bank[:, 0:D], attT[:, fp, :], weights[:, 4 * fn + 3, :], last=not bias)
                        if bias:
                            ins = mm(o_bank[:, 0:D], ones_row[:], rows[:, fn, :], first=False)
                        ins.then_inc(y_ps, 1)
                    if k is not None:
                        key_scores(kn, kg, kp, 3)
                    if u is not None:
                        after(pe, r_xT_done, ug + 1)
                        if f is not None:
                            after(pe, attT_done, fg + 1)
                        mm(ot_bank[:, LOGIT_COLS], r_xT[:, up, :], router[:, layer_of[un], :]).then_inc(r_logit_ps, 1)
                    if w is not None:
                        after(pe, r_onehot_done, 2 * wg + 2)
                        after(pe, r_carry_done, wg)
                        after(pe, r_logit_done, wg + 1)
                        both, counts, totals = onehot[:, wp].rearrange("p k e -> p (k e)"), COUNT_COLS, TOTAL_COLS
                        if wn == 2:
                            mm(ot_bank[:, counts], lower_bf[:], both)
                            ins = mm(ot_bank[:, totals], ones_bf[:, 0:128], both)
                        else:
                            for k_ in range(2):
                                at = counts.start + 16 * k_
                                mm(ot_bank[:, at:at + 16], lower_bf[:], onehot[:, wp, k_, :], last=not k_)
                                if k_:
                                    mm(ot_bank[:, at:at + 16], ones_bf[:, 0:128], onehot[:, wp, 0, :], first=False)
                            for k_ in range(2):
                                at = totals.start + 16 * k_
                                mm(ot_bank[:, at:at + 16], ones_bf[:, 0:128], onehot[:, wp, 0, :], last=False)
                                ins = mm(ot_bank[:, at:at + 16], ones_bf[:, 0:128], onehot[:, wp, 1, :], first=False)
                        ins.then_inc(r_count_ps, 1)
                    if c is not None:
                        after(pe, max_done, 4 * cg + 4)
                        after(pe, attT_done, cg - 1)
                        if u is not None:
                            after(pe, r_xT_done, ug + 1)
                        pe.transpose(ot_bank[:, NEGMAX_COLS], negmax[:, cp].rearrange("p g j -> p (g j)"),
                                     ident[:]).then_inc(negmaxT_ps, 1)
                    if a is not None:
                        st, wts = STAGES[an], (lambda i: weights[:, 4 * an + i, :])
                        cross = sum(x["cross"] for x in STAGES[:an])
                        src = ctxT if st["cross"] else xT
                        if st["cross"]:
                            pe.wait_ge(ctx_in_sem[ap], (a // 2 + (16 * cross + 1)) * 16)
                        after(pe, xT_done, ag + 1)
                        after(pe, k_done, ag)
                        after(pe, v_done, ag)
                        mm(kv_bank[:, K_COLS], wts(1), src[:, ap, :])
                        if st["rope"]:
                            mm(kv_bank[:, KSW_COLS], weights[:, W_SWK, :], src[:, ap, :])
                        mm(kv_bank[:, V_COLS], src[:, ap, :], wts(2)).then_inc(kv_ps, 1)
                        ins = mm(misc_bank[:, Q_COLS], wts(0), xT[:, ap, :])
                        if st["rope"]:
                            ins = mm(misc_bank[:, QSW_COLS], weights[:, W_SWQ, :], xT[:, ap, :])
                        ins.then_inc(q_ps, 1)
                    if k is not None:
                        after(pe, exp_done, 4 * kg + 4)
                        after(pe, v_done, kg + 1)
                        after(pe, resid_done, kg)
                        for h in range(H):
                            ins = mm(o_bank[32 * (h % 4):32 * (h % 4) + HD + 1, 128 * (h // 4):128 * (h // 4) + 128],
                                     v_aug[:, kp, h, :], probs[:, kp, h, :])
                        ins.then_inc(pv_ps, 1)
                warm_up(segment[0])
                sequences(pe, segment, body)

            def experts(l):
                m = MOE[l]
                R, blocks, base = m["R"], m["R"] // 128, sum(x["tiles"] for x in MOE[:l])
                pe.wait_ge(resid_done, B * (2 * l + 3))
                pe.wait_ge(max_done, 4 * B * (2 * l + 3))
                pe.wait_ge(r_carry_done, B * (l + 1))

                def body(t, par):
                    a, p = item(t, par, 1, m["tiles"])
                    if a is not None:
                        g = base + a
                        pe.wait_ge(pack_in_sem[p], (a // 2 + (base // 2 + 1)) * 16)
                        after(pe, rowsT_done, g + 1)
                        for f in range(FCH):
                            after(pe, gelu_done, 4 * g + (f - 3))
                            mm(bank[f][:, 0:R], pack[:, p, 128 * f:128 * f + 128], rowsT[:, p, 0:R]) \
                                .then_inc(fc1_ps, 1)
                    d, q = item(t, par, 0, m["tiles"])
                    if d is not None:
                        g = base + d
                        if l == 0:
                            pe.wait_ge(tile_done, d + 1)
                        else:
                            pe.wait_ge(tile_in_sem[q], (d // 2 + (base + 1)) * 16)
                        after(pe, rowsT_done, g)
                        for r in range(blocks):
                            ins = pe.transpose(ot_bank[:, 128 * r:128 * r + 128], tile_rows[:, q, r, :], ident[:])
                        ins.then_inc(rowsT_ps, 1)
                    if a is not None:
                        g = base + a
                        after(pe, gelu_done, 4 * g + 4)
                        after(pe, rows_out_done, g - 1)
                        for r in range(blocks):
                            for f in range(FCH):
                                ins = mm((o_bank, kv_bank)[p][:, 128 * r:128 * r + 128],
                                         hidden[:, p, f, 128 * r:128 * r + 128],
                                         pack[:, p, F + 128 * f:F + 128 * f + 128], f == 0, f == FCH - 1)
                        ins.then_inc(fc2_ps, 1)
                steps(pe, 2, body, m["tiles"], 4)

            start(pe)
            for l, segment in enumerate(SEGMENTS):
                attention(segment)
                if stop > (2, 5)[l]:
                    experts(l)

        @block.scalar
        def _(act):
            col = lambda i: cols[:, i:i + 1]

            def attention(segment):
                def exponential(kg, kp, gr):
                    after(act, score_ps, 4 * kg + gr + 1)
                    if gr == 0:
                        after(act, pv_ps, kg - 1)
                    act.activation(probs[:, kp, PER * gr:PER * gr + PER, :], score_bank[gr % 2][:],
                                   ACT.Exp, scale=SCALE).then_inc(exp_done, 1)

                def body(n_, t, par):
                    an, a, ag, ap = sequence(segment, n_, t, par, PROJECT)
                    kn, k, kg, kp = sequence(segment, n_, t, par, KEYS)
                    fn, f, fg, fp = sequence(segment, n_, t, par, FINISH)
                    un, u, ug, up = router_item(segment, n_, t, par, ROUTER)
                    if k is not None:
                        exponential(kg, kp, 0)
                        exponential(kg, kp, 1)
                    if f is not None:
                        after(act, attT_ps, fg + 1)
                        after(act, y_ps, fg - 1)
                        act.activation(attT[:, fp, :], ot_bank[:, ATT_COLS], ACT.Identity,
                                       bias=col(COL_BV + fn)).then_inc(attT_done, 1)
                    if u is not None:
                        after(act, r_xT_ps, ug + 1)
                        after(act, r_logit_ps, ug - 1)
                        if un == 2:
                            ins = act.activation(r_xT[:, up, :], ot_bank[:, RX_COLS], ACT.Identity,
                                                 bias=col(COL_LN2B), scale=col(COL_LN2W))
                        else:
                            ins = act.activation(r_xT[:, up, :], ot_bank[:, RX_COLS], ACT.Copy)
                        ins.then_inc(r_xT_done, 1)
                    if k is not None:
                        exponential(kg, kp, 2)
                    if a is not None:
                        after(act, xT_ps, ag + 1)
                        after(act, kv_ps, ag - 1)
                        if STAGES[an]["inner"]:
                            ins = act.activation(xT[:, ap, :], misc_bank[:, XT_COLS], ACT.Identity,
                                                 bias=col(COL_LN1B), scale=col(COL_LN1W))
                        else:
                            ins = act.activation(xT[:, ap, :], misc_bank[:, XT_COLS], ACT.Copy)
                        ins.then_inc(xT_done, 1)
                    if k is not None:
                        exponential(kg, kp, 3)
                    if a is not None:
                        rope_ = STAGES[an]["rope"]
                        after(act, kv_ps, ag + 1)
                        if rope_:
                            after(act, k_done, ag - 1)
                            act.activation(raw[:, ap, 2:4, :],
                                           kv_bank[:].rearrange("p (j s) -> p j s", s=S)[:, 0:3:2, :],
                                           ACT.Copy).then_inc(rawk_done, 1)
                            after(act, q_ps, ag + 1)
                            after(act, q_masked_done, ag - 1)
                            act.activation(raw[:, ap, 0:2, :],
                                           misc_bank[:].rearrange("p (j s) -> p j s", s=S)[:, 1:3, :],
                                           ACT.Copy).then_inc(rawq_done, 1)
                        else:
                            after(act, k_masked_done, ag - 1)
                            after(act, score_ps, 4 * ag - 4)
                            act.activation(kT[:, ap, :], kv_bank[:, K_COLS], ACT.Identity,
                                           bias=col(COL_BK + an)).then_inc(k_done, 1)
                            after(act, q_ps, ag + 1)
                            after(act, rowmax_ps, 4 * ag - 4)
                            act.activation(q_bf[:, ap, :], misc_bank[:, Q_COLS], ACT.Identity,
                                           bias=col(COL_BQ + an)).then_inc(q_bf_done, 1)
                    if k is not None:
                        after(act, pv_ps, kg + 1)
                        after(act, oT_ps, kg - 1)
                        act.activation(o_sb[:, kp].rearrange("p j q -> p (j q)"), o_bank[:], ACT.Copy) \
                            .then_inc(o_done, 1)
                    if a is not None:
                        after(act, pv_ps, ag - 1)
                        act.activation(v_aug[:, ap, :, 0:HD],
                                       kv_bank[:, V_COLS].rearrange("p (h d) -> p h d", d=HD), ACT.Copy) \
                            .then_inc(v_done, 1)
                        if rope_:
                            after(act, qT_done, a + 1)
                            after(act, rowmax_ps, 4 * ag - 4)
                            act.activation(q_bf[:, ap, :], qT[:, ap, :], ACT.Copy).then_inc(q_bf_done, 1)
                sequences(act, segment, body)

            def gates(l):
                act.wait_ge(routed_dve, DIFFS[l])
                act.activation(small[:, 2, :], small[:, 1, :], ACT.Exp).then_inc(routed_act, 1)
                if l == 0:
                    act.activation(wide[:, 1], wide[:, 0], ACT.Exp).then_inc(routed_act, 1)

            def experts(l):
                m = MOE[l]
                R, base = m["R"], sum(x["tiles"] for x in MOE[:l])

                def body(t, par):
                    if isinstance(t, int) and t == 2:
                        gates(l)
                    a, p = item(t, par, 1, m["tiles"])
                    if a is not None:
                        g = base + a
                        after(act, fc2_ps, g - 1)
                        for f in range(FCH):
                            after(act, fc1_ps, 4 * g + f + 1)
                            act.activation(hidden[:, p, f, 0:R], bank[f][:, 0:R], ACT.Gelu,
                                           bias=pack[:, p, 2 * F + f:2 * F + f + 1]).then_inc(gelu_done, 1)
                    d, q = item(t, par, 0, m["tiles"])
                    if d is not None:
                        g = base + d
                        after(act, rowsT_ps, g + 1)
                        after(act, fc1_ps, 4 * g - 4)
                        if l == 0:
                            ins = act.activation(rowsT[:, q, 0:R], ot_bank[:, 0:R], ACT.Identity,
                                                 bias=col(COL_LN2B), scale=col(COL_LN2W))
                        else:
                            ins = act.activation(rowsT[:, q, 0:R], ot_bank[:, 0:R], ACT.Copy)
                        ins.then_inc(rowsT_done, 1)
                steps(act, 2, body, m["tiles"], 4)

            start(act)
            for l, segment in enumerate(SEGMENTS):
                attention(segment)
                if stop > (2, 5)[l]:
                    experts(l)

        @block.vector
        def _(dve):
            seqs, seqs8 = [128, PER, S], [128, HALF, S]
            head_of_row = row_head[:].unsqueeze(2).to_broadcast(seqs8)
            head_of_max = max_head[:].unsqueeze(2).to_broadcast(seqs)
            routed = [0]

            def link(ins):
                routed[0] += 1
                ins.then_inc(routed_dve, 1)
                dve.wait_ge(routed_dve, routed[0])

            def attention(segment):
                def body(n_, t, par):
                    en, e, eg, ep = sequence(segment, n_, t, par, NORM)
                    an, a, ag, ap = sequence(segment, n_, t, par, PROJECT)
                    cn, c, cg, cp = sequence(segment, n_, t, par, ROW_MAX)
                    fn, f, fg, fp = sequence(segment, n_, t, par, FINISH)
                    rn, r, rg, rp = router_item(segment, n_, t, par, NORM2)
                    un, u, ug, up = router_item(segment, n_, t, par, ROUTER)
                    wn, w, wg, wp = router_item(segment, n_, t, par, PLACE)

                    def maximum(gr):
                        after(dve, rowmax_ps, 4 * cg + gr + 1)
                        if gr == 0:
                            after(dve, negmaxT_ps, cg - 1)
                        dve.tensor_reduce(negmax[:, cp, gr, 0:PER],
                                          rowmax_bank[gr % 2][:].rearrange("p (h k) -> p h k", k=S),
                                          X_AXIS, ALU.max, negate=True).then_inc(max_done, 1)
                    if e is not None:
                        if en == 0 and isinstance(e, int) and e in (0, 3):
                            for q in range(4) if e else range(1):
                                dve.wait_ge(x_in_sem[q], 16)
                        elif en == 3:
                            mix(0, e, ep)
                            dve.wait_ge(mix_done, e + 1)
                        elif en:
                            dve.wait_ge(resid_done, eg - B + 1)
                        apart(dve, (aggr_done, eg - 1))
                        dve.bn_stats(stats[:, ep, :], x_all[:, e, :]).then_inc(stats_done, 1)
                    if r is not None:
                        rows_of = h_all if rn == 2 else x_all
                        apart(dve, (resid_done, B * rn + r + 1),
                              (r_aggr_done, rg - 1))
                        dve.bn_stats(r_stats[:, rp, :], rows_of[:, r, :]).then_inc(r_stats_done, 1)
                    if f is not None:
                        per_head = ot_bank[:].rearrange("p (h c) -> p h c", c=32)
                        after(dve, oT_ps, fg + 1)
                        after(dve, att_done, fg - 1)
                        dve.reciprocal(rden[:, fp, :].unsqueeze(2), per_head[:, :, HD:HD + 1]).then_inc(rden_done, 1)
                        after(dve, rden_done, fg + 1)
                        after(dve, attT_ps, fg - 1)
                        dve.tensor_tensor(att[:, fp, :].rearrange("p (h d) -> p h d", d=HD),
                                          per_head[:, :, 0:HD],
                                          rden[:, fp, :].unsqueeze(2).to_broadcast([128, H, HD]),
                                          ALU.mult).then_inc(att_done, 1)
                    if c is not None:
                        maximum(0)
                    if e is not None:
                        apart(dve, (stats_done, eg + 1),
                              (vareps_done, eg - 1),
                              (xn_done, eg - 1))
                        dve.bn_aggr(meanvar[:, ep, :], stats[:, ep, :]).then_inc(aggr_done, 1)
                    if r is not None:
                        apart(dve, (r_stats_done, rg + 1),
                              (r_vareps_done, rg - 1),
                              (r_x_done, rg - 1))
                        dve.bn_aggr(r_meanvar[:, rp, :], r_stats[:, rp, :]).then_inc(r_aggr_done, 1)
                    if c is not None:
                        maximum(1)
                    if e is not None:
                        after(dve, rstd_done, eg + 1)
                        after(dve, xT_ps, eg - 1)
                        if STAGES[en]["inner"]:
                            after(dve, hidden_kept, e - 1)
                        dve.tensor_scalar(xn[:, ep, :], x_all[:, e, :], meanvar[:, ep, 0:1], rstd[:, ep:ep + 1],
                                          ALU.subtract, ALU.mult).then_inc(xn_done, 1)
                    if r is not None:
                        after(dve, r_rstd_done, rg + 1)
                        after(dve, r_xT_ps, rg - 1)
                        after(dve, r_h_kept, rg - 1)
                        dve.tensor_scalar(r_x[:, rp, :], rows_of[:, r, :], r_meanvar[:, rp, 0:1],
                                          r_rstd[:, rp:rp + 1], ALU.subtract, ALU.mult).then_inc(r_x_done, 1)
                    if c is not None:
                        maximum(2)
                        maximum(3)
                    if f is not None:
                        after(dve, y_ps, fg + 1)
                        if STAGES[fn]["inner"]:
                            after(dve, hidden_kept, f + 1)
                            dve.tensor_tensor(h_all[:, f, :], h_all[:, f, :], o_bank[:, 0:D], ALU.add) \
                                .then_inc(h2_done, 1)
                            after(dve, h2_done, f + 1)
                            ins = dve.tensor_tensor(x_all[:, f, :], x_all[:, f, :], h_all[:, f, :], ALU.add)
                        else:
                            ins = dve.tensor_tensor(x_all[:, f, :], x_all[:, f, :], o_bank[:, 0:D], ALU.add)
                        ins.then_inc(resid_done, 1)
                    if c is not None:
                        after(dve, negmaxT_ps, cg + 1)
                        after(dve, score_ps, 4 * cg - 4)
                        dve.tensor_tensor(shift[:, cp], ot_bank[:, NEGMAX_COLS].unsqueeze(1).to_broadcast(seqs),
                                          head_of_max, ALU.mult).then_inc(shift_done, 1)
                    if u is not None:
                        after(dve, r_logit_ps, ug + 1)
                        if w is not None:
                            after(dve, r_count_ps, wg + 1)
                        after(dve, r_kept, ug - 1)
                        dve.tensor_copy(r_row[:, up, LOGITS], ot_bank[:, LOGIT_COLS]).then_inc(r_logit_done, 1)
                    if w is not None:
                        wl = layer_of[wn]
                        per_choice = lambda ap: ap.rearrange("p (k e) -> p k e", k=2)
                        after(dve, r_count_ps, wg + 1)
                        after(dve, r_carry_done, wg)
                        after(dve, r_placed_done, wg - 1)
                        dve.tensor_tensor(place[:, wp], per_choice(ot_bank[:, COUNT_COLS]), carry[:, wl, wp], ALU.add) \
                            .then_inc(r_place_done, 1)
                        dve.tensor_tensor(carry[:, wl, 1 - wp], per_choice(ot_bank[:, TOTAL_COLS]), carry[:, wl, wp],
                                          ALU.add).then_inc(r_carry_done, 1)
                    if a is not None:
                        if STAGES[an]["mask"] == "keys":
                            dve.wait_ge(key_in_sem[ap], (a // 2 + 1) * 16)
                            after(dve, score_ps, 4 * ag - 4)
                            dve.tensor_scalar(keyrow_bf[0:1, ap, :], keyrow[:, ap, :], BIG / SCALE, -BIG / SCALE,
                                              ALU.mult, ALU.add).then_inc(keyrow_done, 1)
                        if STAGES[an]["rope"]:
                            after(dve, rawq_done, a + 1)
                            after(dve, qT_done, a - 1)
                            dve.tensor_tensor(prod[:, ap, 0:2, :], raw[:, ap, 0:2, :], rope[:], ALU.mult) \
                                .then_inc(qprod_done, 1)
                            after(dve, qprod_done, a + 1)
                            after(dve, q_bf_done, ag - 1)
                            dve.tensor_tensor(qT[:, ap, :], prod[:, ap, 0, :], prod[:, ap, 1, :], ALU.add) \
                                .then_inc(qT_done, 1)
                            after(dve, qT_done, a + 1)
                            after(dve, score_ps, 4 * ag - 4)
                            dve.tensor_tensor(q_masked[:, ap], qT[:, ap, :].unsqueeze(1).to_broadcast(seqs8),
                                              head_of_row, ALU.mult).then_inc(q_masked_done, 1)
                        else:
                            after(dve, q_bf_done, ag + 1)
                            after(dve, score_ps, 4 * ag - 4)
                            dve.scalar_tensor_tensor(out=q_masked[:, ap],
                                                     in0=misc_bank[:, Q_COLS].unsqueeze(1).to_broadcast(seqs8),
                                                     scalar=cols[:, COL_BQ + an:COL_BQ + an + 1], in1=head_of_row,
                                                     op0=ALU.add, op1=ALU.mult).then_inc(q_masked_done, 1)
                    if w is not None:
                        after(dve, r_place_done, wg + 1)
                        after(dve, r_sum_done, 2 * wg - 2)
                        dve.tensor_tensor(placed[:, wp], place[:, wp], onehot[:, wp], ALU.mult) \
                            .then_inc(r_placed_done, 1)
                        after(dve, r_placed_done, wg + 1)
                        for q in range(2):
                            dve.tensor_reduce(r_row[:, wp, PLACES.start + q:PLACES.start + q + 1], placed[:, wp, q],
                                              X_AXIS, ALU.add, negate=bool(wn == 2 and q)).then_inc(r_sum_done, 1)
                        after(dve, r_sum_done, 2 * wg + 2)
                        after(dve, sent_done, wg - 1)
                        for q in range(2):
                            if not (isinstance(w, int) and w < 2):
                                if q == wp:
                                    dve.wait_ge(scattered[q], (w // 2 + 16 * wl) * 32)
                        dve.tensor_copy(dest[:, wp, :], r_row[:, wp, PLACES]).then_inc(r_dest_done, 1)
                    if u is not None:
                        after(dve, r_logit_done, ug + 1)
                        E = MOE[layer_of[un]]["E"]
                        apart(dve, (r_logit_done, ug + 1))
                        dve.max(r_row[:, up, TOP], r_row[:, up, 0:E]).then_inc(r_top_done, 1)
                        apart(dve, (r_top_done, ug + 1),
                              (r_choice_done, ug - 1))
                        dve.max_index(topi[:, up, :], r_row[:, up, TOP], r_row[:, up, 0:E]).then_inc(r_topi_done, 1)
                        after(dve, r_topi_done, ug + 1)
                        dve.tensor_copy(r_row[:, up, CHOICE], topi[:, up, 0:2]).then_inc(r_choice_done, 1)
                        after(dve, r_choice_done, ug + 1)
                        after(dve, r_count_ps, ug - 1)
                        after(dve, r_placed_done, ug - 1)
                        for q in range(2):
                            sign = -1.0 if un == 2 and q else 1.0
                            chosen = r_row[:, up, CHOICE.start + q:CHOICE.start + q + 1]
                            dve.tensor_scalar(onehot[:, up, q, :], iotas[:, 0:16], chosen, sign, ALU.is_equal,
                                              ALU.mult).then_inc(r_onehot_done, 1)
                sequences(dve, segment, body)

            e_row = iotas[:, 0:16]

            def tiles(l):
                m = MOE[l]
                dve.wait_ge(r_carry_done, B * (l + 1))
                link(dve.scalar_tensor_tensor(out=per_e[:, 0, :], in0=e_row, scalar=-float(REGION[l]),
                                              in1=carry[:, l, 0, 0, :], op0=ALU.mult, op1=ALU.add))
                if l == 0:
                    link(dve.tensor_tensor(second[:], iotas[:, 64:68].unsqueeze(2).to_broadcast([128, 4, 16]),
                                           per_e[:, 0, :].unsqueeze(1).to_broadcast([128, 4, 16]), ALU.is_gt))
                else:
                    ends, used, i_tile = per_e[:, 3, :], per_e[:, 2, :], iotas[:, 16:64]
                    link(dve.tensor_scalar(per_e[:, 1, :], per_e[:, 0, :], float(m["R"]), None, ALU.add))
                    link(dve.tensor_copy(per_ei[:, 0, :], per_e[:, 1, :]))
                    link(dve.tensor_scalar(per_ei[:, 1, :], per_ei[:, 0, :], m["R"].bit_length() - 1, None,
                                           ALU.arith_shift_right))
                    link(dve.tensor_copy(used, per_ei[:, 1, :]))
                    link(dve.tensor_tensor_scan(ends, ones_e[:], used, 0.0, ALU.mult, ALU.add))
                    link(dve.tensor_tensor(tile_cmp[:, 0], ends.unsqueeze(1).to_broadcast([128, 48, 16]),
                                           i_tile.unsqueeze(2).to_broadcast([128, 48, 16]), ALU.is_le))
                    link(dve.tensor_reduce(tile_f[:, 0, :], tile_cmp[:, 0], X_AXIS, ALU.add))
                    link(dve.tensor_tensor(tile_cmp[:, 1], used.unsqueeze(1).to_broadcast([128, 48, 16]),
                                           tile_cmp[:, 0], ALU.mult))
                    link(dve.tensor_reduce(tile_f[:, 1, :], tile_cmp[:, 1], X_AXIS, ALU.add))
                    link(dve.tensor_scalar(tile_f[:, 2, :], tile_f[:, 0, :], float(m["E"] - 1), None, ALU.min))
                    link(dve.tensor_copy(tile_expert[:], tile_f[:, 2, :]))
                    row = tile_f[:, 3, :]
                    link(dve.tensor_scalar(row, tile_f[:, 0, :], float(REGION[l]), None, ALU.mult))
                    link(dve.scalar_tensor_tensor(out=row, in0=i_tile, scalar=float(m["R"]), in1=row,
                                                  op0=ALU.mult, op1=ALU.add))
                    link(dve.scalar_tensor_tensor(out=row, in0=tile_f[:, 1, :], scalar=-float(m["R"]), in1=row,
                                                  op0=ALU.mult, op1=ALU.add))
                    link(dve.tensor_scalar(tile_f[:, 0, :], row, float(m["E"] * REGION[1]), None, ALU.min))
                    link(dve.tensor_copy(tile_row[:], tile_f[:, 0, :]))
                    link(dve.tensor_tensor(per_e[:, 4, :], ends, used, ALU.subtract))
                    link(dve.tensor_scalar(per_e[:, 4, :], per_e[:, 4, :], float(m["R"]), None, ALU.mult))
                    link(dve.scalar_tensor_tensor(out=per_e[:, 4, :], in0=e_row, scalar=-float(REGION[l]),
                                                  in1=per_e[:, 4, :], op0=ALU.mult, op1=ALU.add))
                assert routed[0] == TILED[l], routed

            def weights_of_choices(l):
                m = MOE[l]
                dve.wait_ge(r_kept, B * (l + 1))
                top1, top2 = kept[:, :, TOP.start], kept[:, :, TOP.start + 1]
                ch = [kept[:, :, CHOICE.start + q] for q in range(2)]
                at = [kept[:, :, PLACES.start + q] for q in range(2)]
                link(dve.tensor_tensor(small[:, 1, :], top2, top1, ALU.subtract))
                if l == 0:
                    link(dve.tensor_tensor(wide[:, 0], kept[:, :, LOGITS],
                                           kept[:, :, TOP.start:TOP.start + 1].to_broadcast([128, B, 16]), ALU.subtract))
                assert routed[0] == DIFFS[l], routed
                if l == 1:
                    for q in range(2):
                        link(dve.tensor_tensor(wide[:, 0], e_row.unsqueeze(1).to_broadcast([128, B, 16]),
                                               kept[:, :, CHOICE.start + q:CHOICE.start + q + 1]
                                               .to_broadcast([128, B, 16]), ALU.is_equal))
                        link(dve.tensor_tensor(wide[:, 0], wide[:, 0],
                                               per_e[:, 4, :].unsqueeze(1).to_broadcast([128, B, 16]), ALU.mult))
                        link(dve.tensor_reduce(small[:, 3, :], wide[:, 0], X_AXIS, ALU.add))
                        link(dve.tensor_tensor(small[:, 3, :], small[:, 3, :], at[q], ALU.add))
                        link(dve.tensor_copy(source[:, q, :], small[:, 3, :]))
                    dve.wait_ge(routed_act, 3)
                    link(dve.tensor_scalar(small[:, 9, :], small[:, 2, :], 1.0, None, ALU.add))
                    link(dve.reciprocal(weight[:, 0, :], small[:, 9, :]))
                    link(dve.tensor_tensor(weight[:, 1, :], weight[:, 0, :], small[:, 2, :], ALU.mult))
                    assert routed[0] == ROUTED[l], routed
                    return
                C = m["cap"]
                slot, after_all, in1, in2, row = (small[:, i, :] for i in (3, 4, 5, 6, 7))
                link(dve.scalar_tensor_tensor(out=slot, in0=ch[0], scalar=-float(REGION[l]), in1=at[0],
                                              op0=ALU.mult, op1=ALU.add))
                link(dve.tensor_scalar(in1, slot, float(C), None, ALU.is_lt))
                dve.wait_ge(routed_act, 2)
                link(dve.tensor_tensor(wide[:, 0], e_row.unsqueeze(1).to_broadcast([128, B, 16]),
                                       kept[:, :, CHOICE.start + 1:CHOICE.start + 2].to_broadcast([128, B, 16]),
                                       ALU.is_equal))
                link(dve.tensor_tensor(wide[:, 0], wide[:, 0],
                                       carry[:, 0, 0, 0, :].unsqueeze(1).to_broadcast([128, B, 16]), ALU.mult))
                link(dve.tensor_reduce(after_all, wide[:, 0], X_AXIS, ALU.add))
                link(dve.tensor_tensor(after_all, after_all, at[1], ALU.subtract))
                link(dve.tensor_scalar(in2, after_all, float(C - REGION[0]), None, ALU.is_lt))
                for q in range(2):
                    link(dve.scalar_tensor_tensor(out=row, in0=ch[q], scalar=float(C - REGION[0]), in1=at[q],
                                                  op0=ALU.mult, op1=ALU.add))
                    link(dve.tensor_scalar(row, row, float(q * (C - REGION[0])), 0.0, ALU.add, ALU.max))
                    link(dve.tensor_scalar(row, row, float(ROWS_OUT[0] - 1), None, ALU.min))
                    link(dve.tensor_copy(source[:, q, :], row))
                z, g1, g2, den = (small[:, i, :] for i in (9, 10, 11, 12))
                link(dve.tensor_reduce(z, wide[:, 1], X_AXIS, ALU.add))
                link(dve.reciprocal(z, z))
                link(dve.tensor_tensor(g1, in1, z, ALU.mult))
                link(dve.tensor_tensor(g2, in2, z, ALU.mult))
                link(dve.tensor_tensor(g2, g2, small[:, 2, :], ALU.mult))
                link(dve.tensor_tensor(den, g1, g2, ALU.add))
                link(dve.tensor_scalar(den, den, float(np.finfo(np.float32).eps), None, ALU.max))
                link(dve.reciprocal(den, den))
                for k, gk in enumerate((g1, g2)):
                    link(dve.scalar_tensor_tensor(out=weight[:, k, :], in0=gk, scalar=m["factor"], in1=den,
                                                  op0=ALU.mult, op1=ALU.mult))
                assert routed[0] == ROUTED[l], routed

            def experts(l):
                m = MOE[l]
                blocks, base = m["R"] // 128, sum(x["tiles"] for x in MOE[:l])

                def body(t, par):
                    if isinstance(t, int) and t == 2:
                        weights_of_choices(l)
                    d, q = item(t, par, 0, m["tiles"])
                    if d is not None and l == 0:
                        dve.wait_ge(tile_in_sem[q], (d // 2 + 1) * 32)
                        for r in range(blocks):
                            ins = dve.scalar_tensor_tensor(out=tile_rows[:, q, r, :], in0=tile_rows2[:, q, r, :],
                                                           scalar=second[:, r, bass.ds(d, 1)], in1=tile_rows[:, q, r, :],
                                                           op0=ALU.mult, op1=ALU.add)
                        ins.then_inc(tile_done, 1)
                    a, p = item(t, par, 1, m["tiles"])
                    if a is None:
                        return
                    g = base + a
                    after(dve, fc2_ps, g + 1)
                    if not (isinstance(a, int) and g < 2):
                        dve.wait_ge(stored[p], (a // 2 + base // 2) * 16)
                    dve.tensor_tensor(rows_out[:, p, 0:blocks, :],
                                      (o_bank, kv_bank)[p][:, 0:128 * blocks].rearrange("p (r d) -> p r d", d=D),
                                      pack[:, p, 2 * F + FCH:].unsqueeze(1).to_broadcast([128, blocks, D]),
                                      ALU.add).then_inc(rows_out_done, 1)
                steps(dve, 2, body, m["tiles"], 4)

            def mix(l, b, p):
                dve.wait_ge(gathered[p], (b // 2 + (16 * l + 1)) * 32)
                dve.scalar_tensor_tensor(out=x_all[:, b, :], in0=moved[:, p, 0, :], scalar=weight[:, 0, bass.ds(b, 1)],
                                         in1=x_all[:, b, :], op0=ALU.mult, op1=ALU.add).then_inc(mix_half, 1)
                dve.wait_ge(mix_half, B * l + b + 1)
                dve.scalar_tensor_tensor(out=x_all[:, b, :], in0=moved[:, p, 1, :], scalar=weight[:, 1, bass.ds(b, 1)],
                                         in1=x_all[:, b, :], op0=ALU.mult, op1=ALU.add).then_inc(mix_done, 1)

            for ap, v in ((ones_bf[:], 1.0), (ones_row[:], 1.0), (v_aug[:], 1.0), (negmax[:], 0.0),
                          (keyrow_bf[:], 0.0)):
                dve.memset(ap, v).then_inc(setup_done, 1)
            dve.memset(o_bank[:], 0.0).then_inc(setup_done, 1)
            dve.memset(ones_e[:], 1.0).then_inc(setup_done, 1)
            dve.wait_ge(const_in, 16 * N_CONST)
            dve.tensor_copy(masks[:].rearrange("p m c -> p (m c)"), masks_f32).then_inc(setup_done, 1)
            dve.tensor_copy(ident_bf[:], ident[:]).then_inc(setup_done, 1)
            dve.tensor_copy(lower_bf[:], lower[:]).then_inc(setup_done, 1)
            start(dve)
            for l, segment in enumerate(SEGMENTS):
                attention(segment)
                if stop > (2, 5)[l]:
                    tiles(l)
                    experts(l)
            if stop > 5:
                steps(dve, 1, lambda t, par: item(t, par, 1)[0] is not None and mix(1, *item(t, par, 1)))

        @block.gpsimd
        def _(pool):
            head_of_row = row_head[:].unsqueeze(2).to_broadcast([128, HALF, S])

            def rsqrt(g, p, variance, to, result, ready, first_done, done, used):
                apart(pool, (ready, g + 1),
                      (done, g - 1))
                pool.tensor_scalar(to[:, p:p + 1], variance[:, p, 1:2], EPS, None, ALU.add).then_inc(first_done, 1)
                apart(pool, (first_done, g + 1),
                      (used, g - 1))
                pool.tensor_tensor(result[:, p:p + 1], to[:, p:p + 1], neghalf[:], ALU.pow).then_inc(done, 1)

            def rows_are_back(l):
                tiles = sum(m["tiles"] for m in MOE[:l + 1])
                pool.wait_ge(stored[0], 16 * ((tiles + 1) // 2))
                pool.wait_ge(stored[1], 16 * (tiles // 2))
                pool.wait_ge(routed_dve, ROUTED[l])

            def gather(l, b, p):
                first = l == 0 and isinstance(b, int) and b < 2
                apart(pool, *([] if first else [(mix_done, B * l + b - 1),
                                                (gathered[p], (b // 2 + 16 * l) * 32)]))
                pool.tensor_copy(index[:, p, :], source[:, :, b]).then_inc(index_done, 1)
                apart(pool, (index_done, B * l + b + 1))
                for k in range(2):
                    pool.indirect_dma_start(
                        out=moved[:, p, k, :], out_offset=None, in_=eout[l],
                        in_offset=bass.IndirectOffsetOnAxis(ap=index[:, p, k:k + 1].bitcast(U32), axis=0)) \
                        .then_inc(gathered[p], 16)

            def attention(segment):
                def body(n_, t, par):
                    en, e, eg, ep = sequence(segment, n_, t, par, NORM)
                    an, a, ag, ap = sequence(segment, n_, t, par, PROJECT)
                    mn, m_, mg, mp = sequence(segment, n_, t, par, MIX)
                    rn, r, rg, rp = router_item(segment, n_, t, par, NORM2)
                    wn, w, wg, wp = router_item(segment, n_, t, par, PLACE)
                    if mn == 3 and m_ is not None:
                        if isinstance(m_, int) and m_ == 0:
                            rows_are_back(0)
                        gather(0, m_, mp)
                    if e is not None:
                        rsqrt(eg, ep, meanvar, vareps, rstd, aggr_done, vareps_done, rstd_done, xn_done)
                        if STAGES[en]["inner"]:
                            apart(pool, (xn_done, eg + 1))
                            pool.tensor_copy(h_all[:, e, :], xn[:, ep, :]).then_inc(hidden_kept, 1)
                    if r is not None:
                        rsqrt(rg, rp, r_meanvar, r_vareps, r_rstd, r_aggr_done, r_vareps_done, r_rstd_done, r_x_done)
                        apart(pool, (r_x_done, rg + 1))
                        pool.tensor_copy(h_all[:, r, :], r_x[:, rp, :]).then_inc(r_h_kept, 1)
                    if a is not None:
                        if STAGES[an]["rope"]:
                            pool.wait_ge(rawk_done, a + 1)
                            after(pool, k_done, ag - 1)
                            pool.tensor_tensor(prod[:, ap, 2:4, :], raw[:, ap, 2:4, :], rope[:], ALU.mult) \
                                .then_inc(kprod_done, 1)
                            pool.wait_ge(kprod_done, a + 1)
                            after(pool, score_ps, 4 * ag - 4)
                            after(pool, k_masked_done, ag - 1)
                            pool.tensor_tensor(kT[:, ap, :], prod[:, ap, 2, :], prod[:, ap, 3, :], ALU.add) \
                                .then_inc(k_done, 1)
                        after(pool, k_done, ag + 1)
                        after(pool, rowmax_ps, 4 * ag - 4)
                        pool.tensor_tensor(k_masked[:, ap], kT[:, ap, :].unsqueeze(1).to_broadcast([128, HALF, S]),
                                           head_of_row, ALU.mult).then_inc(k_masked_done, 1)
                    if w is not None:
                        if isinstance(w, int) and w == 0 and wn == 2:
                            pool.wait_ge(zero_in, 16 * N_ZERO)
                        apart(pool, (r_dest_done, wg + 1),
                              (r_onehot_done, 2 * wg + 2),
                              (r_h_kept, wg + 1))
                        pool.tensor_copy(kept[:, w, :], r_row[:, wp, :]).then_inc(r_kept, 1)
                        first = isinstance(w, int) and w < 2
                        apart(pool, *([] if first and wn == 2 else
                                      [(scattered[wp], (w // 2 + 16 * layer_of[wn]) * 32)]))
                        pool.tensor_copy(sent[:, wp, :], h_all[:, w, :]).then_inc(sent_done, 1)
                        apart(pool, (sent_done, wg + 1))
                        for q in range(2):
                            pool.indirect_dma_start(
                                out=xin[layer_of[wn]],
                                out_offset=bass.IndirectOffsetOnAxis(ap=dest[:, wp, q:q + 1].bitcast(U32), axis=0),
                                in_=sent[:, wp, :], in_offset=None).then_inc(scattered[wp], 16)
                sequences(pool, segment, body)

            pool.memset(neghalf[:], -0.5).then_inc(setup_done, 1)
            pool.memset(hidden[:], 0.0).then_inc(setup_done, 1)
            start(pool)
            for l, segment in enumerate(SEGMENTS):
                attention(segment)
            if stop > 5:
                rows_are_back(1)
                steps(pool, 1, lambda t, par: item(t, par, 0)[0] is not None and gather(1, *item(t, par, 0)))


def constants():
    q, k = np.arange(S)[:, None], np.arange(S)[None, :]
    window = np.where((k <= q) & (q - k < WINDOW), 0.0, -BIG)
    causal = np.where(k <= q, 0.0, -BIG)
    masks = np.stack([np.tile(m, (1, PER)) for m in (window, window.T, causal, causal.T)], 1)
    p = np.arange(128)
    row_head = (p[:, None] % 64) // HD == np.arange(HALF)
    max_head = p[:, None] % 32 == np.arange(PER)
    inv_freq = 1.0 / np.float32(10000.0) ** (np.arange(0, HD, 2, dtype=np.float32) / np.float32(HD))
    theta = np.arange(S, dtype=np.float32)[:, None] * inv_freq[None, :].astype(np.float32)
    cos, sin = (np.tile(np.repeat(f(theta), 2, axis=1), (1, H)).T for f in (np.cos, np.sin))
    sign = np.where(p % 2 == 0, -1.0, 1.0)[:, None]
    iotas = np.concatenate([np.tile(np.arange(16), (128, 1)), np.tile(np.arange(48), (128, 1)),
                            np.arange(4)[None, :] * 128 + p[:, None]], 1)
    e = np.arange(16)
    carry = np.tile(np.array([[e * REGION[0] - 1, (e + 1) * REGION[0]], [e * REGION[1] - 1] * 2]), (128, 1, 1, 1))
    f32 = lambda a: np.ascontiguousarray(a, np.float32)
    return dict(ident=f32(np.eye(128)), masks=f32(masks),
                row_head=f32(row_head), max_head=f32(max_head), rope=f32(np.stack([cos, sin * sign], 1)), iotas=f32(iotas),
                carry=f32(carry), lower=f32(p[:, None] <= p[None, :]))


def layout(inputs):
    a = {k: np.asarray(v) for k, v in inputs.items()}
    qkv = a["L0_attn_w_qkv"]
    w = [qkv[0:128].T, qkv[128:256].T, qkv[256:384].T, a["L0_attn_w_out"].T]
    w += [a["L0_xattn_W" + k] for k in "qkvo"] + [a[f"L0_ffn_{k}_w"] for k in "qkvo"]
    w += [a["L1_attn_W" + k] for k in "qkvo"] + [a["L1_xattn_W" + k] for k in "qkvo"]
    swap = np.arange(128) ^ 1
    w += [a["L1_attn_Wq"][:, swap], a["L1_attn_Wk"][:, swap]]
    zero, one = np.zeros(128, np.float32), np.ones(128, np.float32)
    bias = lambda k: [zero, a["L0_xattn_b" + k], a[f"L0_ffn_{k}_b"], zero, a["L1_xattn_b" + k]]
    cols = bias("q") + bias("k") + bias("v") + [a["L0_ffn_ln1_w"], a["L0_ffn_ln1_b"], a["L0_ffn_ln2_w"],
                                                a["L0_ffn_ln2_b"], one, zero]
    rows = [a["L0_attn_b_out"], a["L0_xattn_bo"], a["L0_ffn_o_b"], zero, a["L1_xattn_bo"]]
    router = np.zeros((128, 2, 16), np.float32)
    router[:, 0, :] = a["L0_ffn_router_w"]
    router[:, 1, 0:8] = a["L1_ffn_Wg"].T

    def pack(w1, b1, w2, b2):
        E = w1.shape[0]
        return np.concatenate([
            w1, w2.reshape(E, FCH, 128, D).transpose(0, 2, 1, 3).reshape(E, 128, FCH * D),
            b1.reshape(E, FCH, 128).transpose(0, 2, 1), np.broadcast_to(b2[:, None, :], (E, 128, D))], axis=2)
    return dict(
        x=a["x"], ctx=a["ctx_1024"].reshape(T, D).T, keymask=a["mask_BxS2_ff1"].reshape(1, T),
        weights=np.stack(w, 1), cols=np.stack(cols, 1), rows=np.stack(rows)[None], router=router,
        pack0=pack(a["L0_ffn_fc1_w"], a["L0_ffn_fc1_b"], a["L0_ffn_fc2_w"], a["L0_ffn_fc2_b"]),
        pack1=pack(a["L1_ffn_W1"].transpose(0, 2, 1), a["L1_ffn_b1"], a["L1_ffn_W2"].transpose(0, 2, 1),
                   a["L1_ffn_b2"]))


def kernel(**inputs):
    import concourse.bacc as bacc
    from concourse.bass_utils import run_bass_kernel_spmd

    nc = bacc.Bacc("TRN2", target_bir_lowering=False, num_devices=1)
    arrays, args = {}, []
    for name, a in {**layout(inputs), **constants()}.items():
        a = np.ascontiguousarray(a)
        arrays[f"in_{name}"] = a
        args.append(nc.dram_tensor(f"in_{name}", a.shape, mybir.dt.from_np(a.dtype), kind="ExternalInput").ap())
    args.append(nc.dram_tensor("out_0", (B, S, D), F32, kind="ExternalOutput").ap())
    build(nc, *args)
    r = run_bass_kernel_spmd(nc, [arrays], core_ids=[0])
    return r.results[0]["out_0"]
```

```python
from contextlib import ExitStack

import numpy as np

import concourse.bass as bass
from concourse import mybir

F32 = mybir.dt.float32
BF16 = mybir.dt.bfloat16
I32 = mybir.dt.int32
U32 = mybir.dt.uint32
ALU = mybir.AluOpType
ACT = mybir.ActivationFunctionType
X_AXIS = mybir.AxisListType.X

B, S, D, H, HD = 32, 128, 128, 16, 8
T = B * S
GROUPS, PER = 4, 4
HALF = 8
SCALE = HD ** -0.5
EPS = 1e-5
BIG = 1e30
WINDOW = 64
F = 512
WARM_UP = 24
MIX, NORM, PROJECT, ROW_MAX, KEYS, FINISH, NORM2, ROUTER, PLACE, SEND = 0, 1, 2, 3, 4, 5, 6, 7, 8, 9
HEAD = SEND
LEAD = [8, 6, 12, 6, 10]
FCH = F // 128

STAGES = [
    dict(name="L0_attn", cross=False, mask="window", rope=False, bo=True, inner=False),
    dict(name="L0_xattn", cross=True, mask=None, rope=False, bo=True, inner=False),
    dict(name="L0_ffn", cross=False, mask="causal", rope=False, bo=True, inner=True),
    dict(name="L1_attn", cross=False, mask="causal", rope=True, bo=False, inner=False),
    dict(name="L1_xattn", cross=True, mask="keys", rope=False, bo=True, inner=False),
]
COL_BQ, COL_BK, COL_BV = 0, 5, 10
COL_LN1W, COL_LN1B, COL_LN2W, COL_LN2B, COL_ONE, COL_ZERO = 15, 16, 17, 18, 19, 20
NCOL = 21
W_SWQ, W_SWK, NW = 20, 21, 22

MOE = [dict(E=16, R=512, tiles=16, cap=2 * T // 16, factor=0.8),
       dict(E=8, R=512, tiles=(2 * T + 8 * 511) // 512, cap=None, factor=1.0)]
REGION = [T + MOE[0]["cap"], T]
ROWS_IN = [MOE[0]["E"] * REGION[0], MOE[1]["E"] * REGION[1] + MOE[1]["R"]]
ROWS_OUT = [MOE[0]["E"] * MOE[0]["cap"], MOE[1]["tiles"] * MOE[1]["R"]]
TILED, DIFFS, ROUTED = (2, 49), (4, 50), (29, 63)
N_ZERO = 2 * B
N_KEPT = 28
LOGITS, TOP, CHOICE, PLACES = slice(0, 16), slice(16, 24), slice(24, 26), slice(26, 28)
HALF_ROWS = [slice(0, 64), slice(64, 128)]
MAX_ROW = [64, 32]
PACK1, PACK2 = F + FCH, F + 128


def build(nc, x_in, ctx_in, keymask_in, weights_in, cols_in, out_bias_in, router_in, pack0_in, pack1_in,
          ident_in, masks_in, row_head_in, upper_head_in, rope_in, iotas_in, carry_in, lower_in, out, stop=99):
    xin = [nc.dram_tensor(f"expert_in{l}", (ROWS_IN[l], D), F32).ap() for l in range(2)]
    eout = [nc.dram_tensor(f"expert_out{l}", (ROWS_OUT[l], D), F32).ap() for l in range(2)]
    packs = [pack0_in, pack1_in]

    with ExitStack() as ctx:
        def sb(name, shape, dt=F32):
            return ctx.enter_context(nc.sbuf_tensor(name, shape, dt))

        def sem(name):
            return ctx.enter_context(nc.semaphore(name))

        x_all = sb("x_all", [128, B, D])
        h_all = sb("h_all", [128, B, D])
        weights = sb("weights", [128, NW, 128])
        cols = sb("cols", [128, NCOL])
        out_bias = sb("out_bias", [128, 5, D])
        router = sb("router", [128, 2, 16])
        ident = sb("ident", [128, 128])
        ident_bf = sb("ident_bf", [128, 128], BF16)
        masks = sb("masks", [128, 4, 512], BF16)
        ones_bf = sb("ones_bf", [128, 512], BF16)
        row_head = sb("row_head", [128, HALF])
        upper_head = sb("upper_head", [128, HALF])
        rope = sb("rope", [128, 2, 128])
        iotas = sb("iotas", [128, 68])
        lower = sb("lower", [128, 128])
        lower_bf = sb("lower_bf", [128, 128], BF16)
        stats = sb("stats", [128, 2, 6])
        meanvar = sb("meanvar", [128, 2, 2])
        vareps = sb("vareps", [128, 2])
        rstd = sb("rstd", [128, 2])
        neghalf = sb("neghalf", [128, 1])
        ones_e = sb("ones_e", [128, 16])
        xn = sb("xn", [128, 2, D])
        xT = sb("xT", [128, 2, S])
        ctxT = sb("ctxT", [128, 2, S])
        raw = sb("raw", [128, 2, 4, S])
        prod = sb("prod", [128, 2, 4, S])
        qT = sb("qT", [128, 2, S])
        q_bf = sb("q_bf", [128, 2, S], BF16)
        kT = sb("kT", [128, 2, S])
        v_aug = sb("v_aug", [128, 2, H, HD + 1])
        k_rows = sb("k_rows", [128, 2, 2, S])
        q_rows = sb("q_rows", [128, 2, 2, HALF, S])
        k_masked = sb("k_masked", [128, 2, HALF, S], BF16)
        keyrow = sb("keyrow", [1, 2, S])
        keyrow_bf = sb("keyrow_bf", [128, 2, S], BF16)
        negmax = sb("negmax", [128, 2, H])
        negmaxT = sb("negmaxT", [H, 2, S])
        probs = sb("probs", [128, 2, H, S])
        masks_f32 = probs[:, 0].rearrange("p h s -> p (h s)")
        o_sb = sb("o_sb", [128, 2, 4, S])
        rden = sb("rden", [128, 2, H])
        att = sb("att", [128, 2, D])
        attT = sb("attT", [128, 2, S])
        bank = [ctx.enter_context(nc.psum_tensor(f"bank{i}", [128, 512], F32)) for i in range(8)]
        rowmax_bank, score_bank, o_bank, ot_bank, kv_bank, misc_bank = (
            bank[0:2], bank[2:4], bank[4], bank[5], bank[6], bank[7])
        XT_COLS, Q_COLS, QSW_COLS = (slice(128 * i, 128 * i + 128) for i in range(3))
        K_COLS, V_COLS, KSW_COLS = (slice(128 * i, 128 * i + 128) for i in range(3))
        ATT_COLS, RX_COLS = slice(0, 128), slice(256, 384)
        LOGIT_COLS, COUNT_COLS, TOTAL_COLS = slice(384, 400), slice(400, 432), slice(432, 464)
        NEGMAX_COLS = slice(0, 128)
        r_stats = sb("r_stats", [128, 2, 6])
        r_meanvar = sb("r_meanvar", [128, 2, 2])
        r_vareps = sb("r_vareps", [128, 2])
        r_rstd = sb("r_rstd", [128, 2])
        r_x = sb("r_x", [128, 2, D])
        r_xT = sb("r_xT", [128, 2, S])
        r_row = sb("r_row", [128, 2, N_KEPT])
        topi = sb("topi", [128, 2, 8], U32)
        onehot = sb("onehot", [128, 2, 2, 16], BF16)
        carry = sb("carry", [128, 2, 2, 2, 16])
        place = sb("place", [128, 2, 2, 16])
        placed = sb("placed", [128, 2, 2, 16])
        dest = sb("dest", [128, 2, 2], I32)
        sent = sb("sent", [128, 2, D])
        kept = sb("kept", [128, B, N_KEPT])
        wide = sb("wide", [128, 2, B, 16])
        small = sb("small", [128, 16, B])
        per_e = sb("per_e", [128, 8, 16])
        per_ei = sb("per_ei", [128, 2, 16], I32)
        tile_cmp = sb("tile_cmp", [128, 2, 48, 16])
        tile_f = sb("tile_f", [128, 4, 48])
        tile_expert = sb("tile_expert", [128, 48], I32)
        tile_row = sb("tile_row", [128, 48], I32)
        second = sb("second", [128, 4, 16])
        source = sb("source", [128, 2, B], I32)
        weight = sb("weight", [128, 2, B])
        index = [sb(f"index{l}", [128, (2, 4)[l], 2], I32) for l in range(2)]
        moved = [sb(f"moved{l}", [128, (2, 4)[l], 2, D]) for l in range(2)]
        pack1 = sb("pack1", [128, 2, PACK1])
        pack2 = sb("pack2", [128, 2, PACK2])
        tile_rows = sb("tile_rows", [128, 2, 4, D])
        tile_rows2 = sb("tile_rows2", [128, 2, 4, D])
        rowsT = sb("rowsT", [128, 2, 512])
        hidden = sb("hidden", [128, 2, FCH, 512])
        rows_out = sb("rows_out", [128, 2, 4, D])

        const_in, setup_done, zero_in, k_rows_zero = (sem(n) for n in "const_in setup_done zero_in k_rows_zero".split())
        x_in_sem = [sem(f"x_in{c}") for c in range(4)]
        ctx_in_sem = [sem(f"ctx_in{p}") for p in range(2)]
        key_in_sem = [sem(f"key_in{p}") for p in range(2)]
        shift_in = [sem(f"shift_in{p}") for p in range(2)]
        pack1_in_sem = [sem(f"pack1_in{p}") for p in range(2)]
        pack2_in_sem = [sem(f"pack2_in{p}") for p in range(2)]
        tile_in_sem = [sem(f"tile_in{p}") for p in range(2)]
        stored = [sem(f"stored{p}") for p in range(2)]
        scattered = [sem(f"scattered{p}") for p in range(2)]
        gathered = [[sem(f"gathered{l}_{p}") for p in range((2, 4)[l])] for l in range(2)]
        (stats_done, aggr_done, vareps_done, rstd_done, xn_done, xT_ps, xT_done, q_ps, kv_ps, q_bf_done,
         q_rows_done, q_rows1_done, k_done, v_done, k_masked_done, rowmax_ps, max_done, negmaxT_ps, negmaxT_done, k_rows_done,
         score_ps, exp_done, pv_ps, o_done, oT_ps, rden_done, att_done, attT_ps, attT_done, y_ps,
         hidden_kept, h2_done, resid_done, keyrow_done, rawk_done, rawq_done, qprod_done, qT_done,
         kprod_done, biased, r_stats_done, r_aggr_done, r_vareps_done, r_rstd_done, r_x_done, r_h_kept, r_xT_ps,
         r_xT_done, r_logit_ps, r_logit_done, r_top_done, r_topi_done, r_choice_done, r_onehot_done,
         r_count_ps, r_place_done, r_carry_done, r_placed_done, r_sum_done, r_dest_done, r_kept, sent_done,
         routed_dve, routed_act, index_done, mix_half, mix_done, tile_done, rowsT_ps, rowsT_done,
         fc1_ps, gelu_done, fc2_ps, rows_out_done, written) = (sem(n) for n in (
            "stats_done aggr_done vareps_done rstd_done xn_done xT_ps xT_done q_ps kv_ps q_bf_done "
            "q_rows_done q_rows1_done k_done v_done k_masked_done rowmax_ps max_done negmaxT_ps negmaxT_done k_rows_done "
            "score_ps exp_done pv_ps o_done oT_ps rden_done att_done attT_ps attT_done y_ps "
            "hidden_kept h2_done resid_done keyrow_done rawk_done rawq_done qprod_done qT_done "
            "kprod_done biased r_stats_done r_aggr_done r_vareps_done r_rstd_done r_x_done r_h_kept r_xT_ps "
            "r_xT_done r_logit_ps r_logit_done r_top_done r_topi_done r_choice_done r_onehot_done "
            "r_count_ps r_place_done r_carry_done r_placed_done r_sum_done r_dest_done r_kept sent_done "
            "routed_dve routed_act index_done mix_half mix_done tile_done rowsT_ps rowsT_done "
            "fc1_ps gelu_done fc2_ps rows_out_done written").split())

        carried = {e: sem(f"carried_{n}") for e, n in ((nc.tensor.engine, "pe"), (nc.vector.engine, "dve"),
                                                     (nc.gpsimd.engine, "pool"), (nc.sync.engine, "sp"))}

        def steps(eng, lag, body, total=B, first=2):
            lead = max(first, lag + lag % 2)
            turns = (total - lead) // 2
            for t in range(lead):
                body(t, t % 2)
            with eng.Fori(0, turns) as i:
                for u in range(2):
                    body(i * 2 + (lead + u), u)
            for t in range(lead + 2 * turns, total + lag):
                body(t, t % 2)

        def item(t, par, lag, total=B):
            b = t - lag
            if isinstance(b, int) and not 0 <= b < total:
                return None, None
            return b, (par + lag) % 2

        def sequences(eng, segment, body):
            for n in segment:
                lead = LEAD[n]
                for t in range(lead):
                    body(n, t, t % 2)
                with eng.Fori(0, (B - lead) // 2) as i:
                    for u in range(2):
                        body(n, i * 2 + (lead + u), u)
            for t in range(B, B + HEAD):
                body(segment[-1], t, t % 2)

        def sequence(segment, n, t, par, lag):
            b = t - lag
            if isinstance(b, int) and b < 0:
                n, b = n - 1, b + B
            if isinstance(b, int) and (n not in segment or b >= B):
                return n, None, None, None
            return n, b, B * n + b, (par + lag) % 2

        def router_item(segment, n, t, par, lag):
            m, b, g, p = sequence(segment, n, t, par, lag)
            if b is None or m not in layer_of:
                return m, None, None, None
            return m, b, B * layer_of[m] + b, p

        def after(eng, semaphore, count):
            if not (isinstance(count, int) and count <= 0):
                eng.wait_ge(semaphore, count)

        def apart(eng, *waits):
            for semaphore, count in waits:
                after(eng, semaphore, count)
            eng.sem_inc(carried[eng.engine])

        def start(eng):
            eng.wait_ge(const_in, 16 * N_CONST)
            eng.wait_ge(setup_done, SETUP)

        N_CONST, SETUP = 12, 14
        layer_of = {2: 0, 4: 1}
        SEGMENTS = [x for x in ([n for n in seg if n < stop] for seg in ((0, 1, 2), (3, 4))) if x]
        block = ctx.enter_context(nc.Block())

        @block.sync
        def _(sp):
            def load_x(c):
                sp.dma_start(x_all[:, 8 * c:8 * c + 8, :],
                             x_in[8 * c:8 * c + 8].rearrange("b t d -> t b d")).then_inc(x_in_sem[c], 16)

            load_x(0)
            for dst, src in ((ident, ident_in), (weights, weights_in), (cols, cols_in), (out_bias, out_bias_in),
                             (row_head, row_head_in), (upper_head, upper_head_in), (rope, rope_in),
                             (router, router_in), (iotas, iotas_in),
                             (lower, lower_in)):
                sp.dma_start(dst[:], src).then_inc(const_in, 16)
            sp.dma_start(carry[:, :, 0], carry_in).then_inc(const_in, 16)
            sp.dma_start(masks_f32, masks_in.rearrange("p m c -> p (m c)")).then_inc(const_in, 16)
            for c in range(1, 4):
                load_x(c)
            sp.wait_ge(setup_done, SETUP)

            def attention(segment):
                def body(n_, t, par):
                    n, e, g, p = sequence(segment, n_, t, par, NORM)
                    cn, c, cg, cp = sequence(segment, n_, t, par, ROW_MAX)
                    if e is not None and STAGES[n]["cross"]:
                        apart(sp, (kv_ps, g - 1))
                        sp.dma_start(ctxT[:, p, :], ctx_in[:, bass.ts(e, S)]).then_inc(ctx_in_sem[p], 16)
                        if STAGES[n]["mask"] == "keys":
                            apart(sp, (keyrow_done, e - 1))
                            sp.dma_start(keyrow[:, p, :], keymask_in[:, bass.ts(e, S)]).then_inc(key_in_sem[p], 16)
                    if c is not None:
                        apart(sp, (negmaxT_done, cg + 1),
                                  (q_rows1_done, cg + 1),
                                  (score_ps, 4 * cg - 4))
                        for half in range(2):
                            sp.dma_start(q_rows[MAX_ROW[half]:MAX_ROW[half] + 1, cp, half],
                                         negmaxT[HALF * half:HALF * half + HALF, cp, :]).then_inc(shift_in[cp], 16)
                        zeros = hidden[:].rearrange("p a b c -> p (a b c)")
                        if cn == 0:
                            R = MOE[0]["R"]
                            ends = xin[0].rearrange("(e h p r) d -> e h p (r d)", h=REGION[0] // R, p=128, r=R // 128)
                            sp.dma_start(ends[bass.ds(c // 2, 1), cp * (REGION[0] // R - 1)]
                                         .rearrange("e p w -> (e p) w"), zeros[:, 0:R]).then_inc(zero_in, 16)
                        elif cn == 1:
                            parts = xin[1].rearrange("(c p r) d -> c p (r d)", c=B, r=10)
                            sp.dma_start(parts[bass.ds(c, 1)].rearrange("c p w -> (c p) w"),
                                         zeros[0:parts.shape[1], 0:10 * D]).then_inc(zero_in, 16)
                sequences(sp, segment, body)

            def experts(l):
                m = MOE[l]
                R, blocks, base = m["R"], m["R"] // 128, sum(x["tiles"] for x in MOE[:l])
                for p in range(2):
                    sp.wait_ge(scattered[p], 16 * 2 * 16 * (l + 1))
                sp.wait_ge(zero_in, 16 * N_ZERO)
                if l == 1:
                    sp.wait_ge(routed_dve, TILED[1])

                def rows_at(a, table, most):
                    return sp.value_load(table[0:1, bass.ds(a, 1)], min_val=0, max_val=most)

                def expert_of(a):
                    expert = a if l == 0 else rows_at(a, tile_expert, m["E"] - 1)
                    return packs[l][bass.ds(expert, 1)].rearrange("e p c -> (e p) c")

                def load(a, g, p):
                    if l == 0:
                        apart(sp, (rowsT_ps, g - 1),
                                  (tile_done, g - 1))
                        regions = xin[0].rearrange("(e h r p) d -> e h p r d", h=REGION[0] // R, p=128, r=blocks)
                        for rows_, h in ((tile_rows, 0), (tile_rows2, REGION[0] // R - 1)):
                            sp.dma_start(rows_[:, p, 0:blocks, :],
                                         regions[bass.ds(a, 1), h].rearrange("e p r d -> (e p) r d")) \
                                .then_inc(tile_in_sem[p], 16)
                    else:
                        row = rows_at(a, tile_row, m["E"] * REGION[1])
                        apart(sp, (rowsT_ps, g - 1))
                        sp.dma_start(tile_rows[:, p, 0:blocks, :],
                                     xin[1][bass.ds(row, R), :].rearrange("(r p) d -> p r d", p=128)) \
                            .then_inc(tile_in_sem[p], 16)
                    apart(sp, (fc1_ps, 4 * g - 4),
                              (gelu_done, 4 * g - 4))
                    sp.dma_start(pack1[:, p, :], expert_of(a)[:, 0:PACK1]).then_inc(pack1_in_sem[p], 16)

                def body(t, par):
                    a, p = item(t, par, 0, m["tiles"])
                    if a is not None:
                        load(a, base + a, p)
                    a, p = item(t, par, 1, m["tiles"])
                    if a is not None:
                        apart(sp, (fc2_ps, base + a - 1),
                                  (rows_out_done, base + a - 1))
                        sp.dma_start(pack2[:, p, :], expert_of(a)[:, PACK1:]).then_inc(pack2_in_sem[p], 16)
                    a, p = item(t, par, 3, m["tiles"])
                    if a is not None:
                        apart(sp, (rows_out_done, base + a + 1))
                        sp.dma_start(eout[l][bass.ts(a, R), :].rearrange("(r p) d -> p r d", p=128),
                                     rows_out[:, p, 0:blocks, :]).then_inc(stored[p], 16)
                steps(sp, 3, body, m["tiles"], 4)

            for l, segment in enumerate(SEGMENTS):
                attention(segment)
                if stop > (2, 5)[l]:
                    experts(l)
            if stop > 5:
                def body(t, par):
                    sp.wait_ge(mix_done, B + t + 1)
                    sp.dma_start(out[bass.ds(t, 1)].rearrange("b t d -> t (b d)"), x_all[:, t, :]) \
                        .then_inc(written, 16)
                steps(sp, 0, body)
                sp.wait_ge(written, 16 * B)
            else:
                sp.wait_ge(resid_done, B * min(stop, 5))
                if stop > 2:
                    sp.wait_ge(mix_done, B)
                sp.dma_start(out.rearrange("b t d -> t b d"), x_all[:]).then_inc(written, 16)
                sp.wait_ge(written, 16)

        @block.tensor
        def _(pe):
            def mm(dst, lhsT, rhs, first=True, last=True):
                return pe.matmul(dst, lhsT, rhs, start=first, stop=last)

            def warm_up(n):
                if n:
                    pe.wait_ge(mix_done, 1)
                for _ in range(WARM_UP):
                    mm(kv_bank[:], ident_bf[:], ones_bf[:])

            half = lambda gr: slice(64 * (gr // 2), 64 * (gr // 2) + 64)
            heads_of = lambda gr: slice(PER * (gr % 2), PER * (gr % 2) + PER)
            mask_of = lambda st: {"window": (0, 1), "causal": (2, 3)}.get(st["mask"], (None, None))

            def row_scores(n, b, g, p, gr):
                st, dst, part, heads = STAGES[n], rowmax_bank[gr % 2], half(gr), heads_of(gr)
                apart(pe, *([(k_masked_done, g + 1), (q_bf_done, g + 1)] if gr == 0 else []),
                      *([(keyrow_done, b + 1)] if gr == 0 and st["mask"] == "keys" else []),
                      *([(negmaxT_done, g)] if gr == 1 else []),
                      (max_done, 4 * g + gr - 1))
                ins = mm(dst[:], q_bf[part, p, :], k_masked[part, p, heads, :], last=st["mask"] is None)
                if st["mask"] in ("window", "causal"):
                    ins = mm(dst[:], ident_bf[:], masks[:, mask_of(st)[0], :], first=False)
                elif st["mask"] == "keys":
                    ins = mm(dst[:], ones_bf[:, 0:128],
                             keyrow_bf[:, p, :].unsqueeze(1).to_broadcast([128, PER, S]), first=False)
                ins.then_inc(rowmax_ps, 1)

            def key_scores(n, b, g, p, gr):
                st, dst = STAGES[n], score_bank[gr % 2]
                if gr == 0:
                    after(pe, k_rows_done, g + 1)
                    after(pe, q_rows_done, g + 1)
                    after(pe, q_rows1_done, g + 1)
                    after(pe, shift_in[p], (b // 2 + (B // 2 * n + 1)) * 32)
                after(pe, exp_done, 4 * g + gr - 1)
                ins = mm(dst[:], k_rows[:, p, gr // 2, :], q_rows[:, p, gr // 2, heads_of(gr), :], last=st["mask"] is None)
                if st["mask"] in ("window", "causal"):
                    ins = mm(dst[:], ident_bf[:], masks[:, mask_of(st)[1], :], first=False)
                elif st["mask"] == "keys":
                    ins = mm(dst[:], keyrow_bf[:, p, :], ones_bf[:], first=False)
                ins.then_inc(score_ps, 1)

            def attention(segment):
                def body(n_, t, par):
                    an, a, ag, ap = sequence(segment, n_, t, par, PROJECT)
                    cn, c, cg, cp = sequence(segment, n_, t, par, ROW_MAX)
                    kn, k, kg, kp = sequence(segment, n_, t, par, KEYS)
                    fn, f, fg, fp = sequence(segment, n_, t, par, FINISH)
                    un, u, ug, up = router_item(segment, n_, t, par, ROUTER)
                    wn, w, wg, wp = router_item(segment, n_, t, par, PLACE)
                    if c is not None:
                        row_scores(cn, c, cg, cp, 0)
                    if c is not None:
                        row_scores(cn, c, cg, cp, 1)
                    if f is not None:
                        after(pe, exp_done, 4 * fg + 4)
                        after(pe, v_done, fg + 1)
                        after(pe, resid_done, fg)
                        for h in range(H):
                            ins = mm(o_bank[32 * (h % 4):32 * (h % 4) + HD + 1, 128 * (h // 4):128 * (h // 4) + 128],
                                     v_aug[:, fp, h, :], probs[:, fp, h, :])
                        ins.then_inc(pv_ps, 1)
                    if a is not None:
                        after(pe, xn_done, ag + 1)
                        after(pe, q_bf_done, ag)
                        after(pe, qT_done, ag)
                        pe.transpose(misc_bank[:, XT_COLS], xn[:, ap, :], ident[:]).then_inc(xT_ps, 1)
                    if k is not None:
                        key_scores(kn, k, kg, kp, 0)
                    if c is not None:
                        row_scores(cn, c, cg, cp, 2)
                    if f is not None:
                        after(pe, o_done, fg + 1)
                        after(pe, attT_done, fg)
                        if w is not None:
                            after(pe, r_logit_done, wg + 1)
                            after(pe, r_carry_done, wg)
                        for j in range(4):
                            ins = pe.transpose(ot_bank[:, 128 * j:128 * j + 128], o_sb[:, fp, j, :], ident[:])
                        ins.then_inc(oT_ps, 1)
                    if k is not None:
                        key_scores(kn, k, kg, kp, 1)
                    if c is not None:
                        row_scores(cn, c, cg, cp, 3)
                    if a is not None:
                        st, wts = STAGES[an], (lambda i: weights[:, 4 * an + i, :])
                        cross = sum(x["cross"] for x in STAGES[:an])
                        src = ctxT if st["cross"] else xT
                        if st["cross"]:
                            pe.wait_ge(ctx_in_sem[ap], (a // 2 + (16 * cross + 1)) * 16)
                        after(pe, xT_done, ag + 1)
                        after(pe, k_done, ag)
                        after(pe, v_done, ag)
                        mm(kv_bank[:, K_COLS], wts(1), src[:, ap, :])
                        if st["rope"]:
                            mm(kv_bank[:, KSW_COLS], weights[:, W_SWK, :], src[:, ap, :])
                        mm(kv_bank[:, V_COLS], src[:, ap, :], wts(2)).then_inc(kv_ps, 1)
                        ins = mm(misc_bank[:, Q_COLS], wts(0), xT[:, ap, :])
                        if st["rope"]:
                            ins = mm(misc_bank[:, QSW_COLS], weights[:, W_SWQ, :], xT[:, ap, :])
                        ins.then_inc(q_ps, 1)
                    if u is not None:
                        after(pe, r_x_done, ug + 1)
                        after(pe, att_done, fg + 1 if f is not None else B * (un + 1))
                        if w is not None:
                            after(pe, r_logit_done, wg + 1)
                            after(pe, r_carry_done, wg)
                        pe.transpose(ot_bank[:, RX_COLS], r_x[:, up, :], ident[:]).then_inc(r_xT_ps, 1)
                    if f is not None:
                        after(pe, att_done, fg + 1)
                        pe.transpose(ot_bank[:, ATT_COLS], att[:, fp, :], ident[:]).then_inc(attT_ps, 1)
                    if k is not None:
                        key_scores(kn, k, kg, kp, 2)
                    if c is not None:
                        after(pe, max_done, 4 * cg + 4)
                        pe.transpose(rowmax_bank[1][0:H, NEGMAX_COLS], negmax[:, cp], ident[:]).then_inc(negmaxT_ps, 1)
                    if f is not None:
                        after(pe, attT_done, fg + 1)
                        mm(o_bank[:, 0:D], attT[:, fp, :], weights[:, 4 * fn + 3, :]).then_inc(y_ps, 1)
                    if k is not None:
                        key_scores(kn, k, kg, kp, 3)
                    if u is not None:
                        after(pe, r_xT_done, ug + 1)
                        if f is not None:
                            after(pe, attT_done, fg + 1)
                        mm(ot_bank[:, LOGIT_COLS], r_xT[:, up, :], router[:, layer_of[un], :]).then_inc(r_logit_ps, 1)
                    if w is not None:
                        after(pe, r_onehot_done, 2 * wg + 2)
                        after(pe, r_carry_done, wg)
                        after(pe, r_logit_done, wg + 1)
                        both, counts, totals = onehot[:, wp].rearrange("p k e -> p (k e)"), COUNT_COLS, TOTAL_COLS
                        if wn == 2:
                            mm(ot_bank[:, counts], lower_bf[:], both)
                            ins = mm(ot_bank[:, totals], ones_bf[:, 0:128], both)
                        else:
                            for k_ in range(2):
                                at = counts.start + 16 * k_
                                mm(ot_bank[:, at:at + 16], lower_bf[:], onehot[:, wp, k_, :], last=not k_)
                                if k_:
                                    mm(ot_bank[:, at:at + 16], ones_bf[:, 0:128], onehot[:, wp, 0, :], first=False)
                            for k_ in range(2):
                                at = totals.start + 16 * k_
                                mm(ot_bank[:, at:at + 16], ones_bf[:, 0:128], onehot[:, wp, 0, :], last=False)
                                ins = mm(ot_bank[:, at:at + 16], ones_bf[:, 0:128], onehot[:, wp, 1, :], first=False)
                        ins.then_inc(r_count_ps, 1)
                warm_up(segment[0])
                sequences(pe, segment, body)

            def experts(l):
                m = MOE[l]
                R, blocks, base = m["R"], m["R"] // 128, sum(x["tiles"] for x in MOE[:l])
                pe.wait_ge(resid_done, B * (2 * l + 3))
                pe.wait_ge(max_done, 4 * B * (2 * l + 3))
                pe.wait_ge(r_carry_done, B * (l + 1))

                def body(t, par):
                    a, p = item(t, par, 1, m["tiles"])
                    if a is not None:
                        g = base + a
                        pe.wait_ge(pack1_in_sem[p], (a // 2 + (base // 2 + 1)) * 16)
                        after(pe, rowsT_done, g + 1)
                        for f in range(FCH):
                            after(pe, gelu_done, 4 * g + (f - 3))
                            mm(bank[f][:, 0:R], pack1[:, p, 128 * f:128 * f + 128], rowsT[:, p, 0:R]) \
                                .then_inc(fc1_ps, 1)
                    d, q = item(t, par, 0, m["tiles"])
                    if d is not None:
                        g = base + d
                        if l == 0:
                            pe.wait_ge(tile_done, d + 1)
                        else:
                            pe.wait_ge(tile_in_sem[q], (d // 2 + (base + 1)) * 16)
                        after(pe, rowsT_done, g)
                        for r in range(blocks):
                            ins = pe.transpose(ot_bank[:, 128 * r:128 * r + 128], tile_rows[:, q, r, :], ident[:])
                        ins.then_inc(rowsT_ps, 1)
                    c, p = item(t, par, 2, m["tiles"])
                    if c is not None:
                        g = base + c
                        pe.wait_ge(pack2_in_sem[p], (c // 2 + (base // 2 + 1)) * 16)
                        after(pe, gelu_done, 4 * g + 4)
                        after(pe, rows_out_done, g - 1)
                        for r in range(blocks):
                            for f in range(FCH):
                                ins = mm((o_bank, kv_bank)[p][:, 128 * r:128 * r + 128],
                                         hidden[:, p, f, 128 * r:128 * r + 128],
                                         pack2[:, p, 128 * f:128 * f + 128], f == 0, f == FCH - 1)
                        ins.then_inc(fc2_ps, 1)
                steps(pe, 3, body, m["tiles"], 4)

            start(pe)
            for l, segment in enumerate(SEGMENTS):
                attention(segment)
                if stop > (2, 5)[l]:
                    experts(l)

        @block.scalar
        def _(act):
            col = lambda i: cols[:, i:i + 1]

            def attention(segment):
                def exponential(kg, kp, gr):
                    after(act, score_ps, 4 * kg + gr + 1)
                    if gr == 0:
                        after(act, pv_ps, kg - 1)
                    act.activation(probs[:, kp, PER * gr:PER * gr + PER, :], score_bank[gr % 2][:],
                                   ACT.Exp, scale=SCALE).then_inc(exp_done, 1)

                def body(n_, t, par):
                    an, a, ag, ap = sequence(segment, n_, t, par, PROJECT)
                    cn, c, cg, cp = sequence(segment, n_, t, par, ROW_MAX)
                    kn, k, kg, kp = sequence(segment, n_, t, par, KEYS)
                    fn, f, fg, fp = sequence(segment, n_, t, par, FINISH)
                    un, u, ug, up = router_item(segment, n_, t, par, ROUTER)
                    if f is not None:
                        after(act, pv_ps, fg + 1)
                        after(act, oT_ps, fg - 1)
                        act.activation(o_sb[:, fp].rearrange("p j q -> p (j q)"), o_bank[:], ACT.Copy) \
                            .then_inc(o_done, 1)
                    if c is not None:
                        after(act, pv_ps, cg - 1)
                        act.activation(v_aug[:, cp, :, 0:HD],
                                       kv_bank[:, V_COLS].rearrange("p (h d) -> p h d", d=HD), ACT.Copy) \
                            .then_inc(v_done, 1)
                    if k is not None:
                        exponential(kg, kp, 0)
                    if a is not None:
                        after(act, xT_ps, ag + 1)
                        after(act, kv_ps, ag - 1)
                        if STAGES[an]["inner"]:
                            ins = act.activation(xT[:, ap, :], misc_bank[:, XT_COLS], ACT.Identity,
                                                 bias=col(COL_LN1B), scale=col(COL_LN1W))
                        else:
                            ins = act.activation(xT[:, ap, :], misc_bank[:, XT_COLS], ACT.Copy)
                        ins.then_inc(xT_done, 1)
                    if k is not None:
                        exponential(kg, kp, 1)
                    if a is not None:
                        rope_ = STAGES[an]["rope"]
                        after(act, kv_ps, ag + 1)
                        if rope_:
                            after(act, k_done, ag - 1)
                            act.activation(raw[:, ap, 2:4, :],
                                           kv_bank[:].rearrange("p (j s) -> p j s", s=S)[:, 0:3:2, :],
                                           ACT.Copy).then_inc(rawk_done, 1)
                            after(act, q_ps, ag + 1)
                            after(act, qprod_done, a - 1)
                            act.activation(raw[:, ap, 0:2, :],
                                           misc_bank[:].rearrange("p (j s) -> p j s", s=S)[:, 1:3, :],
                                           ACT.Copy).then_inc(rawq_done, 1)
                        else:
                            after(act, k_masked_done, ag - 1)
                            act.activation(kT[:, ap, :], kv_bank[:, K_COLS], ACT.Identity,
                                           bias=col(COL_BK + an)).then_inc(k_done, 1)
                            after(act, q_ps, ag + 1)
                            after(act, rowmax_ps, 4 * ag - 4)
                            act.activation(q_bf[:, ap, :], misc_bank[:, Q_COLS], ACT.Identity,
                                           bias=col(COL_BQ + an)).then_inc(q_bf_done, 1)
                            after(act, q_rows_done, ag - 1)
                            after(act, q_rows1_done, ag - 1)
                            act.activation(qT[:, ap, :], misc_bank[:, Q_COLS], ACT.Identity,
                                           bias=col(COL_BQ + an)).then_inc(qT_done, 1)
                    if f is not None:
                        after(act, attT_ps, fg + 1)
                        after(act, y_ps, fg - 1)
                        act.activation(attT[:, fp, :], ot_bank[:, ATT_COLS], ACT.Identity,
                                       bias=col(COL_BV + fn)).then_inc(attT_done, 1)
                    if u is not None:
                        after(act, r_xT_ps, ug + 1)
                        after(act, r_logit_ps, ug - 1)
                        if un == 2:
                            ins = act.activation(r_xT[:, up, :], ot_bank[:, RX_COLS], ACT.Identity,
                                                 bias=col(COL_LN2B), scale=col(COL_LN2W))
                        else:
                            ins = act.activation(r_xT[:, up, :], ot_bank[:, RX_COLS], ACT.Copy)
                        ins.then_inc(r_xT_done, 1)
                    if k is not None:
                        exponential(kg, kp, 2)
                    if k is not None:
                        exponential(kg, kp, 3)
                    if a is not None and not rope_:
                        after(act, score_ps, 4 * ag - 4)
                        for half, rows_ in enumerate(HALF_ROWS):
                            ins = act.activation(k_rows[rows_, ap, half, :], kv_bank[rows_, K_COLS],
                                                 ACT.Identity, bias=cols[rows_, COL_BK + an:COL_BK + an + 1])
                        ins.then_inc(k_rows_done, 1)
                    if a is not None and rope_:
                        after(act, qT_done, ag + 1)
                        after(act, rowmax_ps, 4 * ag - 4)
                        act.activation(q_bf[:, ap, :], qT[:, ap, :], ACT.Copy).then_inc(q_bf_done, 1)
                        after(act, k_done, ag + 1)
                        after(act, score_ps, 4 * ag - 4)
                        for half, rows_ in enumerate(HALF_ROWS):
                            ins = act.activation(k_rows[rows_, ap, half, :], kT[rows_, ap, :], ACT.Copy)
                        ins.then_inc(k_rows_done, 1)
                sequences(act, segment, body)

            def gates(l):
                act.wait_ge(routed_dve, DIFFS[l])
                act.activation(small[:, 2, :], small[:, 1, :], ACT.Exp).then_inc(routed_act, 1)
                if l == 0:
                    act.activation(wide[:, 1], wide[:, 0], ACT.Exp).then_inc(routed_act, 1)

            def experts(l):
                m = MOE[l]
                R, base = m["R"], sum(x["tiles"] for x in MOE[:l])

                def body(t, par):
                    if isinstance(t, int) and t == 2:
                        gates(l)
                    a, p = item(t, par, 1, m["tiles"])
                    if a is not None:
                        g = base + a
                        after(act, fc2_ps, g - 1)
                        for f in range(FCH):
                            after(act, fc1_ps, 4 * g + f + 1)
                            act.activation(hidden[:, p, f, 0:R], bank[f][:, 0:R], ACT.Gelu,
                                           bias=pack1[:, p, F + f:F + f + 1]).then_inc(gelu_done, 1)
                    d, q = item(t, par, 0, m["tiles"])
                    if d is not None:
                        g = base + d
                        after(act, rowsT_ps, g + 1)
                        after(act, fc1_ps, 4 * g - 4)
                        if l == 0:
                            ins = act.activation(rowsT[:, q, 0:R], ot_bank[:, 0:R], ACT.Identity,
                                                 bias=col(COL_LN2B), scale=col(COL_LN2W))
                        else:
                            ins = act.activation(rowsT[:, q, 0:R], ot_bank[:, 0:R], ACT.Copy)
                        ins.then_inc(rowsT_done, 1)
                steps(act, 3, body, m["tiles"], 4)

            start(act)
            for l, segment in enumerate(SEGMENTS):
                attention(segment)
                if stop > (2, 5)[l]:
                    experts(l)

        @block.vector
        def _(dve):
            routed = [0]

            def link(ins):
                routed[0] += 1
                ins.then_inc(routed_dve, 1)
                dve.wait_ge(routed_dve, routed[0])

            def attention(segment):
                def body(n_, t, par):
                    mn, m_, mg, mp = sequence(segment, n_, t, par, MIX)
                    en, e, eg, ep = sequence(segment, n_, t, par, NORM)
                    an, a, ag, ap = sequence(segment, n_, t, par, PROJECT)
                    cn, c, cg, cp = sequence(segment, n_, t, par, ROW_MAX)
                    fn, f, fg, fp = sequence(segment, n_, t, par, FINISH)
                    rn, r, rg, rp = router_item(segment, n_, t, par, NORM2)
                    un, u, ug, up = router_item(segment, n_, t, par, ROUTER)
                    wn, w, wg, wp = router_item(segment, n_, t, par, PLACE)
                    vn, v, vg, vp = router_item(segment, n_, t, par, SEND)

                    def maximum(gr):
                        after(dve, rowmax_ps, 4 * cg + gr + 1)
                        if gr == 0:
                            after(dve, negmaxT_ps, cg - 1)
                        dve.tensor_reduce(negmax[:, cp, PER * gr:PER * gr + PER],
                                          rowmax_bank[gr % 2][:].rearrange("p (h k) -> p h k", k=S),
                                          X_AXIS, ALU.max, negate=True).then_inc(max_done, 1)
                    if c is not None:
                        maximum(0)
                    if mn == 3 and m_ is not None:
                        fetch(0, m_, mp)
                    if e is not None:
                        if en == 0 and isinstance(e, int) and e in (0, 3):
                            for q in range(4) if e else range(1):
                                dve.wait_ge(x_in_sem[q], 16)
                        elif en == 3:
                            mix(0, e, ep)
                            dve.wait_ge(mix_done, e + 1)
                        elif en:
                            dve.wait_ge(resid_done, eg - B + 1)
                        apart(dve, (aggr_done, eg - 1))
                        dve.bn_stats(stats[:, ep, :], x_all[:, e, :]).then_inc(stats_done, 1)
                    if r is not None:
                        rows_of = h_all if rn == 2 else x_all
                        apart(dve, (resid_done, B * rn + r + 1),
                              (r_aggr_done, rg - 1))
                        dve.bn_stats(r_stats[:, rp, :], rows_of[:, r, :]).then_inc(r_stats_done, 1)
                    if c is not None:
                        maximum(1)
                    if e is not None:
                        apart(dve, (stats_done, eg + 1),
                              (vareps_done, eg - 1),
                              (xn_done, eg - 1))
                        dve.bn_aggr(meanvar[:, ep, :], stats[:, ep, :]).then_inc(aggr_done, 1)
                    if r is not None:
                        apart(dve, (r_stats_done, rg + 1),
                              (r_vareps_done, rg - 1),
                              (r_x_done, rg - 1))
                        dve.bn_aggr(r_meanvar[:, rp, :], r_stats[:, rp, :]).then_inc(r_aggr_done, 1)
                    if v is not None:
                        after(dve, r_place_done, vg + 1)
                        after(dve, r_sum_done, 2 * vg - 2)
                        dve.tensor_tensor(placed[:, vp], place[:, vp], onehot[:, vp], ALU.mult) \
                            .then_inc(r_placed_done, 1)
                        after(dve, r_placed_done, vg + 1)
                        for q in range(2):
                            dve.tensor_reduce(r_row[:, vp, PLACES.start + q:PLACES.start + q + 1], placed[:, vp, q],
                                              X_AXIS, ALU.add, negate=bool(vn == 2 and q)).then_inc(r_sum_done, 1)
                        after(dve, r_sum_done, 2 * vg + 2)
                        after(dve, sent_done, vg - 1)
                        for q in range(2):
                            if not (isinstance(v, int) and v < 2):
                                if q == vp:
                                    dve.wait_ge(scattered[q], (v // 2 + 16 * layer_of[vn]) * 32)
                        dve.tensor_copy(dest[:, vp, :], r_row[:, vp, PLACES]).then_inc(r_dest_done, 1)
                    if w is not None:
                        after(dve, r_logit_done, wg + 1)
                        E = MOE[layer_of[wn]]["E"]
                        apart(dve, (r_logit_done, wg + 1))
                        dve.max(r_row[:, wp, TOP], r_row[:, wp, 0:E]).then_inc(r_top_done, 1)
                        apart(dve, (r_top_done, wg + 1),
                              (r_choice_done, wg - 1))
                        dve.max_index(topi[:, wp, :], r_row[:, wp, TOP], r_row[:, wp, 0:E]).then_inc(r_topi_done, 1)
                        after(dve, r_topi_done, wg + 1)
                        dve.tensor_copy(r_row[:, wp, CHOICE], topi[:, wp, 0:2]).then_inc(r_choice_done, 1)
                        after(dve, r_choice_done, wg + 1)
                        after(dve, r_count_ps, wg - 1)
                        after(dve, r_placed_done, wg - 1)
                        for q in range(2):
                            sign = -1.0 if wn == 2 and q else 1.0
                            chosen = r_row[:, wp, CHOICE.start + q:CHOICE.start + q + 1]
                            dve.tensor_scalar(onehot[:, wp, q, :], iotas[:, 0:16], chosen, sign, ALU.is_equal,
                                              ALU.mult).then_inc(r_onehot_done, 1)
                    if f is not None:
                        per_head = ot_bank[:].rearrange("p (h c) -> p h c", c=32)
                        after(dve, oT_ps, fg + 1)
                        after(dve, att_done, fg - 1)
                        dve.reciprocal(rden[:, fp, :].unsqueeze(2), per_head[:, :, HD:HD + 1]).then_inc(rden_done, 1)
                        after(dve, rden_done, fg + 1)
                        after(dve, attT_ps, fg - 1)
                        dve.tensor_tensor(att[:, fp, :].rearrange("p (h d) -> p h d", d=HD),
                                          per_head[:, :, 0:HD],
                                          rden[:, fp, :].unsqueeze(2).to_broadcast([128, H, HD]),
                                          ALU.mult).then_inc(att_done, 1)
                    if c is not None:
                        maximum(2)
                        maximum(3)
                    if c is not None:
                        after(dve, negmaxT_ps, cg + 1)
                        if not (cn == 0 and isinstance(c, int) and c < 2):
                            dve.wait_ge(shift_in[cp], (c // 2 + B // 2 * cn) * 32)
                        dve.tensor_copy(negmaxT[:, cp, :], rowmax_bank[1][0:H, NEGMAX_COLS]).then_inc(negmaxT_done, 1)
                    if e is not None:
                        after(dve, rstd_done, eg + 1)
                        after(dve, xT_ps, eg - 1)
                        if STAGES[en]["inner"]:
                            after(dve, hidden_kept, e - 1)
                        dve.tensor_scalar(xn[:, ep, :], x_all[:, e, :], meanvar[:, ep, 0:1], rstd[:, ep:ep + 1],
                                          ALU.subtract, ALU.mult).then_inc(xn_done, 1)
                    if r is not None:
                        after(dve, r_rstd_done, rg + 1)
                        after(dve, r_xT_ps, rg - 1)
                        after(dve, r_h_kept, rg - 1)
                        dve.tensor_scalar(r_x[:, rp, :], rows_of[:, r, :], r_meanvar[:, rp, 0:1],
                                          r_rstd[:, rp:rp + 1], ALU.subtract, ALU.mult).then_inc(r_x_done, 1)
                    if f is not None:
                        after(dve, y_ps, fg + 1)
                        if STAGES[fn]["inner"]:
                            after(dve, hidden_kept, f + 1)
                            dve.tensor_tensor(h_all[:, f, :], h_all[:, f, :], o_bank[:, 0:D], ALU.add) \
                                .then_inc(h2_done, 1)
                            after(dve, h2_done, f + 1)
                            ins = dve.tensor_tensor(x_all[:, f, :], x_all[:, f, :], h_all[:, f, :], ALU.add)
                        else:
                            if STAGES[fn]["bo"]:
                                after(dve, biased, B * sum(x["bo"] and not x["inner"] for x in STAGES[:fn]) + f + 1)
                            ins = dve.tensor_tensor(x_all[:, f, :], x_all[:, f, :], o_bank[:, 0:D], ALU.add)
                        ins.then_inc(resid_done, 1)
                    if a is not None:
                        if STAGES[an]["mask"] == "keys":
                            dve.wait_ge(key_in_sem[ap], (a // 2 + 1) * 16)
                            after(dve, score_ps, 4 * ag - 4)
                            dve.tensor_scalar(keyrow_bf[0:1, ap, :], keyrow[:, ap, :], BIG / SCALE, -BIG / SCALE,
                                              ALU.mult, ALU.add).then_inc(keyrow_done, 1)
                        if STAGES[an]["rope"]:
                            after(dve, rawq_done, a + 1)
                            after(dve, qT_done, ag - 1)
                            dve.tensor_tensor(prod[:, ap, 0:2, :], raw[:, ap, 0:2, :], rope[:], ALU.mult) \
                                .then_inc(qprod_done, 1)
                            after(dve, qprod_done, a + 1)
                            after(dve, q_bf_done, ag - 1)
                            after(dve, q_rows1_done, ag - 1)
                            dve.tensor_tensor(qT[:, ap, :], prod[:, ap, 0, :], prod[:, ap, 1, :], ALU.add) \
                                .then_inc(qT_done, 1)
                        after(dve, qT_done, ag + 1)
                        after(dve, score_ps, 4 * ag - 4)
                        dve.tensor_tensor(q_rows[0:64, ap, 0], qT[0:64, ap, :].unsqueeze(1).to_broadcast([64, HALF, S]),
                                          row_head[0:64, :].unsqueeze(2).to_broadcast([64, HALF, S]),
                                          ALU.mult).then_inc(q_rows_done, 1)
                        if an in layer_of:
                            dve.tensor_tensor(q_rows[64:128, ap, 1],
                                              qT[64:128, ap, :].unsqueeze(1).to_broadcast([64, HALF, S]),
                                              row_head[64:128, :].unsqueeze(2).to_broadcast([64, HALF, S]),
                                              ALU.mult).then_inc(q_rows1_done, 1)
                    if u is not None:
                        after(dve, r_logit_ps, ug + 1)
                        if w is not None:
                            after(dve, r_count_ps, wg + 1)
                        after(dve, r_kept, ug - 1)
                        dve.tensor_copy(r_row[:, up, LOGITS], ot_bank[:, LOGIT_COLS]).then_inc(r_logit_done, 1)
                    if w is not None:
                        wl = layer_of[wn]
                        per_choice = lambda ap: ap.rearrange("p (k e) -> p k e", k=2)
                        after(dve, r_count_ps, wg + 1)
                        after(dve, r_carry_done, wg)
                        after(dve, r_placed_done, wg - 1)
                        dve.tensor_tensor(place[:, wp], per_choice(ot_bank[:, COUNT_COLS]), carry[:, wl, wp], ALU.add) \
                            .then_inc(r_place_done, 1)
                        dve.tensor_tensor(carry[:, wl, 1 - wp], per_choice(ot_bank[:, TOTAL_COLS]), carry[:, wl, wp],
                                          ALU.add).then_inc(r_carry_done, 1)
                sequences(dve, segment, body)

            e_row = iotas[:, 0:16]

            def tiles(l):
                m = MOE[l]
                dve.wait_ge(r_carry_done, B * (l + 1))
                link(dve.scalar_tensor_tensor(out=per_e[:, 0, :], in0=e_row, scalar=-float(REGION[l]),
                                              in1=carry[:, l, 0, 0, :], op0=ALU.mult, op1=ALU.add))
                if l == 0:
                    link(dve.tensor_tensor(second[:], iotas[:, 64:68].unsqueeze(2).to_broadcast([128, 4, 16]),
                                           per_e[:, 0, :].unsqueeze(1).to_broadcast([128, 4, 16]), ALU.is_gt))
                else:
                    ends, used, i_tile = per_e[:, 3, :], per_e[:, 2, :], iotas[:, 16:64]
                    link(dve.tensor_scalar(per_e[:, 1, :], per_e[:, 0, :], float(m["R"]), None, ALU.add))
                    link(dve.tensor_copy(per_ei[:, 0, :], per_e[:, 1, :]))
                    link(dve.tensor_scalar(per_ei[:, 1, :], per_ei[:, 0, :], m["R"].bit_length() - 1, None,
                                           ALU.arith_shift_right))
                    link(dve.tensor_copy(used, per_ei[:, 1, :]))
                    link(dve.tensor_tensor_scan(ends, ones_e[:], used, 0.0, ALU.mult, ALU.add))
                    link(dve.tensor_tensor(tile_cmp[:, 0], ends.unsqueeze(1).to_broadcast([128, 48, 16]),
                                           i_tile.unsqueeze(2).to_broadcast([128, 48, 16]), ALU.is_le))
                    link(dve.tensor_reduce(tile_f[:, 0, :], tile_cmp[:, 0], X_AXIS, ALU.add))
                    link(dve.tensor_tensor(tile_cmp[:, 1], used.unsqueeze(1).to_broadcast([128, 48, 16]),
                                           tile_cmp[:, 0], ALU.mult))
                    link(dve.tensor_reduce(tile_f[:, 1, :], tile_cmp[:, 1], X_AXIS, ALU.add))
                    link(dve.tensor_scalar(tile_f[:, 2, :], tile_f[:, 0, :], float(m["E"] - 1), None, ALU.min))
                    link(dve.tensor_copy(tile_expert[:], tile_f[:, 2, :]))
                    row = tile_f[:, 3, :]
                    link(dve.tensor_scalar(row, tile_f[:, 0, :], float(REGION[l]), None, ALU.mult))
                    link(dve.scalar_tensor_tensor(out=row, in0=i_tile, scalar=float(m["R"]), in1=row,
                                                  op0=ALU.mult, op1=ALU.add))
                    link(dve.scalar_tensor_tensor(out=row, in0=tile_f[:, 1, :], scalar=-float(m["R"]), in1=row,
                                                  op0=ALU.mult, op1=ALU.add))
                    link(dve.tensor_scalar(tile_f[:, 0, :], row, float(m["E"] * REGION[1]), None, ALU.min))
                    link(dve.tensor_copy(tile_row[:], tile_f[:, 0, :]))
                    link(dve.tensor_tensor(per_e[:, 4, :], ends, used, ALU.subtract))
                    link(dve.tensor_scalar(per_e[:, 4, :], per_e[:, 4, :], float(m["R"]), None, ALU.mult))
                    link(dve.scalar_tensor_tensor(out=per_e[:, 4, :], in0=e_row, scalar=-float(REGION[l]),
                                                  in1=per_e[:, 4, :], op0=ALU.mult, op1=ALU.add))
                assert routed[0] == TILED[l], routed

            def weights_of_choices(l):
                m = MOE[l]
                dve.wait_ge(r_kept, B * (l + 1))
                top1, top2 = kept[:, :, TOP.start], kept[:, :, TOP.start + 1]
                ch = [kept[:, :, CHOICE.start + q] for q in range(2)]
                at = [kept[:, :, PLACES.start + q] for q in range(2)]
                link(dve.tensor_tensor(small[:, 1, :], top2, top1, ALU.subtract))
                if l == 0:
                    link(dve.tensor_tensor(wide[:, 0], kept[:, :, LOGITS],
                                           kept[:, :, TOP.start:TOP.start + 1].to_broadcast([128, B, 16]), ALU.subtract))
                assert routed[0] == DIFFS[l], routed
                if l == 1:
                    for q in range(2):
                        link(dve.tensor_tensor(wide[:, 0], e_row.unsqueeze(1).to_broadcast([128, B, 16]),
                                               kept[:, :, CHOICE.start + q:CHOICE.start + q + 1]
                                               .to_broadcast([128, B, 16]), ALU.is_equal))
                        link(dve.tensor_tensor(wide[:, 0], wide[:, 0],
                                               per_e[:, 4, :].unsqueeze(1).to_broadcast([128, B, 16]), ALU.mult))
                        link(dve.tensor_reduce(small[:, 3, :], wide[:, 0], X_AXIS, ALU.add))
                        link(dve.tensor_tensor(small[:, 3, :], small[:, 3, :], at[q], ALU.add))
                        link(dve.tensor_copy(source[:, q, :], small[:, 3, :]))
                    dve.wait_ge(routed_act, 3)
                    link(dve.tensor_scalar(small[:, 9, :], small[:, 2, :], 1.0, None, ALU.add))
                    link(dve.reciprocal(weight[:, 0, :], small[:, 9, :]))
                    link(dve.tensor_tensor(weight[:, 1, :], weight[:, 0, :], small[:, 2, :], ALU.mult))
                    assert routed[0] == ROUTED[l], routed
                    return
                C = m["cap"]
                slot, after_all, in1, in2, row = (small[:, i, :] for i in (3, 4, 5, 6, 7))
                link(dve.scalar_tensor_tensor(out=slot, in0=ch[0], scalar=-float(REGION[l]), in1=at[0],
                                              op0=ALU.mult, op1=ALU.add))
                link(dve.tensor_scalar(in1, slot, float(C), None, ALU.is_lt))
                dve.wait_ge(routed_act, 2)
                link(dve.tensor_tensor(wide[:, 0], e_row.unsqueeze(1).to_broadcast([128, B, 16]),
                                       kept[:, :, CHOICE.start + 1:CHOICE.start + 2].to_broadcast([128, B, 16]),
                                       ALU.is_equal))
                link(dve.tensor_tensor(wide[:, 0], wide[:, 0],
                                       carry[:, 0, 0, 0, :].unsqueeze(1).to_broadcast([128, B, 16]), ALU.mult))
                link(dve.tensor_reduce(after_all, wide[:, 0], X_AXIS, ALU.add))
                link(dve.tensor_tensor(after_all, after_all, at[1], ALU.subtract))
                link(dve.tensor_scalar(in2, after_all, float(C - REGION[0]), None, ALU.is_lt))
                for q in range(2):
                    link(dve.scalar_tensor_tensor(out=row, in0=ch[q], scalar=float(C - REGION[0]), in1=at[q],
                                                  op0=ALU.mult, op1=ALU.add))
                    link(dve.tensor_scalar(row, row, float(q * (C - REGION[0])), 0.0, ALU.add, ALU.max))
                    link(dve.tensor_scalar(row, row, float(ROWS_OUT[0] - 1), None, ALU.min))
                    link(dve.tensor_copy(source[:, q, :], row))
                z, g1, g2, den = (small[:, i, :] for i in (9, 10, 11, 12))
                link(dve.tensor_reduce(z, wide[:, 1], X_AXIS, ALU.add))
                link(dve.reciprocal(z, z))
                link(dve.tensor_tensor(g1, in1, z, ALU.mult))
                link(dve.tensor_tensor(g2, in2, z, ALU.mult))
                link(dve.tensor_tensor(g2, g2, small[:, 2, :], ALU.mult))
                link(dve.tensor_tensor(den, g1, g2, ALU.add))
                link(dve.tensor_scalar(den, den, float(np.finfo(np.float32).eps), None, ALU.max))
                link(dve.reciprocal(den, den))
                for k, gk in enumerate((g1, g2)):
                    link(dve.scalar_tensor_tensor(out=weight[:, k, :], in0=gk, scalar=m["factor"], in1=den,
                                                  op0=ALU.mult, op1=ALU.mult))
                assert routed[0] == ROUTED[l], routed

            def experts(l):
                m = MOE[l]
                blocks, base = m["R"] // 128, sum(x["tiles"] for x in MOE[:l])

                def body(t, par):
                    if isinstance(t, int) and t == 2:
                        weights_of_choices(l)
                    d, q = item(t, par, 0, m["tiles"])
                    if d is not None and l == 0:
                        dve.wait_ge(tile_in_sem[q], (d // 2 + 1) * 32)
                        for r in range(blocks):
                            ins = dve.scalar_tensor_tensor(out=tile_rows[:, q, r, :], in0=tile_rows2[:, q, r, :],
                                                           scalar=second[:, r, bass.ds(d, 1)], in1=tile_rows[:, q, r, :],
                                                           op0=ALU.mult, op1=ALU.add)
                        ins.then_inc(tile_done, 1)
                    a, p = item(t, par, 2, m["tiles"])
                    if a is None:
                        return
                    g = base + a
                    after(dve, fc2_ps, g + 1)
                    if not (isinstance(a, int) and g < 2):
                        dve.wait_ge(stored[p], (a // 2 + base // 2) * 16)
                    dve.tensor_tensor(rows_out[:, p, 0:blocks, :],
                                      (o_bank, kv_bank)[p][:, 0:128 * blocks].rearrange("p (r d) -> p r d", d=D),
                                      pack2[:, p, F:].unsqueeze(1).to_broadcast([128, blocks, D]),
                                      ALU.add).then_inc(rows_out_done, 1)
                steps(dve, 3, body, m["tiles"], 4)

            def fetch(l, b, p):
                n = len(gathered[l])
                if not (isinstance(b, int) and b < n):
                    dve.wait_ge(gathered[l][p], (b // n) * 32)
                dve.tensor_copy(index[l][:, p, :], source[:, :, b]).then_inc(index_done, 1)

            def mix(l, b, p):
                dve.wait_ge(gathered[l][p], (b // len(gathered[l]) + 1) * 32)
                dve.scalar_tensor_tensor(out=x_all[:, b, :], in0=moved[l][:, p, 0, :], scalar=weight[:, 0, bass.ds(b, 1)],
                                         in1=x_all[:, b, :], op0=ALU.mult, op1=ALU.add).then_inc(mix_half, 1)
                dve.wait_ge(mix_half, B * l + b + 1)
                dve.scalar_tensor_tensor(out=x_all[:, b, :], in0=moved[l][:, p, 1, :], scalar=weight[:, 1, bass.ds(b, 1)],
                                         in1=x_all[:, b, :], op0=ALU.mult, op1=ALU.add).then_inc(mix_done, 1)

            for ap, v in ((ones_bf[:], 1.0), (v_aug[:], 1.0), (q_rows[:], 0.0), (negmax[:], 0.0),
                          (keyrow_bf[:], 0.0)):
                dve.memset(ap, v).then_inc(setup_done, 1)
            dve.memset(o_bank[:], 0.0).then_inc(setup_done, 1)
            dve.memset(k_rows[:], 0.0).then_inc(k_rows_zero, 1)
            dve.wait_ge(k_rows_zero, 1)
            for half, row in enumerate(MAX_ROW):
                dve.memset(k_rows[row:row + 1, :, half, :], 1.0).then_inc(setup_done, 1)
            dve.memset(ones_e[:], 1.0).then_inc(setup_done, 1)
            dve.wait_ge(const_in, 16 * N_CONST)
            dve.tensor_copy(masks[:].rearrange("p m c -> p (m c)"), masks_f32).then_inc(setup_done, 1)
            dve.tensor_copy(ident_bf[:], ident[:]).then_inc(setup_done, 1)
            dve.tensor_copy(lower_bf[:], lower[:]).then_inc(setup_done, 1)
            start(dve)
            for l, segment in enumerate(SEGMENTS):
                attention(segment)
                if stop > (2, 5)[l]:
                    tiles(l)
                    experts(l)
            if stop > 5:
                for t in range(4):
                    fetch(1, t, t)
                mix(1, 0, 0)
                with dve.Fori(0, B // 4 - 1) as i:
                    for u in range(4):
                        fetch(1, i * 4 + (4 + u), u)
                        mix(1, i * 4 + (1 + u), (1 + u) % 4)
                for t in range(B - 3, B):
                    mix(1, t, t % 4)

        @block.gpsimd
        def _(pool):
            head_of_row = row_head[:].unsqueeze(2).to_broadcast([128, HALF, S])

            def rsqrt(g, p, variance, to, result, ready, first_done, done, used):
                apart(pool, (ready, g + 1),
                      (done, g - 1))
                pool.tensor_scalar(to[:, p:p + 1], variance[:, p, 1:2], EPS, None, ALU.add).then_inc(first_done, 1)
                apart(pool, (first_done, g + 1),
                      (used, g - 1))
                pool.tensor_tensor(result[:, p:p + 1], to[:, p:p + 1], neghalf[:], ALU.pow).then_inc(done, 1)

            def rows_are_back(l):
                tiles = sum(m["tiles"] for m in MOE[:l + 1])
                pool.wait_ge(stored[0], 16 * ((tiles + 1) // 2))
                pool.wait_ge(stored[1], 16 * (tiles // 2))
                pool.wait_ge(routed_dve, ROUTED[l])

            def gather(l, b, p):
                apart(pool, (mix_done, B * l + b + 1 - len(gathered[l])),
                      (index_done, B * l + b + 1))
                for k in range(2):
                    pool.indirect_dma_start(
                        out=moved[l][:, p, k, :], out_offset=None, in_=eout[l],
                        in_offset=bass.IndirectOffsetOnAxis(ap=index[l][:, p, k:k + 1].bitcast(U32), axis=0)) \
                        .then_inc(gathered[l][p], 16)

            def attention(segment):
                def body(n_, t, par):
                    en, e, eg, ep = sequence(segment, n_, t, par, NORM)
                    an, a, ag, ap = sequence(segment, n_, t, par, PROJECT)
                    mn, m_, mg, mp = sequence(segment, n_, t, par, MIX)
                    rn, r, rg, rp = router_item(segment, n_, t, par, NORM2)
                    wn, w, wg, wp = router_item(segment, n_, t, par, SEND)
                    if mn == 3 and m_ is not None:
                        if isinstance(m_, int) and m_ == 0:
                            rows_are_back(0)
                        gather(0, m_, mp)
                    if e is not None:
                        rsqrt(eg, ep, meanvar, vareps, rstd, aggr_done, vareps_done, rstd_done, xn_done)
                    if r is not None:
                        rsqrt(rg, rp, r_meanvar, r_vareps, r_rstd, r_aggr_done, r_vareps_done, r_rstd_done, r_x_done)
                    if a is not None:
                        if STAGES[an]["rope"]:
                            pool.wait_ge(rawk_done, a + 1)
                            after(pool, k_done, ag - 1)
                            pool.tensor_tensor(prod[:, ap, 2:4, :], raw[:, ap, 2:4, :], rope[:], ALU.mult) \
                                .then_inc(kprod_done, 1)
                            pool.wait_ge(kprod_done, a + 1)
                            after(pool, k_rows_done, ag - 1)
                            after(pool, k_masked_done, ag - 1)
                            pool.tensor_tensor(kT[:, ap, :], prod[:, ap, 2, :], prod[:, ap, 3, :], ALU.add) \
                                .then_inc(k_done, 1)
                        after(pool, k_done, ag + 1)
                        after(pool, rowmax_ps, 4 * ag - 4)
                        pool.tensor_tensor(k_masked[:, ap], kT[:, ap, :].unsqueeze(1).to_broadcast([128, HALF, S]),
                                           head_of_row, ALU.mult).then_inc(k_masked_done, 1)
                        if an not in layer_of:
                            after(pool, score_ps, 4 * ag - 4)
                            pool.wait_ge(qT_done, ag + 1)
                            pool.tensor_tensor(q_rows[:, ap, 1], qT[:, ap, :].unsqueeze(1).to_broadcast([128, HALF, S]),
                                               upper_head[:].unsqueeze(2).to_broadcast([128, HALF, S]),
                                               ALU.mult).then_inc(q_rows1_done, 1)
                    if e is not None:
                        if STAGES[en]["inner"]:
                            apart(pool, (xn_done, eg + 1))
                            pool.tensor_tensor(h_all[:, e, :], xn[:, ep, :], out_bias[:, en, :], ALU.add) \
                                .then_inc(hidden_kept, 1)
                        elif STAGES[en]["bo"]:
                            apart(pool, (xn_done, eg + 1))
                            pool.tensor_tensor(x_all[:, e, :], x_all[:, e, :], out_bias[:, en, :], ALU.add) \
                                .then_inc(biased, 1)
                    if r is not None:
                        apart(pool, (r_x_done, rg + 1))
                        pool.tensor_copy(h_all[:, r, :], r_x[:, rp, :]).then_inc(r_h_kept, 1)
                    if w is not None:
                        if isinstance(w, int) and w == 0 and wn == 2:
                            pool.wait_ge(zero_in, 16 * N_ZERO)
                        apart(pool, (r_dest_done, wg + 1),
                              (r_onehot_done, 2 * wg + 2),
                              (r_h_kept, wg + 1))
                        pool.tensor_copy(kept[:, w, :], r_row[:, wp, :]).then_inc(r_kept, 1)
                        first = isinstance(w, int) and w < 2
                        apart(pool, *([] if first and wn == 2 else
                                      [(scattered[wp], (w // 2 + 16 * layer_of[wn]) * 32)]))
                        pool.tensor_copy(sent[:, wp, :], h_all[:, w, :]).then_inc(sent_done, 1)
                        apart(pool, (sent_done, wg + 1))
                        for q in range(2):
                            pool.indirect_dma_start(
                                out=xin[layer_of[wn]],
                                out_offset=bass.IndirectOffsetOnAxis(ap=dest[:, wp, q:q + 1].bitcast(U32), axis=0),
                                in_=sent[:, wp, :], in_offset=None).then_inc(scattered[wp], 16)
                sequences(pool, segment, body)

            pool.memset(neghalf[:], -0.5).then_inc(setup_done, 1)
            pool.memset(hidden[:], 0.0).then_inc(setup_done, 1)
            start(pool)
            for l, segment in enumerate(SEGMENTS):
                attention(segment)
            if stop > 5:
                rows_are_back(1)
                for t in range(4):
                    gather(1, t, t)
                with pool.Fori(1, B // 4) as i:
                    for u in range(4):
                        gather(1, i * 4 + u, u)


def constants():
    q, k = np.arange(S)[:, None], np.arange(S)[None, :]
    window = np.where((k <= q) & (q - k < WINDOW), 0.0, -BIG)
    causal = np.where(k <= q, 0.0, -BIG)
    masks = np.stack([np.tile(m, (1, PER)) for m in (window, window.T, causal, causal.T)], 1)
    p = np.arange(128)
    row_head = (p[:, None] % 64) // HD == np.arange(HALF)
    inv_freq = 1.0 / np.float32(10000.0) ** (np.arange(0, HD, 2, dtype=np.float32) / np.float32(HD))
    theta = np.arange(S, dtype=np.float32)[:, None] * inv_freq[None, :].astype(np.float32)
    cos, sin = (np.tile(np.repeat(f(theta), 2, axis=1), (1, H)).T for f in (np.cos, np.sin))
    sign = np.where(p % 2 == 0, -1.0, 1.0)[:, None]
    iotas = np.concatenate([np.tile(np.arange(16), (128, 1)), np.tile(np.arange(48), (128, 1)),
                            np.arange(4)[None, :] * 128 + p[:, None]], 1)
    e = np.arange(16)
    carry = np.tile(np.array([[e * REGION[0] - 1, (e + 1) * REGION[0]], [e * REGION[1] - 1] * 2]), (128, 1, 1, 1))
    f32 = lambda a: np.ascontiguousarray(a, np.float32)
    return dict(ident=f32(np.eye(128)), masks=f32(masks),
                row_head=f32(row_head), upper_head=f32(row_head * (p[:, None] >= 64)), rope=f32(np.stack([cos, sin * sign], 1)), iotas=f32(iotas),
                carry=f32(carry), lower=f32(p[:, None] <= p[None, :]))


def layout(inputs):
    a = {k: np.asarray(v) for k, v in inputs.items()}
    qkv = a["L0_attn_w_qkv"]
    w = [qkv[0:128].T, qkv[128:256].T, qkv[256:384].T, a["L0_attn_w_out"].T]
    w += [a["L0_xattn_W" + k] for k in "qkvo"] + [a[f"L0_ffn_{k}_w"] for k in "qkvo"]
    w += [a["L1_attn_W" + k] for k in "qkvo"] + [a["L1_xattn_W" + k] for k in "qkvo"]
    swap = np.arange(128) ^ 1
    w += [a["L1_attn_Wq"][:, swap], a["L1_attn_Wk"][:, swap]]
    zero, one = np.zeros(128, np.float32), np.ones(128, np.float32)
    bias = lambda k: [zero, a["L0_xattn_b" + k], a[f"L0_ffn_{k}_b"], zero, a["L1_xattn_b" + k]]
    cols = bias("q") + bias("k") + bias("v") + [a["L0_ffn_ln1_w"], a["L0_ffn_ln1_b"], a["L0_ffn_ln2_w"],
                                                a["L0_ffn_ln2_b"], one, zero]
    out_bias = [a["L0_attn_b_out"], a["L0_xattn_bo"], a["L0_ffn_o_b"], zero, a["L1_xattn_bo"]]
    router = np.zeros((128, 2, 16), np.float32)
    router[:, 0, :] = a["L0_ffn_router_w"]
    router[:, 1, 0:8] = a["L1_ffn_Wg"].T

    def pack(w1, b1, w2, b2):
        E = w1.shape[0]
        return np.concatenate([
            w1, b1.reshape(E, FCH, 128).transpose(0, 2, 1),
            w2.reshape(E, FCH, 128, D).transpose(0, 2, 1, 3).reshape(E, 128, FCH * D), np.broadcast_to(b2[:, None, :], (E, 128, D))], axis=2)
    return dict(
        x=a["x"], ctx=a["ctx_1024"].reshape(T, D).T, keymask=a["mask_BxS2_ff1"].reshape(1, T),
        weights=np.stack(w, 1), cols=np.stack(cols, 1), out_bias=np.broadcast_to(np.stack(out_bias), (128, 5, 128)), router=router,
        pack0=pack(a["L0_ffn_fc1_w"], a["L0_ffn_fc1_b"], a["L0_ffn_fc2_w"], a["L0_ffn_fc2_b"]),
        pack1=pack(a["L1_ffn_W1"].transpose(0, 2, 1), a["L1_ffn_b1"], a["L1_ffn_W2"].transpose(0, 2, 1),
                   a["L1_ffn_b2"]))


def kernel(**inputs):
    import concourse.bacc as bacc
    from concourse.bass_utils import run_bass_kernel_spmd

    nc = bacc.Bacc("TRN2", target_bir_lowering=False, num_devices=1)
    arrays, args = {}, []
    for name, a in {**layout(inputs), **constants()}.items():
        a = np.ascontiguousarray(a)
        arrays[f"in_{name}"] = a
        args.append(nc.dram_tensor(f"in_{name}", a.shape, mybir.dt.from_np(a.dtype), kind="ExternalInput").ap())
    args.append(nc.dram_tensor("out_0", (B, S, D), F32, kind="ExternalOutput").ap())
    build(nc, *args)
    r = run_bass_kernel_spmd(nc, [arrays], core_ids=[0])
    return r.results[0]["out_0"]
```
